# Optimizing a Trainium2 kernel written in Bass

```python
import numpy as np
import jax
import jax.numpy as jnp

def _softmax(x, axis=-1):
    return jax.nn.softmax(x, axis=axis)

def _gelu(x):
    return jax.nn.gelu(x, approximate=True)

def _silu(x):
    return jax.nn.silu(x)

def _sigmoid(x):
    return jax.nn.sigmoid(x)

def _layernorm(x, axis=-1, eps=1e-05):
    m = jnp.mean(x, axis=axis, keepdims=True)
    v = jnp.var(x, axis=axis, keepdims=True)
    return (x - m) / jnp.sqrt(v + eps)

def _scatter_add(tgt, idx, src, axis=0):
    return tgt.at[idx].add(src)

def _segment_sum(src, seg, n):
    return jax.ops.segment_sum(src, seg, n)
kernel_name = 'mk_hybrid_d1_jaxref_r8_029641'

def setup_inputs(seed: int=0):
    np.random.seed(seed)
    _w = jnp.asarray

    def _L0_attn_a_setup():
        import jax, jax.numpy as jnp
        import numpy as np
        D_MODEL = 128
        N_HEAD = 16
        HEAD_DIM = D_MODEL // N_HEAD
        B, T = (2, 256)
        ROPE_BASE = 10000.0

        def _rotary_cos_sin(seq_len, head_dim, dtype):
            inv_freq = 1.0 / ROPE_BASE ** (jnp.arange(0, head_dim, 2, dtype=jnp.float32) / head_dim)
            t = jnp.arange(seq_len, dtype=jnp.float32)
            freqs = jnp.outer(t, inv_freq)
            cos = jnp.cos(freqs).astype(dtype)[None, :, None, :]
            sin = jnp.sin(freqs).astype(dtype)[None, :, None, :]
            return (cos, sin)

        def _apply_rotary(x, cos, sin):
            d = x.shape[3] // 2
            x1, x2 = (x[..., :d], x[..., d:])
            y1 = x1 * cos + x2 * sin
            y2 = -x1 * sin + x2 * cos
            return jnp.concatenate([y1, y2], axis=3).astype(x.dtype)
        key = jax.random.key(seed)
        ks = jax.random.split(key, 7)
        s = 1.0 / np.sqrt(D_MODEL)
        return {'x': jax.random.normal(ks[0], (B, T, D_MODEL), dtype=jnp.float32), 'Wq': jax.random.normal(ks[1], (D_MODEL, D_MODEL), dtype=jnp.float32) * s, 'Wk': jax.random.normal(ks[2], (D_MODEL, D_MODEL), dtype=jnp.float32) * s, 'Wq2': jax.random.normal(ks[3], (D_MODEL, D_MODEL), dtype=jnp.float32) * s, 'Wk2': jax.random.normal(ks[4], (D_MODEL, D_MODEL), dtype=jnp.float32) * s, 'Wv': jax.random.normal(ks[5], (D_MODEL, D_MODEL), dtype=jnp.float32) * s, 'Wproj': jax.random.normal(ks[6], (D_MODEL, D_MODEL), dtype=jnp.float32) * s}
    _L0_attn_a_in = _L0_attn_a_setup()

    def _L0_attn_b_setup():
        import jax, jax.numpy as jnp
        import numpy as np
        import math
        B, N, D = (64, 64, 128)
        SHELL_DIM, RFF_DIM, ORDER = (64, 32, 4)
        CHARGE_COUPLING, SHELL_COUPLING = (1.0, 0.5)
        DIST_COUPLING, DIST_SCALE = (0.3, 10.0)
        COMBINED_DIM = 64

        def _forward(x, W_charge, b_charge, W_shell, b_shell, omega, rff_bias, W_combine, W_v, b_v, W_out, b_out, log_temp):
            b, n, d = x.shape
            q = jnp.tanh(x @ W_charge.T + b_charge)[..., 0]
            coeffs = jnp.asarray([(-CHARGE_COUPLING) ** m / math.factorial(m) for m in range(ORDER + 1)], dtype=x.dtype)
            mags = jnp.sqrt(jnp.abs(coeffs) + 1e-10)
            phi_c = mags * q[..., None] ** jnp.arange(ORDER + 1)
            shell = x @ W_shell.T + b_shell
            shell = shell / jnp.maximum(jnp.linalg.norm(shell, axis=-1, keepdims=True), 1e-12)
            proj = shell @ omega.T + rff_bias
            rff_scale = math.sqrt(2.0 / (2 * RFF_DIM)) * math.sqrt(math.exp(-SHELL_COUPLING))
            phi_s = jnp.concatenate([jnp.cos(proj), jnp.sin(proj)], axis=-1) * rff_scale
            tp = (phi_c[..., :, None] * phi_s[..., None, :]).reshape(b, n, -1)
            phi = tp @ W_combine.T
            idx = jnp.arange(n)
            T = jnp.exp(-DIST_COUPLING * jnp.abs(idx[:, None] - idx[None, :]).astype(x.dtype) / DIST_SCALE)
            temp = jax.nn.softplus(log_temp) + 0.1
            logits = jnp.einsum('bnd,bmd->bnm', phi, phi) * T / temp
            causal = idx[:, None] >= idx[None, :]
            logits = jnp.where(causal, logits, -jnp.inf)
            attn = jax.nn.softmax(logits, axis=-1)
            V = x @ W_v.T + b_v
            out = jnp.einsum('bnm,bmd->bnd', attn, V)
            return out @ W_out.T + b_out
        key = jax.random.key(seed)
        ks = jax.random.split(key, 12)
        s = 0.02
        inp = {'x': jax.random.normal(ks[0], (B, N, D), dtype=jnp.float32), 'W_charge': jax.random.normal(ks[1], (1, D), dtype=jnp.float32) * s, 'b_charge': jnp.zeros((1,), dtype=jnp.float32), 'W_shell': jax.random.normal(ks[2], (SHELL_DIM, D), dtype=jnp.float32) * s, 'b_shell': jnp.zeros((SHELL_DIM,), dtype=jnp.float32), 'omega': jax.random.normal(ks[3], (RFF_DIM, SHELL_DIM), dtype=jnp.float32) * math.sqrt(SHELL_COUPLING), 'rff_bias': jax.random.uniform(ks[4], (RFF_DIM,), dtype=jnp.float32) * (2.0 * math.pi), 'W_combine': jax.random.normal(ks[5], (COMBINED_DIM, (ORDER + 1) * 2 * RFF_DIM), dtype=jnp.float32) * s, 'W_v': jax.random.normal(ks[6], (D, D), dtype=jnp.float32) * s, 'b_v': jnp.zeros((D,), dtype=jnp.float32), 'W_out': jax.random.normal(ks[7], (D, D), dtype=jnp.float32) * s, 'b_out': jnp.zeros((D,), dtype=jnp.float32), 'log_temp': jnp.zeros((), dtype=jnp.float32)}
        return inp
    _L0_attn_b_in = _L0_attn_b_setup()

    def _L0_ffn_setup():
        import jax, jax.numpy as jnp
        import numpy as np
        LN_EPS = 1e-05

        def layer_norm(x, g, b):
            mu = jnp.mean(x, axis=-1, keepdims=True)
            var = jnp.var(x, axis=-1, keepdims=True)
            return (x - mu) / jnp.sqrt(var + LN_EPS) * g + b

        def balanced_assignment(scores):
            T, E = scores.shape
            C = T // E
            taken = jnp.zeros((T,), dtype=bool)
            parts = []
            for e in range(E):
                s = jnp.where(taken, -jnp.inf, scores[:, e])
                _, idx = jax.lax.top_k(s, C)
                parts.append(idx)
                taken = taken.at[idx].set(True)
            return jnp.concatenate(parts)
        key = jax.random.key(seed)
        ks = jax.random.split(key, 4)
        B, S, D, F, E = (4, 256, 128, 512, 8)
        return {'x': jax.random.normal(ks[0], (B, S, D), dtype=jnp.float32), 'centroids': jax.random.normal(ks[1], (E, D), dtype=jnp.float32) * 0.1, 'ln_g': jnp.ones((D,), dtype=jnp.float32), 'ln_b': jnp.zeros((D,), dtype=jnp.float32), 'w1': jax.random.normal(ks[2], (E, D, F), dtype=jnp.float32) * 0.02, 'b1': jnp.zeros((E, F), dtype=jnp.float32), 'w2': jax.random.normal(ks[3], (E, F, D), dtype=jnp.float32) * 0.02, 'b2': jnp.zeros((E, D), dtype=jnp.float32)}
    _L0_ffn_in = _L0_ffn_setup()
    _d = {'L0_attn_a_x': _L0_attn_a_in['x'], 'L0_attn_a_Wq': _L0_attn_a_in['Wq'], 'L0_attn_a_Wk': _L0_attn_a_in['Wk'], 'L0_attn_a_Wq2': _L0_attn_a_in['Wq2'], 'L0_attn_a_Wk2': _L0_attn_a_in['Wk2'], 'L0_attn_a_Wv': _L0_attn_a_in['Wv'], 'L0_attn_a_Wproj': _L0_attn_a_in['Wproj'], 'L0_attn_b_W_charge': _L0_attn_b_in['W_charge'], 'L0_attn_b_b_charge': _L0_attn_b_in['b_charge'], 'L0_attn_b_W_shell': _L0_attn_b_in['W_shell'], 'L0_attn_b_b_shell': _L0_attn_b_in['b_shell'], 'L0_attn_b_omega': _L0_attn_b_in['omega'], 'L0_attn_b_rff_bias': _L0_attn_b_in['rff_bias'], 'L0_attn_b_W_combine': _L0_attn_b_in['W_combine'], 'L0_attn_b_W_v': _L0_attn_b_in['W_v'], 'L0_attn_b_b_v': _L0_attn_b_in['b_v'], 'L0_attn_b_W_out': _L0_attn_b_in['W_out'], 'L0_attn_b_b_out': _L0_attn_b_in['b_out'], 'L0_attn_b_log_temp': _L0_attn_b_in['log_temp'], 'L0_ffn_centroids': _L0_ffn_in['centroids'], 'L0_ffn_ln_g': _L0_ffn_in['ln_g'], 'L0_ffn_ln_b': _L0_ffn_in['ln_b'], 'L0_ffn_w1': _L0_ffn_in['w1'], 'L0_ffn_b1': _L0_ffn_in['b1'], 'L0_ffn_w2': _L0_ffn_in['w2'], 'L0_ffn_b2': _L0_ffn_in['b2']}
    _x0 = _d['L0_attn_a_x']
    _d['L0_attn_a_x'] = jax.random.normal(jax.random.fold_in(jax.random.key(seed), 1), (32, 256, 128), dtype=_x0.dtype)
    del _x0
    return _d

def reference(L0_attn_a_x, L0_attn_a_Wq, L0_attn_a_Wk, L0_attn_a_Wq2, L0_attn_a_Wk2, L0_attn_a_Wv, L0_attn_a_Wproj, L0_attn_b_W_charge, L0_attn_b_b_charge, L0_attn_b_W_shell, L0_attn_b_b_shell, L0_attn_b_omega, L0_attn_b_rff_bias, L0_attn_b_W_combine, L0_attn_b_W_v, L0_attn_b_b_v, L0_attn_b_W_out, L0_attn_b_b_out, L0_attn_b_log_temp, L0_ffn_centroids, L0_ffn_ln_g, L0_ffn_ln_b, L0_ffn_w1, L0_ffn_b1, L0_ffn_w2, L0_ffn_b2):

    def _L0_attn_a_ref(x, Wq, Wk, Wq2, Wk2, Wv, Wproj):
        import jax, jax.numpy as jnp
        import numpy as np
        D_MODEL = 128
        N_HEAD = 16
        HEAD_DIM = D_MODEL // N_HEAD
        B, T = (2, 256)
        ROPE_BASE = 10000.0

        def _rotary_cos_sin(seq_len, head_dim, dtype):
            inv_freq = 1.0 / ROPE_BASE ** (jnp.arange(0, head_dim, 2, dtype=jnp.float32) / head_dim)
            t = jnp.arange(seq_len, dtype=jnp.float32)
            freqs = jnp.outer(t, inv_freq)
            cos = jnp.cos(freqs).astype(dtype)[None, :, None, :]
            sin = jnp.sin(freqs).astype(dtype)[None, :, None, :]
            return (cos, sin)

        def _apply_rotary(x, cos, sin):
            d = x.shape[3] // 2
            x1, x2 = (x[..., :d], x[..., d:])
            y1 = x1 * cos + x2 * sin
            y2 = -x1 * sin + x2 * cos
            return jnp.concatenate([y1, y2], axis=3).astype(x.dtype)
        Bx, Tx, C = x.shape
        H, Dh = (N_HEAD, HEAD_DIM)

        def proj(W):
            return (x @ W.T).reshape(Bx, Tx, H, Dh)
        q, k, q2, k2, v = (proj(Wq), proj(Wk), proj(Wq2), proj(Wk2), proj(Wv))
        cos, sin = _rotary_cos_sin(Tx, Dh, x.dtype)
        q = _apply_rotary(q, cos, sin)
        k = _apply_rotary(k, cos, sin)
        q2 = _apply_rotary(q2, cos, sin)
        k2 = _apply_rotary(k2, cos, sin)
        scores = jnp.einsum('bqhd,bkhd->bhqk', q, k)
        scores2 = jnp.einsum('bqhd,bkhd->bhqk', q2, k2)
        pattern = scores / Dh * (scores2 / Dh)
        causal = jnp.tril(jnp.ones((Tx, Tx), dtype=bool))
        pattern = jnp.where(causal[None, None, :, :], pattern, 0.0)
        z = jnp.einsum('bhqk,bkhd->bhqd', pattern, v)
        y = z.transpose(0, 2, 1, 3).reshape(Bx, Tx, C)
        return y @ Wproj.T

    def _L0_attn_b_ref(x, W_charge, b_charge, W_shell, b_shell, omega, rff_bias, W_combine, W_v, b_v, W_out, b_out, log_temp):
        import jax, jax.numpy as jnp
        import numpy as np
        import math
        B, N, D = (64, 64, 128)
        SHELL_DIM, RFF_DIM, ORDER = (64, 32, 4)
        CHARGE_COUPLING, SHELL_COUPLING = (1.0, 0.5)
        DIST_COUPLING, DIST_SCALE = (0.3, 10.0)
        COMBINED_DIM = 64

        def _forward(x, W_charge, b_charge, W_shell, b_shell, omega, rff_bias, W_combine, W_v, b_v, W_out, b_out, log_temp):
            b, n, d = x.shape
            q = jnp.tanh(x @ W_charge.T + b_charge)[..., 0]
            coeffs = jnp.asarray([(-CHARGE_COUPLING) ** m / math.factorial(m) for m in range(ORDER + 1)], dtype=x.dtype)
            mags = jnp.sqrt(jnp.abs(coeffs) + 1e-10)
            phi_c = mags * q[..., None] ** jnp.arange(ORDER + 1)
            shell = x @ W_shell.T + b_shell
            shell = shell / jnp.maximum(jnp.linalg.norm(shell, axis=-1, keepdims=True), 1e-12)
            proj = shell @ omega.T + rff_bias
            rff_scale = math.sqrt(2.0 / (2 * RFF_DIM)) * math.sqrt(math.exp(-SHELL_COUPLING))
            phi_s = jnp.concatenate([jnp.cos(proj), jnp.sin(proj)], axis=-1) * rff_scale
            tp = (phi_c[..., :, None] * phi_s[..., None, :]).reshape(b, n, -1)
            phi = tp @ W_combine.T
            idx = jnp.arange(n)
            T = jnp.exp(-DIST_COUPLING * jnp.abs(idx[:, None] - idx[None, :]).astype(x.dtype) / DIST_SCALE)
            temp = jax.nn.softplus(log_temp) + 0.1
            logits = jnp.einsum('bnd,bmd->bnm', phi, phi) * T / temp
            causal = idx[:, None] >= idx[None, :]
            logits = jnp.where(causal, logits, -jnp.inf)
            attn = jax.nn.softmax(logits, axis=-1)
            V = x @ W_v.T + b_v
            out = jnp.einsum('bnm,bmd->bnd', attn, V)
            return out @ W_out.T + b_out
        return _forward(x, W_charge, b_charge, W_shell, b_shell, omega, rff_bias, W_combine, W_v, b_v, W_out, b_out, log_temp)

    def _L0_ffn_ref(x, centroids, ln_g, ln_b, w1, b1, w2, b2):
        import jax, jax.numpy as jnp
        import numpy as np
        LN_EPS = 1e-05

        def layer_norm(x, g, b):
            mu = jnp.mean(x, axis=-1, keepdims=True)
            var = jnp.var(x, axis=-1, keepdims=True)
            return (x - mu) / jnp.sqrt(var + LN_EPS) * g + b

        def balanced_assignment(scores):
            T, E = scores.shape
            C = T // E
            taken = jnp.zeros((T,), dtype=bool)
            parts = []
            for e in range(E):
                s = jnp.where(taken, -jnp.inf, scores[:, e])
                _, idx = jax.lax.top_k(s, C)
                parts.append(idx)
                taken = taken.at[idx].set(True)
            return jnp.concatenate(parts)
        D = x.shape[-1]
        feat = x.reshape(-1, D)
        T = feat.shape[0]
        E = centroids.shape[0]
        C = T // E
        norm = layer_norm(feat, ln_g, ln_b)
        scores = jax.lax.stop_gradient(norm @ centroids.T)
        sort_by_expert = balanced_assignment(scores)
        routed = feat[sort_by_expert].reshape(E, C, D)
        h = layer_norm(routed, ln_g, ln_b)
        h = jax.nn.gelu(jnp.einsum('ecd,edf->ecf', h, w1) + b1[:, None, :])
        h = jnp.einsum('ecf,efd->ecd', h, w2) + b2[:, None, :]
        out = routed + h
        inv = jnp.zeros((T,), dtype=jnp.int32).at[sort_by_expert].set(jnp.arange(T, dtype=jnp.int32))
        return out.reshape(T, D)[inv].reshape(x.shape)
    x = L0_attn_a_x
    x = x + _L0_attn_a_ref(_layernorm(x, axis=-1), L0_attn_a_Wq, L0_attn_a_Wk, L0_attn_a_Wq2, L0_attn_a_Wk2, L0_attn_a_Wv, L0_attn_a_Wproj)
    x = x + _L0_ffn_ref(_layernorm(x, axis=-1), L0_ffn_centroids, L0_ffn_ln_g, L0_ffn_ln_b, L0_ffn_w1, L0_ffn_b1, L0_ffn_w2, L0_ffn_b2)
    x = x + _L0_attn_b_ref(_layernorm(x, axis=-1), L0_attn_b_W_charge, L0_attn_b_b_charge, L0_attn_b_W_shell, L0_attn_b_b_shell, L0_attn_b_omega, L0_attn_b_rff_bias, L0_attn_b_W_combine, L0_attn_b_W_v, L0_attn_b_b_v, L0_attn_b_W_out, L0_attn_b_b_out, L0_attn_b_log_temp)
    x = x + _L0_ffn_ref(_layernorm(x, axis=-1), L0_ffn_centroids, L0_ffn_ln_g, L0_ffn_ln_b, L0_ffn_w1, L0_ffn_b1, L0_ffn_w2, L0_ffn_b2)
    return x

_drawn_inputs = setup_inputs


def setup_inputs(seed=0):
    import zlib

    import numpy as np

    out = dict(_drawn_inputs(seed))
    spreads = {'L0_attn_b_b_shell': (0.0, 0.8),
     'L0_attn_b_b_v': (0.0, 0.8),
     'L0_attn_b_b_out': (0.0, 0.1),
     'L0_ffn_ln_g': (1.0, 0.2),
     'L0_ffn_ln_b': (0.0, 2.0),
     'L0_ffn_b1': (0.0, 0.506),
     'L0_ffn_b2': (0.0, 0.1)}
    factors = {'L0_attn_b_W_charge': 8.0,
     'L0_attn_b_W_shell': 8.0,
     'L0_attn_b_omega': 8.0,
     'L0_attn_b_rff_bias': 8.0,
     'L0_attn_b_W_combine': 8.0,
     'L0_attn_b_W_v': 8.0,
     'L0_attn_b_W_out': 6.293}
    for name, (base, spread) in spreads.items():
        noise = np.random.default_rng([zlib.crc32(name.encode()), seed]).standard_normal(out[name].shape)
        drawn = base * np.exp(spread * noise) if base else spread * noise
        out[name] = jnp.asarray(drawn.astype(out[name].dtype))
    for name, factor in factors.items():
        out[name] = (out[name] * factor).astype(out[name].dtype)
    return out
```

```python
import math
from contextlib import ExitStack

import concourse.bass as bass
from concourse import mybir

F32 = mybir.dt.float32
BF16 = mybir.dt.bfloat16
I32 = mybir.dt.int32
U32 = mybir.dt.uint32
ALU = mybir.AluOpType
ACT = mybir.ActivationFunctionType
AX = mybir.AxisListType

P = 128
D = 128
B, T = 32, 256
TOKENS = B * T
TILES = TOKENS // P
PER = T // P
H = 16
DH = D // H
E = 8
CAP = TOKENS // E
F = 512
FC = F // P
SLOTS = CAP // P
SHELL, RFF, ORDER = 64, 32, 4
NM = ORDER + 1
FEAT = SHELL + 1 + RFF
EPS = 1e-5
GROUP = 4
PASSES = 8
CANDS = 15
TAKEN = -1.5e38
ROUND = 1.5 * 2.0**23
TWO_PI = (6.28125, 0.0019350051879882812, 3.0199159819567e-07)
PI = 3.1415925
ROOM = 1


def wait_apart(eng, semaphore, value, passed):
    eng.wait_ge(semaphore, value)
    eng.sem_inc(passed, 1)


class Chain:

    def __init__(self, eng, sem):
        self.eng, self.sem, self.n = eng, sem, 0

    def __call__(self, ins):
        self.n += 1
        ins.then_inc(self.sem, 1)
        self.eng.wait_ge(self.sem, self.n)


def phase(nc, body, *args):
    used = []

    def sem(name):
        used.append(nc.alloc_semaphore(name))
        return used[-1]

    body(nc, sem, *args)
    nc.clear_and_free_semaphores(used)
    nc.all_engine_barrier()


def build(nc, d):
    with ExitStack() as whole:
        def keep(name, shape, dt=F32):
            return whole.enter_context(nc.sbuf_tensor(name, shape, dt))

        k = {
            "x": keep("x", [P, TILES, D]),
            "ident": keep("ident", [P, P]),
            "rstd": keep("rstd", [P, TILES]),
            "shift": keep("shift", [P, TILES]),
            "scores": keep("scores", [P, E, TILES]),
        }
        norm_rows = nc.dram_tensor("norm_rows", (TOKENS, D), F32, kind="Internal").ap()
        ffn_rows = nc.dram_tensor("ffn_rows", (TOKENS, D), F32, kind="Internal").ap()
        phase(nc, load_x, d, k)
        phase(nc, statistics, k, k["x"], "a")
        phase(nc, attention_a, d, k)
        phase(nc, normalise_for_experts, d, k, norm_rows, 0)
        phase(nc, experts, d, k, norm_rows, ffn_rows, 0)
        phase(nc, add_rows, k, ffn_rows, None, 0)
        phase(nc, statistics, k, k["x"], "b")
        phase(nc, attention_b, d, k)
        phase(nc, normalise_for_experts, d, k, norm_rows, 1)
        phase(nc, experts, d, k, norm_rows, ffn_rows, 1)
        phase(nc, add_rows, k, ffn_rows, d["out"], 1)


def load_x(nc, sem, d, k):
    loaded = sem("x_loaded")
    x_dram = d["L0_attn_a_x"].rearrange("b (t p) d -> p (b t) d", p=P)
    with nc.Block() as block:
        @block.sync
        def _(sp):
            for q in range(4):
                part = slice(q * TILES // 4, (q + 1) * TILES // 4)
                sp.dma_start(k["x"][:, part, :], x_dram[:, part, :]).then_inc(loaded, 16)
            sp.dma_start(k["ident"][:], d["c_ident"]).then_inc(loaded, 16)
            sp.wait_ge(loaded, 80)


def statistics(nc, sem, k, src, tag):
    with ExitStack() as ctx:
        def sb(name, shape, dt=F32):
            return ctx.enter_context(nc.sbuf_tensor(f"{name}_{tag}", shape, dt))

        halves = sb("halves", [P, TILES, 6])
        moment = sb("moment", [P, TILES])
        gap = sb("gap", [P, TILES])
        gap2 = sb("gap2", [P, TILES])
        var = sb("var", [P, TILES])
        std = sb("std", [P, TILES])
        msum = sb("msum", [P, TILES])
        eps = sb("eps", [P, 1])
        halves_done = sem(f"halves_done_{tag}")
        step = sem(f"stat_step_{tag}")
        var_done = sem(f"var_done_{tag}")
        std_done = sem(f"std_done_{tag}")
        with nc.Block() as block:
            @block.vector
            def _(dve):
                link = Chain(dve, step)
                link(dve.memset(eps[:], EPS))
                with dve.Fori(0, TILES // 4) as i:
                    for j in range(4):
                        dve.bn_stats(halves[:, 4 * i + j, :], src[:, 4 * i + j, :]).then_inc(halves_done, 1)
                dve.wait_ge(halves_done, TILES)
                link(dve.tensor_tensor(moment[:], halves[:, :, 2], halves[:, :, 5], ALU.add))
                link(dve.tensor_tensor(gap[:], halves[:, :, 1], halves[:, :, 4], ALU.subtract))
                link(dve.tensor_tensor(msum[:], halves[:, :, 1], halves[:, :, 4], ALU.add))
                link(dve.tensor_tensor(gap2[:], gap[:], gap[:], ALU.mult))
                dve.scalar_tensor_tensor(var[:], gap2[:], D / 4.0, moment[:], ALU.mult, ALU.add).then_inc(var_done, 1)
                dve.wait_ge(std_done, 1)
                link(dve.reciprocal(k["rstd"][:], std[:]))
                link(dve.scalar_tensor_tensor(k["shift"][:], msum[:], -0.5, k["rstd"][:], ALU.mult, ALU.mult))

            @block.scalar
            def _(act):
                act.wait_ge(step, 1)
                act.wait_ge(var_done, 1)
                act.activation(std[:], var[:], ACT.Sqrt, bias=eps[:], scale=1.0 / D).then_inc(std_done, 1)


def attention_a(nc, sem, d, k):
    with ExitStack() as ctx:
        def sb(name, shape, dt=F32):
            return ctx.enter_context(nc.sbuf_tensor(f"{name}_aa", shape, dt))

        def ps(name):
            return ctx.enter_context(nc.psum_tensor(f"{name}_aa", [P, 512], F32))

        w_rope = sb("w_rope", [P, 4, 2, D])
        w_v = sb("w_v", [P, D])
        w_proj = sb("w_proj", [P, 4, D])
        rope = sb("rope", [P, 2, T])
        xn = sb("xn", [P, PER, D])
        xn_t = sb("xn_t", [P, T])
        turned = sb("turned", [P, 2, 2, T])
        qr = sb("qr", [P, 2, T])
        kr = [sb(f"kr{i}", [P, 2, T]) for i in range(2)]
        q_spread = [sb(f"q_spread{i}", [P, H, 2, T]) for i in range(2)]
        v = [sb(f"v{i}", [P, PER, H, 32]) for i in range(2)]
        s2 = [sb(f"s2_{i}", [P, 384]) for i in range(2)]
        patt = [sb(f"patt{i}", [P, 384]) for i in range(4)]
        z_t = sb("z_t", [P, 4, T])
        p_s1 = [ps(f"p_s1_{i}") for i in range(2)]
        p_s2 = [ps(f"p_s2_{i}") for i in range(2)]
        p_rope = [ps(f"p_rope{i}") for i in range(2)]
        p_misc = ps("p_misc")
        p_z = ps("p_z")

        weights = sem("aa_weights_loaded")
        cleared = sem("aa_cleared")
        xn_done = sem("aa_xn_done")
        xt_done = sem("aa_xt_done")
        xt_copied = sem("aa_xt_copied")
        v_done = sem("aa_v_done")
        v_copied = sem("aa_v_copied")
        rope_done = sem("aa_rope_products_done")
        turned_done = sem("aa_turned_done")
        added_k = sem("aa_keys_added")
        added_q = sem("aa_queries_added")
        spread = [sem(f"aa_spread{i}") for i in range(2)]
        s_done = sem("aa_scores_done")
        s2_copied = sem("aa_s2_copied")
        patt_done = sem("aa_pattern_done")
        masked = sem("aa_masked")
        z_head = sem("aa_z_head_done")
        z_copied = sem("aa_z_copied")
        y_done = sem("aa_y_done")
        x_added = sem("aa_x_added")
        passed = sem("aa_passed")

        def plan(step, prep):
            with nc_loop(step) as i:
                for par in range(2):
                    prep(2 * i + par, par, i, True)
            prep(B - 2, 0, (B - 2) // 2, True)
            prep(B - 1, 1, (B - 2) // 2, False)

        def nc_loop(eng):
            return eng.Fori(0, (B - 2) // 2)

        with nc.Block() as block:
            @block.sync
            def _(sp):
                for counter in (z_head, y_done, x_added, z_copied):
                    sp.sem_inc(counter, ROOM)
                sp.dma_start(w_rope[:], d["w_rope"]).then_inc(weights, 16)
                sp.dma_start(w_v[:], d["w_v_t"]).then_inc(weights, 16)
                sp.dma_start(w_proj[:], d["w_proj_pad"]).then_inc(weights, 16)
                sp.dma_start(rope[:], d["c_rope"]).then_inc(weights, 16)
                sp.wait_ge(cleared, 4)

                def queries(g, par):
                    sp.wait_ge(added_q, g + 1)
                    for h in range(H):
                        rows = slice(DH * h, DH * h + DH)
                        sp.dma_start(q_spread[par][rows, h, :, :], qr[rows, :, :]).then_inc(spread[par], 16)

                queries(0, 0)

                def turn(g, par, i, more):
                    if more:
                        queries(g + 1, 1 - par)

                plan(sp, turn)

            @block.gpsimd
            def _(pool):
                for t in (q_spread[0], q_spread[1], v[0], v[1]):
                    pool.memset(t[:], 0.0).then_inc(cleared, 1)

                def keys(g, par):
                    pool.wait_ge(turned_done, 4 * g + 2)
                    pool.tensor_tensor(kr[par][:], turned[:, :, 0, :], turned[:, :, 1, :], ALU.add).then_inc(added_k, 1)

                def queries(g, par, last_spread=None):
                    pool.wait_ge(turned_done, 4 * g + 4)
                    if last_spread is not None:
                        pool.wait_ge(*last_spread)
                    pool.tensor_tensor(qr[:], turned[:, :, 0, :], turned[:, :, 1, :], ALU.add).then_inc(added_q, 1)

                keys(0, 0)
                queries(0, 0)

                def turn(g, par, i, more):
                    for h in range(H):
                        wait_apart(pool, patt_done, H * g + h + 1, passed)
                        diag = patt[h % 4][:, :].rearrange("p (c q) -> p c q", q=P)[:, 0:3:2, :]
                        pool.affine_select(out=diag, in_=diag, pattern=[[0, 2], [1, P]], compare_op=ALU.is_ge,
                                           fill=0.0, base=0, channel_multiplier=-1).then_inc(masked, 1)
                        if more and h == 8:
                            keys(g + 1, 1 - par)
                        if more and h == 12:
                            queries(g + 1, 1 - par, (spread[par], 256 * i + 256))

                plan(pool, turn)

            @block.scalar
            def _(act):
                act.wait_ge(cleared, 4)

                def normalise(g):
                    for t in range(PER):
                        n = PER * g + t
                        act.activation(xn[:, t, :], k["x"][:, n, :], ACT.Identity, bias=k["shift"][:, n:n + 1] if isinstance(n, int) else k["shift"][:, bass.ds(n, 1)],
                                       scale=k["rstd"][:, n:n + 1] if isinstance(n, int) else k["rstd"][:, bass.ds(n, 1)]).then_inc(xn_done, 1)

                def copy_xt(g):
                    act.wait_ge(xt_done, g + 1)
                    act.activation(xn_t[:], p_misc[:, 0:T], ACT.Identity).then_inc(xt_copied, 1)

                def copy_v(g, par):
                    act.wait_ge(v_done, g + 1)
                    act.activation(v[par][:, :, :, 0:DH], p_misc[:, T:2 * T].rearrange("p (t h e) -> p t h e", t=PER, e=DH),
                                   ACT.Identity).then_inc(v_copied, 1)

                normalise(0)
                copy_xt(0)
                copy_v(0, 0)

                def turn(g, par, i, more):
                    for h in range(H):
                        act.wait_ge(s_done, H * g + h + 1)
                        if h >= 2:
                            act.wait_ge(patt_done, H * g + h - 1)
                        else:
                            act.wait_ge(z_head, ROOM + H * g)
                        act.activation(s2[h % 2][:], p_s2[h % 2][:, 0:384], ACT.Identity).then_inc(s2_copied, 1)
                        if more and h == 0:
                            normalise(g + 1)
                        if more and h == 3:
                            copy_xt(g + 1)
                        if more and h == 5:
                            copy_v(g + 1, 1 - par)
                        if h == 9:
                            act.wait_ge(z_head, ROOM + H * g + 8)
                            act.wait_ge(y_done, ROOM + g)
                            act.activation(z_t[:, 0:2, :], p_z[:, :].rearrange("p (c q) -> p c q", c=2), ACT.Identity).then_inc(z_copied, 1)
                    act.wait_ge(z_head, ROOM + H * g + H)
                    act.activation(z_t[:, 2:4, :], p_z[:, :].rearrange("p (c q) -> p c q", c=2), ACT.Identity).then_inc(z_copied, 1)

                plan(act, turn)

            @block.vector
            def _(dve):
                dve.wait_ge(weights, 64)

                def turn_pair(g, which):
                    dve.wait_ge(rope_done, 2 * g + which + 1)
                    if which:
                        dve.wait_ge(added_k, g + 1)
                    else:
                        dve.wait_ge(added_q, g)
                    for term in range(2):
                        dve.tensor_tensor(turned[:, :, term, :], p_rope[term][:, :].rearrange("p (a q) -> p a q", a=2),
                                          rope[:, term:term + 1, :].broadcast_to([P, 2, T]), ALU.mult).then_inc(turned_done, 1)

                turn_pair(0, 0)
                turn_pair(0, 1)

                def turn(g, par, i, more):
                    for h in range(H):
                        dve.wait_ge(s2_copied, H * g + h + 1)
                        if h >= 4:
                            dve.wait_ge(z_head, ROOM + H * g + h - 3)
                        dve.tensor_tensor(patt[h % 4][:], p_s1[h % 2][:, 0:384], s2[h % 2][:], ALU.mult).then_inc(patt_done, 1)
                        if more and h == 7:
                            turn_pair(g + 1, 0)
                        if more and h == 11:
                            turn_pair(g + 1, 1)
                    dve.wait_ge(y_done, ROOM + g + 1)
                    xs = k["x"][:, bass.ds(PER * g, PER), :] if not isinstance(g, int) else k["x"][:, PER * g:PER * g + PER, :]
                    dve.scalar_tensor_tensor(xs, p_misc[:, 0:T].rearrange("p (t e) -> p t e", t=PER), 1.0 / (DH * DH),
                                             xs, ALU.mult, ALU.add).then_inc(x_added, 1)

                plan(dve, turn)

            @block.tensor
            def _(pe):
                pe.wait_ge(weights, 64)

                def transposes(g):
                    pe.wait_ge(xn_done, PER * g + PER)
                    for t in range(PER):
                        mm = pe.transpose(p_misc[:, t * P:(t + 1) * P], xn[:, t, :], k["ident"][:])
                    mm.then_inc(xt_done, 1)

                def values(g):
                    pe.wait_ge(xt_copied, g + 1)
                    for t in range(PER):
                        mm = pe.matmul(p_misc[:, T + t * P:T + (t + 1) * P], xn_t[:, t * P:(t + 1) * P], w_v[:],
                                       start=True, stop=True)
                    mm.then_inc(v_done, 1)

                def rope_products(g, which):
                    if which:
                        pe.wait_ge(turned_done, 4 * g + 2)
                    else:
                        pe.wait_ge(turned_done, 4 * g)
                    for term in range(2):
                        for a in range(2):
                            mm = pe.matmul(p_rope[term][:, a * T:(a + 1) * T], w_rope[:, 2 * which + a, term, :], xn_t[:],
                                           start=True, stop=True)
                    mm.then_inc(rope_done, 1)

                def z(g, par, h):
                    pe.wait_ge(masked, H * g + h + 1)
                    if h == 0:
                        pe.wait_ge(v_copied, g + 1)
                        pe.wait_ge(z_copied, ROOM + 2 * g)
                    if h == 8:
                        pe.wait_ge(z_copied, ROOM + 2 * g + 1)
                    c = h % 4
                    out = p_z[32 * c:32 * c + 32, (h // 4 % 2) * T:(h // 4 % 2 + 1) * T]
                    pe.matmul(out, v[par][:, 0, h, :], patt[h % 4][:, 0:T], start=True, stop=False)
                    pe.matmul(out[:, P:T], v[par][:, 1, h, :], patt[h % 4][:, T:384], start=False, stop=True,
                              ).then_inc(z_head, 1)

                def output(g):
                    pe.wait_ge(z_copied, ROOM + 2 * g + 2)
                    for t in range(PER):
                        for j in range(4):
                            mm = pe.matmul(p_misc[:, t * P:(t + 1) * P], z_t[:, j, t * P:(t + 1) * P], w_proj[:, j, :],
                                           start=(j == 0), stop=(j == 3))
                    mm.then_inc(y_done, 1)

                transposes(0)
                values(0)
                rope_products(0, 0)
                rope_products(0, 1)

                def turn(g, par, i, more):
                    pe.wait_ge(added_k, g + 1)
                    pe.wait_ge(spread[par], 256 * i + 256)
                    for h in range(H):
                        if h >= 2:
                            pe.wait_ge(patt_done, H * g + h - 1)
                        for a, bank in enumerate((p_s2[h % 2], p_s1[h % 2])):
                            pe.matmul(bank[:, 0:T], kr[par][:, a, 0:P], q_spread[par][:, h, a, :], start=True, stop=True)
                            mm = pe.matmul(bank[:, T:384], kr[par][:, a, P:T], q_spread[par][:, h, a, P:T],
                                           start=True, stop=True)
                        mm.then_inc(s_done, 1)
                        if h >= 2:
                            z(g, par, h - 2)
                        if more and h == 2:
                            pe.wait_ge(x_added, ROOM + g)
                            transposes(g + 1)
                        if more and h == 4:
                            values(g + 1)
                        if more and h == 5:
                            rope_products(g + 1, 0)
                        if more and h == 9:
                            rope_products(g + 1, 1)
                    z(g, par, H - 2)
                    z(g, par, H - 1)
                    output(g)

                plan(pe, turn)


def normalise_for_experts(nc, sem, d, k, norm_rows, layer):
    tag = f"n{layer}"
    steps = TILES // GROUP
    with ExitStack() as outer:
        a = outer.enter_context(nc.sbuf_tensor(f"a_{tag}", [P, TILES, D], F32))
        statistics(nc, sem, k, k["x"], f"{tag}x")
        a_done = sem(f"a_done_{tag}")
        with nc.Block() as block:
            @block.scalar
            def _(act):
                with act.Fori(0, steps) as i:
                    for j in range(GROUP):
                        n = GROUP * i + j
                        act.activation(a[:, n, :], k["x"][:, n, :], ACT.Identity, bias=k["shift"][:, bass.ds(n, 1)],
                                       scale=k["rstd"][:, bass.ds(n, 1)]).then_inc(a_done, 1)

            @block.gpsimd
            def _(pool):
                with pool.Fori(0, steps) as i:
                    part = bass.ds(GROUP * i, GROUP)
                    pool.wait_ge(a_done, GROUP * i + GROUP)
                    pool.tensor_tensor(k["x"][:, part, :], k["x"][:, part, :], a[:, part, :], ALU.add)
        statistics(nc, sem, k, a, f"{tag}a")
        with ExitStack() as ctx:
            def sb(name, shape, dt=F32):
                return ctx.enter_context(nc.sbuf_tensor(f"{name}_{tag}", shape, dt))

            def ps(name):
                return ctx.enter_context(nc.psum_tensor(f"{name}_{tag}", [P, 512], F32))

            gain = sb("gain", [P, D])
            bias = sb("bias", [P, D])
            cent = sb("cent", [P, E])
            norm = [sb(f"norm{i}", [P, GROUP, D]) for i in range(2)]
            norm_t = [sb(f"norm_t{i}", [P, GROUP, P]) for i in range(2)]
            p_t = [ps(f"p_t{i}") for i in range(2)]
            p_sc = [ps(f"p_sc{i}") for i in range(2)]
            loaded = sem(f"gb_loaded_{tag}")
            scaled = sem(f"scaled_{tag}")
            gained = sem(f"gained_{tag}")
            norm_done = [sem(f"norm_done{i}_{tag}") for i in range(2)]
            stored = [sem(f"norm_stored{i}_{tag}") for i in range(2)]
            turned = [sem(f"turned{i}_{tag}") for i in range(2)]
            copied = [sem(f"turned_copied{i}_{tag}") for i in range(2)]
            scored = [sem(f"scored{i}_{tag}") for i in range(2)]
            kept = [sem(f"score_kept{i}_{tag}") for i in range(2)]
            rows = norm_rows.rearrange("(n p) d -> p n d", p=P)
            with nc.Block() as block:
                @block.sync
                def _(sp):
                    for counter in (*stored, *turned, *copied, *kept, *scored):
                        sp.sem_inc(counter, ROOM)
                    sp.dma_start(gain[:], d["L0_ffn_ln_g"].rearrange("(a d) -> a d", a=1).broadcast_to([P, D])).then_inc(loaded, 16)
                    sp.dma_start(bias[:], d["L0_ffn_ln_b"].rearrange("(a d) -> a d", a=1).broadcast_to([P, D])).then_inc(loaded, 16)
                    sp.dma_start(cent[:], d["centroids_t"]).then_inc(loaded, 16)
                    with sp.Fori(0, steps // 2) as i:
                        for par in range(2):
                            part = rows[:, bass.ds((2 * i + par) * GROUP, GROUP), :]
                            sp.wait_ge(norm_done[par], i + 1)
                            sp.dma_start(part, norm[par][:]).then_inc(stored[par], 16)
                    sp.wait_ge(stored[0], ROOM + 16 * (steps // 2))
                    sp.wait_ge(stored[1], ROOM + 16 * (steps // 2))

                @block.vector
                def _(dve):
                    dve.wait_ge(loaded, 48)
                    with dve.Fori(0, steps // 2) as i:
                        for par in range(2):
                            g = 2 * i + par
                            dve.wait_ge(stored[par], ROOM + 16 * i)
                            dve.wait_ge(turned[par], ROOM + i)
                            for j in range(GROUP):
                                n = GROUP * g + j
                                dve.tensor_scalar(norm[par][:, j, :], a[:, n, :], k["rstd"][:, bass.ds(n, 1)],
                                                  k["shift"][:, bass.ds(n, 1)], ALU.mult, ALU.add).then_inc(scaled, 1)
                            dve.wait_ge(scaled, GROUP * g + GROUP)
                            dve.tensor_tensor(norm[par][:], norm[par][:], gain[:, None, :].broadcast_to([P, GROUP, D]),
                                              ALU.mult).then_inc(gained, 1)
                            dve.wait_ge(gained, g + 1)
                            dve.tensor_tensor(norm[par][:], norm[par][:], bias[:, None, :].broadcast_to([P, GROUP, D]),
                                              ALU.add).then_inc(norm_done[par], 1)
                            dve.wait_ge(scored[par], ROOM + i + 1)
                            dve.tensor_copy(k["scores"][:, :, bass.ds(GROUP * g, GROUP)],
                                            p_sc[par][:, 0:GROUP * E].rearrange("p (n e) -> p e n", e=E)).then_inc(kept[par], 1)

                @block.tensor
                def _(pe):
                    pe.wait_ge(loaded, 48)
                    with pe.Fori(0, steps // 2) as i:
                        for par in range(2):
                            pe.wait_ge(norm_done[par], i + 1)
                            pe.wait_ge(copied[par], ROOM + i)
                            for j in range(GROUP):
                                mm = pe.transpose(p_t[par][:, j * P:(j + 1) * P], norm[par][:, j, :], k["ident"][:])
                            mm.then_inc(turned[par], 1)
                            pe.wait_ge(copied[par], ROOM + i + 1)
                            pe.wait_ge(kept[par], ROOM + i)
                            for j in range(GROUP):
                                mm = pe.matmul(p_sc[par][:, j * E:(j + 1) * E], norm_t[par][:, j, :], cent[:],
                                               start=True, stop=True)
                            mm.then_inc(scored[par], 1)

                @block.scalar
                def _(act):
                    with act.Fori(0, steps // 2) as i:
                        for par in range(2):
                            act.wait_ge(turned[par], ROOM + i + 1)
                            act.wait_ge(scored[par], ROOM + i)
                            act.activation(norm_t[par][:], p_t[par][:, :].rearrange("p (j q) -> p j q", j=GROUP),
                                           ACT.Identity).then_inc(copied[par], 1)


def experts(nc, sem, d, k, norm_rows, ffn_rows, layer):
    tag = f"e{layer}"
    with ExitStack() as ctx:
        def sb(name, shape, dt=F32):
            return ctx.enter_context(nc.sbuf_tensor(f"{name}_{tag}", shape, dt))

        def ps(name):
            return ctx.enter_context(nc.psum_tensor(f"{name}_{tag}", [P, 512], F32))

        first_cand = sb("first_cand", [P, CANDS])
        digits = sb("digits", [P, PASSES, CANDS], U32)
        weight = sb("weight", [P, PASSES])
        before = sb("before", [P, P], BF16)
        ones = sb("ones", [P, P], BF16)
        lanes = sb("lanes", [P, P], BF16)
        place = sb("place", [P, TILES, 2, SLOTS], BF16)
        eighth = sb("eighth", [P, 2, SLOTS], BF16)
        ones_f = sb("ones_f", [P, TILES])
        avail = sb("avail", [P, TILES])
        s = sb("s", [P, TILES])
        cand = sb("cand", [P, CANDS], U32)
        reach = sb("reach", [P, TILES, CANDS], BF16)
        count = sb("count", [P, CANDS])
        passed = sb("passed", [P, CANDS])
        found_f = sb("found_f", [P, 1])
        found = sb("found", [P, 1], U32)
        prefix = sb("prefix", [P, 1], U32)
        flip = sb("flip", [P, 1], U32)
        above = sb("above", [P, TILES], BF16)
        equal = sb("equal", [P, TILES], BF16)
        total = sb("total", [P, TILES])
        need = sb("need", [P, 1])
        rank = sb("rank", [P, TILES])
        within = sb("within", [P, TILES])
        chosen = sb("chosen", [P, TILES], BF16)
        slot = sb("slot", [P, TILES])
        slot_i = sb("slot_i", [P, TILES], I32)
        low = sb("low", [P, TILES], I32)
        high = sb("high", [P, TILES], I32)
        low_f = sb("low_f", [P, TILES])
        high_f = sb("high_f", [P, TILES])
        lane_of = sb("lane_of", [P, TILES, P], BF16)
        tile_of = sb("tile_of", [P, TILES, 2, SLOTS], BF16)
        tok_hi = sb("tok_hi", [P, SLOTS])
        index = [sb(f"index{i}", [P, SLOTS], U32) for i in range(2)]
        w1 = [sb(f"w1_{i}", [P, F]) for i in range(2)]
        w2 = [sb(f"w2_{i}", [P, FC, D]) for i in range(2)]
        b1 = [sb(f"b1_{i}", [P, FC]) for i in range(2)]
        b2 = [sb(f"b2_{i}", [P, D]) for i in range(2)]
        rows = [sb(f"rows{i}", [P, SLOTS, D]) for i in range(2)]
        rows_t = sb("rows_t", [P, CAP])
        hid = sb("hid", [P, FC, CAP])
        y = sb("y", [P, SLOTS, D])
        yb = [sb(f"yb{i}", [P, SLOTS, D]) for i in range(2)]
        p_cnt = ps("p_cnt")
        p_pre = ps("p_pre")
        p_tot = ps("p_tot")
        p_idx = ps("p_idx")
        p_t = ps("p_t")
        p_h = [ps(f"p_h{i}") for i in range(2)]
        p_y = ps("p_y")

        consts = sem(f"consts_{tag}")
        wl = [sem(f"expert_loaded{i}_{tag}") for i in range(2)]
        reached = sem(f"reached_{tag}")
        counted = sem(f"counted_{tag}")
        sv = sem(f"search_step_{tag}")
        marked = sem(f"marked_{tag}")
        ranked = sem(f"ranked_{tag}")
        onehot = sem(f"onehot_{tag}")
        listed = sem(f"listed_{tag}")
        index_done = sem(f"index_done_{tag}")
        gathered = [sem(f"gathered{i}_{tag}") for i in range(2)]
        rt_done = sem(f"rows_turned_{tag}")
        rt_copied = sem(f"rows_t_copied_{tag}")
        up_done = sem(f"up_done_{tag}")
        gelu_done = sem(f"gelu_done_{tag}")
        down_done = sem(f"down_done_{tag}")
        y_copied = sem(f"y_copied_{tag}")
        y_ready = sem(f"y_ready_{tag}")
        scattered = [sem(f"scattered{i}_{tag}") for i in range(2)]
        scatters_seen = sem(f"scatters_seen_{tag}")
        wait_passed = sem(f"passed_{tag}")

        def plan(eng, turn):
            turn(0, 0, 0, search=True, compute=False)
            with eng.Fori(0, (E - 2) // 2) as i:
                turn(2 * i + 1, 1, i, search=True, compute=True)
                turn(2 * i + 2, 0, i + 1, search=True, compute=True)
            turn(E - 1, 1, E // 2 - 1, search=False, compute=True)
            turn(E, 0, E // 2, search=None, compute=True)

        LINKS = 1 + 6 * PASSES + 2 - 1 + 1 + 6 + 14

        with nc.Block() as block:
            @block.sync
            def _(sp):
                for counter in (y_ready, scatters_seen, rt_copied, y_copied, up_done, down_done, rt_done):
                    sp.sem_inc(counter, ROOM)
                for dst, src in ((first_cand, "c_first_cand"), (digits, "c_digits"), (weight, "c_weight"),
                                 (before, "c_before"), (lanes, "c_lanes"), (place, "c_place"), (eighth, "c_eighth")):
                    sp.dma_start(dst[:], d[src]).then_inc(consts, 16)

                def turn(e, par, i, search, compute):
                    if search is None:
                        return
                    at = bass.ds(e, 1) if not isinstance(e, int) else slice(e, e + 1)
                    w1_src = d["L0_ffn_w1"][at, :, :].rearrange("a p f -> (a p) f")
                    w2_src = d["L0_ffn_w2"][at, :, :].rearrange("a (p c) n -> (a p) c n", c=FC)
                    b1_src = d["L0_ffn_b1"][at, :].rearrange("a (p c) -> (a p) c", c=FC)
                    b2_src = d["L0_ffn_b2"][at, :].broadcast_to([P, D])
                    if not isinstance(e, int) or e > 0:
                        sp.wait_ge(y_ready, ROOM + e - 1)
                    sp.dma_start(w1[par][:], w1_src).then_inc(wl[par], 16)
                    sp.dma_start(w2[par][:], w2_src).then_inc(wl[par], 16)
                    sp.dma_start(b1[par][:], b1_src).then_inc(wl[par], 16)
                    sp.dma_start(b2[par][:], b2_src).then_inc(wl[par], 16)

                plan(sp, turn)

            @block.vector
            def _(dve):
                dve.wait_ge(consts, 16 * 7)
                dve.memset(ones[:], 1.0).then_inc(sv, 1)
                dve.memset(ones_f[:], 1.0).then_inc(sv, 1)
                dve.memset(avail[:], -TAKEN).then_inc(sv, 1)
                dve.wait_ge(sv, 3)

                def turn(e, par, i, search, compute):
                    if search is None:
                        return
                    base = 3 + LINKS * e
                    done = [0]

                    def link(ins):
                        done[0] += 1
                        ins.then_inc(sv, 1)
                        dve.wait_ge(sv, base + done[0])

                    at = bass.ds(e, 1) if not isinstance(e, int) else slice(e, e + 1)
                    if search:
                        link(dve.tensor_tensor(s[:], k["scores"][:, at, :].rearrange("p a n -> p (a n)"), avail[:], ALU.min))
                        for n in range(PASSES):
                            c = (first_cand[:] if n == 0 else cand[:].bitcast(F32))[:, None, :].broadcast_to([P, TILES, CANDS])
                            dve.tensor_tensor(reach[:], s[:, :, None].broadcast_to([P, TILES, CANDS]), c,
                                              ALU.is_ge).then_inc(reached, 1)
                            dve.wait_ge(counted, PASSES * e + n + 1)
                            link(dve.tensor_reduce(count[:], p_cnt[:, 0:8 * CANDS].rearrange("p (n c) -> p c n", c=CANDS), AX.X, ALU.add))
                            link(dve.tensor_scalar(passed[:], count[:], float(CAP), weight[:, n:n + 1], ALU.is_ge, ALU.mult))
                            link(dve.tensor_reduce(found_f[:], passed[:], AX.X, ALU.add))
                            link(dve.tensor_copy(found[:], found_f[:]))
                            if n == 0:
                                link(dve.tensor_scalar(flip[:].bitcast(I32), found[:].bitcast(I32), -1, 31, ALU.bitwise_xor, ALU.arith_shift_right))
                                link(dve.tensor_scalar(flip[:].bitcast(I32), flip[:].bitcast(I32), -2**31, None, ALU.bitwise_or))
                                link(dve.tensor_tensor(prefix[:], found[:], flip[:], ALU.bitwise_xor))
                            else:
                                link(dve.tensor_tensor(prefix[:], prefix[:], found[:], ALU.bitwise_xor))
                            if n + 1 < PASSES:
                                link(dve.tensor_scalar(cand[:], digits[:, n + 1, :], prefix[:, 0:1], None, ALU.bitwise_xor))
                        limit = prefix[:].bitcast(F32)
                        link(dve.tensor_scalar(above[:], s[:], limit, None, ALU.is_gt))
                        dve.tensor_scalar(equal[:], s[:], limit, None, ALU.is_equal).then_inc(marked, 1)
                        dve.wait_ge(ranked, 2 * e + 1)
                        link(dve.tensor_reduce(need[:], p_idx[:, 0:TILES], AX.X, ALU.add))
                        link(dve.tensor_scalar(need[:], need[:], -1.0, float(CAP), ALU.mult, ALU.add))
                        link(dve.tensor_tensor_scan(total[:], ones_f[:], p_tot[:, 0:TILES], 0.0, ALU.mult, ALU.add))
                        link(dve.tensor_tensor(rank[:], total[:], p_tot[:, 0:TILES], ALU.subtract))
                        link(dve.tensor_tensor(rank[:], rank[:], p_pre[:, 0:TILES], ALU.add))
                        link(dve.scalar_tensor_tensor(within[:], rank[:], need[:, 0:1], equal[:], ALU.is_lt, ALU.mult))
                        dve.tensor_tensor(chosen[:], within[:], above[:], ALU.add).then_inc(marked, 1)
                    else:
                        dve.tensor_scalar(chosen[:], avail[:], 0.0, None, ALU.is_gt).then_inc(marked, 1)
                    dve.wait_ge(ranked, 2 * e + 2 if search else 2 * E - 1)
                    link(dve.tensor_tensor_scan(total[:], ones_f[:], p_tot[:, 0:TILES], 0.0, ALU.mult, ALU.add))
                    link(dve.tensor_tensor(rank[:], total[:], p_tot[:, 0:TILES], ALU.subtract))
                    link(dve.tensor_tensor(rank[:], rank[:], p_pre[:, 0:TILES], ALU.add))
                    link(dve.scalar_tensor_tensor(slot[:], rank[:], 1.0, chosen[:], ALU.add, ALU.mult))
                    link(dve.tensor_scalar(slot_i[:], slot[:], -1.0, None, ALU.add))
                    link(dve.tensor_scalar(low[:], slot_i[:], P - 1, None, ALU.bitwise_and))
                    link(dve.tensor_scalar(high[:], slot_i[:], 7, None, ALU.arith_shift_right))
                    link(dve.tensor_copy(low_f[:], low[:]))
                    link(dve.tensor_copy(high_f[:], high[:]))
                    link(dve.tensor_tensor(lane_of[:], low_f[:, :, None].broadcast_to([P, TILES, P]),
                                           lanes[:, None, :].broadcast_to([P, TILES, P]), ALU.is_equal))
                    link(dve.tensor_tensor(tile_of[:].rearrange("p n a b -> p n (a b)"), high_f[:, :, None].broadcast_to([P, TILES, 2 * SLOTS]),
                                           eighth[:].rearrange("p a b -> p (a b)")[:, None, :].broadcast_to([P, TILES, 2 * SLOTS]), ALU.is_equal))
                    dve.tensor_tensor(tile_of[:], tile_of[:], place[:], ALU.mult).then_inc(onehot, 1)
                    link(dve.tensor_scalar(slot[:], chosen[:], 2 * TAKEN, -TAKEN, ALU.mult, ALU.add))
                    link(dve.tensor_tensor(avail[:], avail[:], slot[:], ALU.min))
                    dve.wait_ge(listed, e + 1)
                    if not isinstance(e, int) or e > 0:
                        dve.wait_ge(scatters_seen, ROOM + e - 1)
                    link(dve.tensor_scalar(tok_hi[:], p_idx[:, 0:SLOTS], float(P), None, ALU.mult))
                    dve.tensor_tensor(index[par][:], tok_hi[:], p_idx[:, SLOTS:2 * SLOTS], ALU.add).then_inc(index_done, 1)
                    assert not search or done[0] == LINKS, done

                plan(dve, turn)

            @block.tensor
            def _(pe):
                pe.wait_ge(consts, 16 * 7)
                pe.wait_ge(sv, 3)

                def turn(e, par, i, search, compute):
                    o = 1 - par
                    oi = i if par == 1 else i - 1
                    c = e - 1

                    def turn_rows(half):
                        if half == 0:
                            pe.wait_ge(gathered[o], 16 * SLOTS * (oi + 1))
                            pe.wait_ge(wl[o], 64 * (oi + 1))
                        pe.wait_ge(rt_copied, ROOM + 2 * c + half)
                        for j in range(4):
                            mm = pe.transpose(p_t[:, j * P:(j + 1) * P], rows[o][:, 4 * half + j, :], k["ident"][:])
                        mm.then_inc(rt_done, 1)

                    def up(m):
                        f, half = m % FC, m // FC
                        pe.wait_ge(rt_copied, ROOM + 2 * c + half + 1)
                        if m >= 2:
                            pe.wait_ge(gelu_done, 8 * c + m - 1)
                        pe.matmul(p_h[m % 2][:], w1[o][:, f:F:FC], rows_t[:, half * 512:(half + 1) * 512],
                                  start=True, stop=True).then_inc(up_done, 1)

                    def down(t):
                        pe.wait_ge(gelu_done, 8 * c + (4 if t < 4 else 8))
                        if t % 4 == 0:
                            pe.wait_ge(y_copied, ROOM + 2 * c + t // 4)
                        for f in range(FC):
                            mm = pe.matmul(p_y[:, (t % 4) * D:(t % 4 + 1) * D], hid[:, f, t * P:(t + 1) * P], w2[o][:, f, :],
                                           start=(f == 0), stop=(f == FC - 1))
                        if t % 4 == 3:
                            mm.then_inc(down_done, 1)

                    def ranks(marks, value):
                        pe.wait_ge(marked, value)
                        pe.matmul(p_pre[:, 0:TILES], before[:], marks[:], start=True, stop=True)
                        return pe.matmul(p_tot[:, 0:TILES], ones[:], marks[:], start=True, stop=True)

                    def choose():
                        if search:
                            ranks(equal, 2 * e + 1)
                            pe.matmul(p_idx[:, 0:TILES], ones[:], above[:], start=True, stop=True).then_inc(ranked, 1)
                            ranks(chosen, 2 * e + 2).then_inc(ranked, 1)
                        else:
                            ranks(chosen, 2 * E - 1).then_inc(ranked, 1)
                        pe.wait_ge(onehot, e + 1)
                        for n in range(TILES):
                            mm = pe.matmul(p_idx[:, 0:2 * SLOTS], lane_of[:, n, :], tile_of[:, n, :, :].rearrange("p a b -> p (a b)"),
                                           start=(n == 0), stop=(n == TILES - 1))
                        mm.then_inc(listed, 1)

                    pieces = [[], [lambda: turn_rows(0)], [lambda: turn_rows(1), lambda: up(0), lambda: up(1)],
                              [lambda: up(2), lambda: up(3)], [lambda: up(4), lambda: up(5)],
                              [lambda: up(6), lambda: up(7), lambda: down(0)],
                              [lambda: down(1), lambda: down(2), lambda: down(3)],
                              [lambda: down(4), lambda: down(5), lambda: down(6), lambda: down(7)]]
                    if search is False:
                        choose()
                    for n in range(PASSES):
                        if search:
                            pe.wait_ge(reached, PASSES * e + n + 1)
                            for q in range(8):
                                mm = pe.matmul(p_cnt[:, 0:8 * CANDS], ones[:],
                                               reach[:, q * 8:(q + 1) * 8, :].rearrange("p n c -> p (n c)"),
                                               start=(q == 0), stop=(q == 7))
                            mm.then_inc(counted, 1)
                        if compute:
                            for piece in pieces[n]:
                                piece()

                    if search:
                        choose()

                plan(pe, turn)

            @block.scalar
            def _(act):
                def turn(e, par, i, search, compute):
                    if not compute:
                        return
                    o = 1 - par
                    oi = i if par == 1 else i - 1
                    c = e - 1

                    def copy_rows(half):
                        act.wait_ge(rt_done, ROOM + 2 * c + half + 1)
                        act.wait_ge(up_done, ROOM + 8 * c)
                        act.activation(rows_t[:, half * 512:(half + 1) * 512], p_t[:], ACT.Identity).then_inc(rt_copied, 1)

                    def gelu(m):
                        f, half = m % FC, m // FC
                        act.wait_ge(up_done, ROOM + 8 * c + m + 1)
                        act.wait_ge(down_done, ROOM + 2 * c)
                        act.wait_ge(wl[o], 64 * (oi + 1))
                        act.activation(hid[:, f, half * 512:(half + 1) * 512], p_h[m % 2][:], ACT.Gelu_apprx_tanh,
                                       bias=b1[o][:, f:f + 1]).then_inc(gelu_done, 1)

                    def copy_y(half):
                        act.wait_ge(down_done, ROOM + 2 * c + half + 1)
                        act.wait_ge(y_ready, ROOM + c)
                        act.activation(y[:, 4 * half:4 * half + 4, :], p_y[:, :].rearrange("p (t n) -> p t n", n=D),
                                       ACT.Identity).then_inc(y_copied, 1)

                    copy_rows(0)
                    copy_rows(1)
                    for m in range(8):
                        gelu(m)
                    copy_y(0)
                    copy_y(1)

                plan(act, turn)

            @block.gpsimd
            def _(pool):
                def turn(e, par, i, search, compute):
                    if compute:
                        o = 1 - par
                        oi = i if par == 1 else i - 1
                        c = e - 1
                        pool.wait_ge(y_copied, ROOM + 2 * c + 2)
                        pool.wait_ge(wl[o], 64 * (oi + 1))
                        pool.tensor_tensor(yb[o][:], y[:], b2[o][:, None, :].broadcast_to([P, SLOTS, D]), ALU.add).then_inc(y_ready, 1)
                        wait_apart(pool, y_ready, ROOM + c + 1, wait_passed)
                        for j in range(SLOTS):
                            pool.indirect_dma_start(ffn_rows, bass.IndirectOffsetOnAxis(ap=index[o][:, j:j + 1], axis=0),
                                                    yb[o][:, j, :], None).then_inc(scattered[o], 16)
                    if search is not None:
                        if compute:
                            pool.wait_ge(rt_done, ROOM + 2 * e - 2)
                        wait_apart(pool, index_done, e + 1, wait_passed)
                        for j in range(SLOTS):
                            pool.indirect_dma_start(rows[par][:, j, :], None, norm_rows,
                                                    bass.IndirectOffsetOnAxis(ap=index[par][:, j:j + 1], axis=0)).then_inc(gathered[par], 16)
                    if compute:
                        pool.wait_ge(scattered[o], 16 * SLOTS * (oi + 1))
                        pool.sem_inc(scatters_seen, 1)

                plan(pool, turn)


def add_rows(nc, sem, k, rows_dram, out, layer):
    tag = f"r{layer}"
    steps = 8
    per = TILES // steps
    with ExitStack() as ctx:
        buf = [ctx.enter_context(nc.sbuf_tensor(f"buf{i}_{tag}", [P, per, D], F32)) for i in range(2)]
        loaded = [sem(f"rows_loaded{i}_{tag}") for i in range(2)]
        added = sem(f"rows_added_{tag}")
        stored = sem(f"out_stored_{tag}")
        rows = rows_dram.rearrange("(n p) d -> p n d", p=P)
        out_v = out.rearrange("b (t p) d -> p (b t) d", p=P) if out is not None else None
        with nc.Block() as block:
            @block.sync
            def _(sp):
                for g in range(steps):
                    if g >= 2:
                        sp.wait_ge(added, g - 1)
                    sp.dma_start(buf[g % 2][:], rows[:, g * per:(g + 1) * per, :]).then_inc(loaded[g % 2], 16)
            if out is not None:
                @block.scalar
                def _(act):
                    for g in range(steps):
                        act.wait_ge(added, g + 1)
                        act.dma_start(out_v[:, g * per:(g + 1) * per, :], k["x"][:, g * per:(g + 1) * per, :]).then_inc(stored, 16)
                    act.wait_ge(stored, 16 * steps)

            @block.vector
            def _(dve):
                for g in range(steps):
                    dve.wait_ge(loaded[g % 2], 16 * (g // 2) + 16)
                    part = k["x"][:, g * per:(g + 1) * per, :]
                    dve.tensor_tensor(part, part, buf[g % 2][:], ALU.add).then_inc(added, 1)


def attention_b(nc, sem, d, k):
    with ExitStack() as outer:
        def keep(name, shape, dt=F32):
            return outer.enter_context(nc.sbuf_tensor(f"{name}_ab", shape, dt))

        values = keep("values", [P, TILES, D])
        phases = keep("phases", [P, TILES, 2, RFF])
        powers = keep("powers", [P, TILES, NM])
        decay = keep("decay", [P, T])
        features(nc, d, k, sem, values, phases, powers, decay)
        attend(nc, d, k, sem, values, phases, powers, decay)


def features(nc, d, k, sem, values, phases, powers, decay):
    W = FEAT + D
    steps = TILES // GROUP
    with ExitStack() as ctx:
        def sb(name, shape, dt=F32):
            return ctx.enter_context(nc.sbuf_tensor(f"{name}_fe", shape, dt))

        def ps(name):
            return ctx.enter_context(nc.psum_tensor(f"{name}_fe", [P, 512], F32))

        w_all = sb("w_all", [P, W])
        w_shell = sb("w_shell", [SHELL, D])
        omega_t = sb("omega_t", [SHELL, RFF])
        b_shell = sb("b_shell", [SHELL, P])
        b_all = sb("b_all", [P, W])
        b_rff = sb("b_rff", [P, RFF])
        temp = sb("temp", [P, 1])
        small = [sb(f"small{i}", [P, 1]) for i in range(6)]
        a = [sb(f"a{i}", [P, GROUP, D]) for i in range(2)]
        a_t = [sb(f"a_t{i}", [P, GROUP, P]) for i in range(2)]
        feat = sb("feat", [P, TILES, FEAT])
        sq = sb("sq", [P, TILES, SHELL])
        ss = sb("ss", [P, TILES])
        length = sb("length", [P, TILES])
        proj = sb("proj", [P, TILES, RFF])
        turns = sb("turns", [P, TILES, RFF])
        arg = sb("arg", [P, TILES, 2, RFF])
        charge = sb("charge", [P, TILES])
        c_mag = sb("c_mag", [P, NM])
        p_t = [ps(f"p_t{i}") for i in range(2)]
        p_f = [[ps(f"p_f{i}{j}") for j in range(2)] for i in range(2)]
        p_w = ps("p_w")

        loaded = sem("fe_loaded")
        product = sem("fe_weight_product")
        step = sem("fe_step")
        ast = sem("fe_act_step")
        a_done = sem("fe_a_done")
        turned = [sem(f"fe_turned{i}") for i in range(2)]
        copied = [sem(f"fe_copied{i}") for i in range(2)]
        made = [sem(f"fe_made{i}") for i in range(2)]
        kept = sem("fe_kept")
        ss_done = sem("fe_ss_done")
        arg_done = sem("fe_arg_done")
        with nc.Block() as block:
            @block.sync
            def _(sp):
                for counter in (*copied, kept, *turned, *made):
                    sp.sem_inc(counter, ROOM)
                for dst, src in ((w_all[:, 0:SHELL], d["w_shell_t"]), (w_all[:, SHELL:SHELL + 1], d["w_charge_t"]),
                                 (w_all[:, FEAT:W], d["w_vb_t"]), (w_shell[:], d["L0_attn_b_W_shell"]),
                                 (omega_t[:], d["omega_t"]),
                                 (b_shell[:], d["b_shell_wide"]),
                                 (b_all[:, 0:SHELL], d["L0_attn_b_b_shell"].rearrange("(a b) -> a b", a=1).broadcast_to([P, SHELL])),
                                 (b_all[:, SHELL:SHELL + 1], d["L0_attn_b_b_charge"].rearrange("(a b) -> a b", a=1).broadcast_to([P, 1])),
                                 (b_all[:, FEAT:W], d["L0_attn_b_b_v"].rearrange("(a b) -> a b", a=1).broadcast_to([P, D])),
                                 (b_rff[:], d["L0_attn_b_rff_bias"].rearrange("(a b) -> a b", a=1).broadcast_to([P, RFF])),
                                 (temp[:], d["L0_attn_b_log_temp"].broadcast_to([P, 1])),
                                 (decay[:], d["c_decay"]), (c_mag[:], d["c_mag"])):
                    sp.dma_start(dst, src).then_inc(loaded, 16)

            @block.tensor
            def _(pe):
                pe.wait_ge(loaded, 16 * 13)
                pe.matmul(p_w[:, 0:RFF], w_shell[:], omega_t[:], start=True, stop=True).then_inc(product, 1)
                pe.matmul(p_w[:, RFF:2 * RFF], b_shell[:], omega_t[:], start=True, stop=True).then_inc(product, 1)
                pe.wait_ge(step, 2)
                with pe.Fori(0, steps // 2) as i:
                    for par in range(2):
                        g = 2 * i + par
                        pe.wait_ge(a_done, GROUP * g + GROUP)
                        pe.wait_ge(copied[par], ROOM + i)
                        for j in range(GROUP):
                            mm = pe.transpose(p_t[par][:, j * P:(j + 1) * P], a[par][:, j, :], k["ident"][:])
                        mm.then_inc(turned[par], 1)
                        pe.wait_ge(copied[par], ROOM + i + 1)
                        pe.wait_ge(kept, ROOM + 8 * i)
                        for j in range(GROUP):
                            mm = pe.matmul(p_f[par][j // 2][:, (j % 2) * 256:(j % 2) * 256 + W], a_t[par][:, j, :], w_all[:],
                                           start=True, stop=True)
                        mm.then_inc(made[par], 1)

            @block.scalar
            def _(act):
                link = Chain(act, ast)
                act.wait_ge(loaded, 16 * 13)
                link(act.activation(small[0][:], temp[:], ACT.Abs))
                link(act.activation(small[1][:], small[0][:], ACT.Exp, scale=-1.0))
                link(act.activation(small[2][:], small[1][:], ACT.Ln, bias=1.0))
                link(act.activation(small[3][:], temp[:], ACT.Relu))
                with act.Fori(0, steps // 2) as i:
                    for par in range(2):
                        g = 2 * i + par
                        act.wait_ge(turned[par], ROOM + i)
                        for j in range(GROUP):
                            n = GROUP * g + j
                            act.activation(a[par][:, j, :], k["x"][:, n, :], ACT.Identity, bias=k["shift"][:, bass.ds(n, 1)],
                                           scale=k["rstd"][:, bass.ds(n, 1)]).then_inc(a_done, 1)
                        act.wait_ge(turned[par], ROOM + i + 1)
                        act.wait_ge(made[par], ROOM + i)
                        act.activation(a_t[par][:], p_t[par][:, :].rearrange("p (j q) -> p j q", j=GROUP),
                                       ACT.Identity).then_inc(copied[par], 1)
                act.wait_ge(ss_done, 1)
                link(act.activation(length[:], ss[:], ACT.Sqrt))
                act.wait_ge(kept, ROOM + 4 * steps)
                link(act.activation(charge[:], feat[:, :, SHELL], ACT.Tanh))
                act.wait_ge(arg_done, 1)
                link(act.activation(phases[:], arg[:], ACT.Sin))

            @block.vector
            def _(dve):
                link = Chain(dve, step)
                dve.wait_ge(product, 2)
                link(dve.tensor_copy(w_all[:, SHELL + 1:FEAT], p_w[:, 0:RFF]))
                link(dve.tensor_copy(b_all[:, SHELL + 1:FEAT], p_w[:, RFF:2 * RFF]))
                dve.wait_ge(ast, 4)
                link(dve.tensor_tensor(small[4][:], small[2][:], small[3][:], ALU.add))
                link(dve.tensor_scalar(small[4][:], small[4][:], 0.1, None, ALU.add))
                link(dve.reciprocal(small[5][:], small[4][:]))
                link(dve.tensor_scalar(decay[:], decay[:], small[5][:, 0:1], None, ALU.mult))
                with dve.Fori(0, steps // 2) as i:
                    for par in range(2):
                        g = 2 * i + par
                        dve.wait_ge(made[par], ROOM + i + 1)
                        for half in range(2):
                            part = bass.ds(GROUP * g + 2 * half, 2)
                            src = p_f[par][half][:, :].rearrange("p (t w) -> p t w", t=2)
                            dve.tensor_tensor(feat[:, part, :], src[:, :, 0:FEAT],
                                              b_all[:, None, 0:FEAT].broadcast_to([P, 2, FEAT]), ALU.add).then_inc(kept, 1)
                            dve.tensor_tensor(values[:, part, :], src[:, :, FEAT:W],
                                              b_all[:, None, FEAT:W].broadcast_to([P, 2, D]), ALU.add).then_inc(kept, 1)
                dve.wait_ge(kept, ROOM + 4 * steps)
                shell = feat[:, :, 0:SHELL]
                link(dve.tensor_tensor(sq[:], shell, shell, ALU.mult))
                dve.tensor_reduce(ss[:], sq[:], AX.X, ALU.add).then_inc(ss_done, 1)
                dve.wait_ge(ast, 5)
                link(dve.tensor_scalar(length[:], length[:], 1e-12, None, ALU.max))
                link(dve.reciprocal(ss[:], length[:]))
                link(dve.tensor_tensor(proj[:], feat[:, :, SHELL + 1:FEAT], ss[:, :, None].broadcast_to([P, TILES, RFF]), ALU.mult))
                link(dve.tensor_tensor(proj[:], proj[:], b_rff[:, None, :].broadcast_to([P, TILES, RFF]), ALU.add))
                for half, quarter in ((0, 0.25), (1, 0.0)):
                    to = arg[:, :, half, :]
                    link(dve.tensor_scalar(turns[:], proj[:], 1.0 / (2 * math.pi), quarter, ALU.mult, ALU.add))
                    link(dve.tensor_scalar(turns[:], turns[:], ROUND, ROUND, ALU.add, ALU.subtract))
                    link(dve.scalar_tensor_tensor(to, turns[:], -TWO_PI[0], proj[:], ALU.mult, ALU.add))
                    link(dve.scalar_tensor_tensor(to, turns[:], -TWO_PI[1], to, ALU.mult, ALU.add))
                    link(dve.scalar_tensor_tensor(to, turns[:], -TWO_PI[2], to, ALU.mult, ALU.add))
                    if half == 0:
                        link(dve.tensor_scalar(to, to, math.pi / 2, None, ALU.add))
                    ins = dve.tensor_scalar(to, to, -PI, PI, ALU.max, ALU.min)
                    if half == 0:
                        link(ins)
                    else:
                        ins.then_inc(arg_done, 1)
                dve.wait_ge(ast, 6)
                link(dve.memset(powers[:, :, 0], 1.0))
                for m in range(1, NM):
                    link(dve.tensor_tensor(powers[:, :, m], powers[:, :, m - 1], charge[:], ALU.mult))
                link(dve.tensor_tensor(powers[:], powers[:], c_mag[:, None, :].broadcast_to([P, TILES, NM]), ALU.mult))


def attend(nc, d, k, sem, values, phases, powers, decay):
    KC = 3
    with ExitStack() as ctx:
        def sb(name, shape, dt=F32):
            return ctx.enter_context(nc.sbuf_tensor(f"{name}_at", shape, dt))

        def ps(name):
            return ctx.enter_context(nc.psum_tensor(f"{name}_at", [P, 512], F32))

        w_comb = sb("w_comb", [P, KC, P])
        w_out = sb("w_out", [P, D])
        b_out = sb("b_out", [P, D])
        bar = sb("bar", [P, P], BF16)
        ident_b = sb("ident_b", [P, P], BF16)
        tp = [sb(f"tp{i}", [P, PER, KC * P]) for i in range(2)]
        tp_t = [sb(f"tp_t{i}", [P, KC, T]) for i in range(2)]
        phi_t = [sb(f"phi_t{i}", [P, T]) for i in range(2)]
        v = [sb(f"v{i}", [P, PER, D]) for i in range(2)]
        logit = [sb(f"logit{i}", [P, 384]) for i in range(2)]
        prob = [sb(f"prob{i}", [P, 384]) for i in range(2)]
        prob_t = [sb(f"prob_t{i}", [P, 384]) for i in range(2)]
        o_t = [sb(f"o_t{i}", [P, T]) for i in range(2)]
        top = [sb(f"top{i}", [P, PER]) for i in range(2)]
        ntop = [sb(f"ntop{i}", [P, PER]) for i in range(2)]
        mass = [sb(f"mass{i}", [P, PER]) for i in range(2)]
        rmass = [sb(f"rmass{i}", [P, PER]) for i in range(2)]
        p_tp = [ps(f"p_tp{i}") for i in range(2)]
        p_phi = ps("p_phi")
        p_s = [ps(f"p_s{i}") for i in range(2)]
        p_pt = ps("p_pt")
        p_o = ps("p_o")
        p_y = ps("p_y")

        loaded = sem("at_loaded")
        padded = sem("at_padded")
        tp_done = sem("at_tp_done")
        v_done = sem("at_v_done")
        tpt_done = sem("at_tp_turned")
        tpt_copied = sem("at_tp_copied")
        phi_done = sem("at_phi_done")
        phi_copied = sem("at_phi_copied")
        s_done = sem("at_scores_done")
        l_done = sem("at_logits_done")
        n_done = sem("at_ntop_done")
        e_done = sem("at_exp_done")
        pt_done = sem("at_prob_turned")
        pt_copied = sem("at_prob_copied")
        o_done = sem("at_o_done")
        o_copied = sem("at_o_copied")
        y_done = sem("at_y_done")
        r_done = sem("at_mass_inverted")
        xb_done = sem("at_bias_added")
        x_done = sem("at_x_added")
        passed = sem("at_passed")

        def plan(eng, turn):
            with eng.Fori(0, B // 2) as i:
                for par in range(2):
                    turn(2 * i + par, par)

        with nc.Block() as block:
            @block.sync
            def _(sp):
                for counter in (tpt_copied, phi_copied, l_done, pt_copied, o_copied, x_done):
                    sp.sem_inc(counter, ROOM)
                for dst, src in ((w_comb[:], d["w_comb_pad"]), (w_out[:], d["w_out_t"]),
                                 (b_out[:], d["L0_attn_b_b_out"].rearrange("(a b) -> a b", a=1).broadcast_to([P, D])),
                                 (bar[:], d["c_bar"]), (ident_b[:], d["c_ident_b"])):
                    sp.dma_start(dst, src).then_inc(loaded, 16)

            @block.gpsimd
            def _(pool):
                pool.wait_ge(loaded, 80)
                for par in range(2):
                    pool.memset(tp[par][:, :, NM * 2 * RFF:KC * P], 0.0).then_inc(padded, 1)
                pool.wait_ge(padded, 2)

                def turn(g, par):
                    at = bass.ds(PER * g, PER)
                    pool.wait_ge(tpt_done, PER * (g + 1))
                    for t in range(PER):
                        tile = bass.ds(PER * g + t, 1)
                        pool.tensor_tensor(tp[par][:, t, 0:NM * 2 * RFF].rearrange("p (m f) -> p m f", m=NM),
                                           phases[:, tile, :, :].rearrange("p a b c -> p a (b c)").broadcast_to([P, NM, 2 * RFF]),
                                           powers[:, tile, :].rearrange("p a m -> p m a").broadcast_to([P, NM, 2 * RFF]),
                                           ALU.mult).then_inc(tp_done, 1)
                    pool.wait_ge(o_done, g + 1)
                    pool.tensor_copy(v[par][:], values[:, at, :]).then_inc(v_done, 1)
                    pool.tensor_tensor(k["x"][:, at, :], k["x"][:, at, :], b_out[:, None, :].broadcast_to([P, PER, D]),
                                       ALU.add).then_inc(xb_done, 1)

                plan(pool, turn)

            @block.tensor
            def _(pe):
                pe.wait_ge(loaded, 80)
                pe.sem_inc(tpt_done, 2 * PER)
                pe.sem_inc(o_done, 2)

                def turn(g, par):
                    for t in range(PER):
                        pe.wait_ge(tp_done, PER * g + t + 1)
                        pe.wait_ge(tpt_copied, ROOM + PER * g)
                        for c in range(KC):
                            mm = pe.transpose(p_tp[t][:, c * P:(c + 1) * P], tp[par][:, t, c * P:(c + 1) * P], k["ident"][:])
                        mm.then_inc(tpt_done, 1)
                    pe.wait_ge(tpt_copied, ROOM + PER * g + PER)
                    pe.wait_ge(phi_copied, ROOM + g)
                    for c in range(KC):
                        mm = pe.matmul(p_phi[:, 0:T], w_comb[:, c, :], tp_t[par][:, c, :], start=(c == 0), stop=(c == KC - 1))
                    mm.then_inc(phi_done, 1)
                    pe.wait_ge(phi_copied, ROOM + g + 1)
                    pe.wait_ge(l_done, ROOM + 2 * g)
                    pe.matmul(p_s[par][:, 0:P], phi_t[par][:, 0:P], phi_t[par][:, 0:P], start=True, stop=False)
                    pe.matmul(p_s[par][:, 0:P], ident_b[:], bar[:], start=False, stop=True)
                    pe.matmul(p_s[par][:, P:2 * P], phi_t[par][:, P:T], phi_t[par][:, 0:P], start=True, stop=True)
                    pe.matmul(p_s[par][:, 2 * P:3 * P], phi_t[par][:, P:T], phi_t[par][:, P:T], start=True, stop=False)
                    pe.matmul(p_s[par][:, 2 * P:3 * P], ident_b[:], bar[:], start=False, stop=True).then_inc(s_done, 1)
                    pe.wait_ge(e_done, 2 * g + 2)
                    pe.wait_ge(pt_copied, ROOM + g)
                    for c in range(3):
                        mm = pe.transpose(p_pt[:, c * P:(c + 1) * P], prob[par][:, c * P:(c + 1) * P], k["ident"][:])
                    mm.then_inc(pt_done, 1)
                    pe.wait_ge(pt_copied, ROOM + g + 1)
                    pe.wait_ge(v_done, g + 1)
                    pe.wait_ge(o_copied, ROOM + g)
                    pe.matmul(p_o[:, 0:T], v[par][:, 0, :], prob_t[par][:, 0:T], start=True, stop=False)
                    pe.matmul(p_o[:, P:T], v[par][:, 1, :], prob_t[par][:, T:384], start=False, stop=True).then_inc(o_done, 1)
                    pe.wait_ge(o_copied, ROOM + g + 1)
                    pe.wait_ge(x_done, ROOM + 2 * g)
                    for t in range(PER):
                        mm = pe.matmul(p_y[:, t * D:(t + 1) * D], o_t[par][:, t * P:(t + 1) * P], w_out[:], start=True, stop=True)
                    mm.then_inc(y_done, 1)

                plan(pe, turn)

            @block.scalar
            def _(act):
                def turn(g, par):
                    for t in range(PER):
                        act.wait_ge(tpt_done, PER * (g + 2) + t + 1)
                        act.activation(tp_t[par][:, :, t * P:(t + 1) * P], p_tp[t][:, 0:KC * P].rearrange("p (c q) -> p c q", c=KC),
                                       ACT.Identity).then_inc(tpt_copied, 1)
                    act.wait_ge(phi_done, g + 1)
                    act.activation(phi_t[par][:], p_phi[:, 0:T], ACT.Identity).then_inc(phi_copied, 1)
                    act.wait_ge(n_done, g + 1)
                    for t in range(PER):
                        cols = slice(0, P) if t == 0 else slice(P, 384)
                        act.activation(prob[par][:, cols], logit[par][:, cols], ACT.Exp, bias=ntop[par][:, t:t + 1],
                                       accum_out=mass[par][:, t:t + 1]).then_inc(e_done, 1)
                    act.wait_ge(o_done, g + 3)
                    act.activation(o_t[par][:], p_o[:, 0:T], ACT.Identity).then_inc(o_copied, 1)

                plan(act, turn)

            @block.vector
            def _(dve):
                def turn(g, par):
                    wait_apart(dve, s_done, g + 1, passed)
                    dve.tensor_tensor_reduce(logit[par][:, 0:P], p_s[par][:, 0:P], decay[:, P:T], 1.0, -3.0e38,
                                             ALU.mult, ALU.max, top[par][:, 0:1]).then_inc(l_done, 1)
                    dve.tensor_tensor_reduce(logit[par][:, P:384], p_s[par][:, P:384], decay[:], 1.0, -3.0e38,
                                             ALU.mult, ALU.max, top[par][:, 1:2]).then_inc(l_done, 1)
                    dve.wait_ge(l_done, ROOM + 2 * g + 2)
                    dve.tensor_scalar(ntop[par][:], top[par][:], -1.0, None, ALU.mult).then_inc(n_done, 1)
                    dve.wait_ge(e_done, 2 * g + 2)
                    dve.reciprocal(rmass[par][:], mass[par][:]).then_inc(r_done, 1)
                    dve.wait_ge(pt_done, g + 1)
                    dve.tensor_copy(prob_t[par][:], p_pt[:, 0:384]).then_inc(pt_copied, 1)
                    dve.wait_ge(y_done, g + 1)
                    dve.wait_ge(r_done, g + 1)
                    dve.wait_ge(xb_done, g + 1)
                    for t in range(PER):
                        tile = bass.ds(PER * g + t, 1)
                        xs = k["x"][:, tile, :].rearrange("p a e -> p (a e)")
                        dve.scalar_tensor_tensor(xs, p_y[:, t * D:(t + 1) * D], rmass[par][:, t:t + 1], xs,
                                                 ALU.mult, ALU.add).then_inc(x_done, 1)

                plan(dve, turn)


def _layouts(i):
    import numpy as np

    def rope_pair(w):
        t = np.asarray(w).T
        half = np.arange(D).reshape(H, 2, DH // 2)[:, ::-1, :].reshape(D)
        return np.stack([t, t[:, half]], 0)

    out = {}
    ws = [rope_pair(i[n]) for n in ("L0_attn_a_Wk", "L0_attn_a_Wk2", "L0_attn_a_Wq", "L0_attn_a_Wq2")]
    out["w_rope"] = np.stack(ws, 0).transpose(2, 0, 1, 3)
    out["w_v_t"] = np.asarray(i["L0_attn_a_Wv"]).T
    proj_t = np.asarray(i["L0_attn_a_Wproj"]).T.reshape(4, 4, DH, D)
    pad = np.zeros((4, 32, 4, D), np.float32)
    pad[:, :DH] = proj_t.transpose(1, 2, 0, 3)
    out["w_proj_pad"] = pad.reshape(P, 4, D)
    out["centroids_t"] = np.asarray(i["L0_ffn_centroids"]).T
    out["w_shell_t"] = np.asarray(i["L0_attn_b_W_shell"]).T
    out["w_charge_t"] = np.asarray(i["L0_attn_b_W_charge"]).T
    out["w_vb_t"] = np.asarray(i["L0_attn_b_W_v"]).T
    out["w_out_t"] = np.asarray(i["L0_attn_b_W_out"]).T
    out["omega_t"] = np.asarray(i["L0_attn_b_omega"]).T
    out["b_shell_wide"] = np.repeat(np.asarray(i["L0_attn_b_b_shell"])[:, None], P, 1)
    comb = np.zeros((3 * P, P), np.float32)
    comb[:NM * 2 * RFF, :64] = np.asarray(i["L0_attn_b_W_combine"]).T
    out["w_comb_pad"] = comb.reshape(3, P, P).transpose(1, 0, 2)
    return {n: np.ascontiguousarray(a) for n, a in out.items()}


def _constants():
    import numpy as np
    bfloat16 = mybir.dt.np(BF16)
    c = {"c_ident": np.eye(P, dtype=np.float32)}
    inv = 1.0 / 10000.0 ** (np.arange(0, DH, 2, dtype=np.float32) / np.float32(DH))
    freqs = np.outer(np.arange(T, dtype=np.float32), inv.astype(np.float32)).astype(np.float32)
    cos, sin = np.cos(freqs).astype(np.float32).T, np.sin(freqs).astype(np.float32).T
    c["c_rope"] = np.stack([np.tile(np.concatenate([cos, cos]), (H, 1)),
                            np.tile(np.concatenate([sin, -sin]), (H, 1))], 1)
    keys = (np.arange(1, CANDS + 1, dtype=np.uint64) << 28).astype(np.uint32)
    bits = np.where(keys >> 31, keys ^ np.uint32(1 << 31), ~keys)
    c["c_first_cand"] = np.tile(bits.view(np.float32), (P, 1))
    shifts = 28 - 4 * np.arange(PASSES)
    dig = np.stack([(np.arange(1, CANDS + 1, dtype=np.uint64) << int(s)).astype(np.uint32) for s in shifts])
    c["c_digits"] = np.tile(dig, (P, 1, 1))
    c["c_weight"] = np.tile((2.0 ** shifts).astype(np.float32), (P, 1))
    p = np.arange(P)
    c["c_before"] = (p[:, None] < p[None, :]).astype(bfloat16)
    c["c_lanes"] = np.tile(p.astype(bfloat16), (P, 1))
    place = np.zeros((P, TILES, 2, SLOTS), np.float32)
    place[:, :, 0, :] = np.arange(TILES)[None, :, None]
    place[:, :, 1, :] = p[:, None, None]
    c["c_place"] = place.astype(bfloat16)
    c["c_eighth"] = np.tile(np.arange(SLOTS).astype(bfloat16), (P, 2, 1))
    q, m = np.arange(P)[:, None], np.arange(T)[None, :]
    c["c_decay"] = np.exp(np.float32(-0.3) * np.abs(q + P - m).astype(np.float32) / np.float32(10.0)).astype(np.float32)
    c["c_bar"] = np.where(p[:, None] < p[None, :], -1e30, 0.0).astype(bfloat16)
    c["c_ident_b"] = np.eye(P).astype(bfloat16)
    scale = math.sqrt(2.0 / (2 * RFF)) * math.sqrt(math.exp(-0.5))
    mags = [math.sqrt(1.0 / math.factorial(m) + 1e-10) * scale for m in range(NM)]
    c["c_mag"] = np.tile(np.array(mags, np.float32), (P, 1))
    return c


_DIRECT = ["L0_attn_a_x", "L0_attn_b_b_charge", "L0_attn_b_W_shell", "L0_attn_b_b_shell", "L0_attn_b_rff_bias",
           "L0_attn_b_b_v", "L0_attn_b_b_out", "L0_ffn_ln_g", "L0_ffn_ln_b", "L0_ffn_w1", "L0_ffn_b1", "L0_ffn_w2",
           "L0_ffn_b2"]


def kernel(**inputs):
    import numpy as _np
    import concourse.bacc as _bacc
    from concourse import mybir as _mybir
    from concourse.bass_utils import run_bass_kernel_spmd as _run

    nc = _bacc.Bacc("TRN2", target_bir_lowering=False, num_devices=1)
    arrays = {n: _np.ascontiguousarray(inputs[n]) for n in _DIRECT}
    arrays["L0_attn_b_log_temp"] = _np.asarray(inputs["L0_attn_b_log_temp"]).reshape(1, 1)
    arrays.update(_layouts(inputs))
    arrays.update({n: _np.ascontiguousarray(a) for n, a in _constants().items()})
    handles = {n: nc.dram_tensor(n, a.shape, _mybir.dt.from_np(a.dtype), kind="ExternalInput").ap() for n, a in arrays.items()}
    handles["out"] = nc.dram_tensor("out", (B, T, D), F32, kind="ExternalOutput").ap()
    build(nc, handles)
    r = _run(nc, [arrays], core_ids=[0])
    return r.results[0]["out"]
```

```python
import math
from contextlib import ExitStack

import concourse.bass as bass
from concourse import mybir

F32 = mybir.dt.float32
BF16 = mybir.dt.bfloat16
I32 = mybir.dt.int32
U32 = mybir.dt.uint32
ALU = mybir.AluOpType
ACT = mybir.ActivationFunctionType
AX = mybir.AxisListType

P = 128
D = 128
B, T = 32, 256
TOKENS = B * T
TILES = TOKENS // P
PER = T // P
H = 16
DH = D // H
E = 8
CAP = TOKENS // E
F = 512
FC = F // P
SLOTS = CAP // P
SHELL, RFF, ORDER = 64, 32, 4
NM = ORDER + 1
FEAT = SHELL + 1 + RFF
EPS = 1e-5
GROUP = 4
PASSES = 8
CANDS = 15
TAKEN = -1.5e38
ROUND = 1.5 * 2.0**23
TWO_PI = (6.28125, 0.0019350051879882812, 3.0199159819567e-07)
PI = 3.1415925
ROOM = 1


def wait_apart(eng, semaphore, value, passed):
    eng.wait_ge(semaphore, value)
    eng.sem_inc(passed, 1)


class Chain:

    def __init__(self, eng, sem):
        self.eng, self.sem, self.n = eng, sem, 0

    def __call__(self, ins):
        self.n += 1
        ins.then_inc(self.sem, 1)
        self.eng.wait_ge(self.sem, self.n)


def phase(nc, body, *args):
    used = []

    def sem(name):
        used.append(nc.alloc_semaphore(name))
        return used[-1]

    body(nc, sem, *args)
    nc.clear_and_free_semaphores(used)
    nc.all_engine_barrier()


def build(nc, d):
    with ExitStack() as whole:
        def keep(name, shape, dt=F32):
            return whole.enter_context(nc.sbuf_tensor(name, shape, dt))

        k = {
            "x": keep("x", [P, TILES, D]),
            "ident": keep("ident", [P, P]),
            "rstd": keep("rstd", [P, TILES]),
            "shift": keep("shift", [P, TILES]),
            "halves": keep("halves", [P, TILES, 6]),
            "scores": keep("scores", [P, E, TILES]),
        }
        norm_rows = nc.dram_tensor("norm_rows", (TOKENS, D), F32, kind="Internal").ap()
        ffn_rows = nc.dram_tensor("ffn_rows", (TOKENS, D), F32, kind="Internal").ap()
        phase(nc, load_x, d, k)
        phase(nc, statistics, k, "a")
        phase(nc, attention_a, d, k)
        phase(nc, normalise_for_experts, d, k, norm_rows, 0)
        phase(nc, experts, d, k, norm_rows, ffn_rows, 0)
        phase(nc, add_rows, k, ffn_rows, None, 0)
        phase(nc, statistics, k, "b")
        phase(nc, attention_b, d, k)
        phase(nc, normalise_for_experts, d, k, norm_rows, 1)
        phase(nc, experts, d, k, norm_rows, ffn_rows, 1)
        phase(nc, add_rows, k, ffn_rows, d["out"], 1)


def load_x(nc, sem, d, k):
    loads = 4
    loaded = [sem(f"x_loaded{q}") for q in range(loads)]
    ident_loaded = sem("ident_loaded")
    measured = sem("x_measured")
    x_dram = d["L0_attn_a_x"].rearrange("b (t p) d -> p (b t) d", p=P)
    with nc.Block() as block:
        @block.sync
        def _(sp):
            for q in range(loads):
                part = slice(q * TILES // loads, (q + 1) * TILES // loads)
                sp.dma_start(k["x"][:, part, :], x_dram[:, part, :]).then_inc(loaded[q], 16)
            sp.dma_start(k["ident"][:], d["c_ident"]).then_inc(ident_loaded, 16)
            sp.wait_ge(ident_loaded, 16)

        @block.vector
        def _(dve):
            for q in range(loads):
                dve.wait_ge(loaded[q], 16)
                for n in range(q * TILES // loads, (q + 1) * TILES // loads):
                    dve.bn_stats(k["halves"][:, n, :], k["x"][:, n, :]).then_inc(measured, 1)


def statistics(nc, sem, k, tag, twice=False):
    with ExitStack() as ctx:
        def sb(name, shape, dt=F32):
            return ctx.enter_context(nc.sbuf_tensor(f"{name}_{tag}", shape, dt))

        halves = k["halves"]
        moment = sb("moment", [P, TILES])
        gap = sb("gap", [P, TILES])
        gap2 = sb("gap2", [P, TILES])
        var = sb("var", [P, TILES])
        std = sb("std", [P, TILES])
        msum = sb("msum", [P, TILES])
        eps = sb("eps", [P, 1])
        step = sem(f"stat_step_{tag}")
        var_done = sem(f"var_done_{tag}")
        std_done = sem(f"std_done_{tag}")
        with nc.Block() as block:
            @block.vector
            def _(dve):
                link = Chain(dve, step)
                link(dve.memset(eps[:], EPS))
                link(dve.tensor_tensor(moment[:], halves[:, :, 2], halves[:, :, 5], ALU.add))
                link(dve.tensor_tensor(gap[:], halves[:, :, 1], halves[:, :, 4], ALU.subtract))
                link(dve.tensor_tensor(msum[:], halves[:, :, 1], halves[:, :, 4], ALU.add))
                link(dve.tensor_tensor(gap2[:], gap[:], gap[:], ALU.mult))
                dve.scalar_tensor_tensor(var[:], gap2[:], D / 4.0, moment[:], ALU.mult, ALU.add).then_inc(var_done, 1)
                dve.wait_ge(std_done, 1)
                link(dve.reciprocal(k["rstd"][:], std[:]))
                link(dve.scalar_tensor_tensor(k["shift"][:], msum[:], -0.5, k["rstd"][:], ALU.mult, ALU.mult))
                if twice:
                    link(dve.tensor_tensor(gap[:], var[:], k["rstd"][:], ALU.mult))
                    link(dve.tensor_tensor(var[:], gap[:], k["rstd"][:], ALU.mult))
                    dve.tensor_scalar(k["rstd_1"][:], k["rstd"][:], 1.0, None, ALU.add).then_inc(var_done, 1)
                    dve.wait_ge(std_done, 2)
                    link(dve.reciprocal(gap2[:], std[:]))
                    link(dve.tensor_tensor(k["rstd_2"][:], k["rstd"][:], gap2[:], ALU.mult))
                    link(dve.tensor_tensor(k["shift_2"][:], k["shift"][:], gap2[:], ALU.mult))

            @block.scalar
            def _(act):
                act.wait_ge(step, 1)
                for n in range(2 if twice else 1):
                    act.wait_ge(var_done, n + 1)
                    if n:
                        act.wait_ge(step, 9)
                    act.activation(std[:], var[:], ACT.Sqrt, bias=eps[:], scale=1.0 / D).then_inc(std_done, 1)


def attention_a(nc, sem, d, k):
    QUADS = H // 4
    PAIRS = H // 2
    FH = DH * DH
    with ExitStack() as ctx:
        def sb(name, shape, dt=F32):
            return ctx.enter_context(nc.sbuf_tensor(f"{name}_aa", shape, dt))

        def ps(name):
            return ctx.enter_context(nc.psum_tensor(f"{name}_aa", [P, 512], F32))

        w_qk = sb("w_qk", [P, 4, D])
        w_v = sb("w_v", [P, D])
        w_proj = sb("w_proj", [P, 4, D])
        rope = sb("rope", [P, PER, 2, DH])
        causal = sb("causal", [P, P])
        xn = sb("xn", [P, PER, D])
        xn_t = sb("xn_t", [P, T])
        straight = sb("straight", [P, PER, 4 * H, 2, DH // 2])
        crossed = sb("crossed", [P, PER, 4 * H, 2, DH // 2])
        roped = sb("roped", [P, PER, 4, H, DH])
        feat_q = sb("feat_q", [P, PER, H, DH, DH])
        feat_k = sb("feat_k", [P, PER, H, DH, DH])
        q_t = [sb(f"q_t{i}", [P, H, T]) for i in range(2)]
        k_t = [sb(f"k_t{i}", [P, PAIRS, T]) for i in range(2)]
        v = [sb(f"v{i}", [P, PER, H, 32]) for i in range(2)]
        kv = sb("kv", [P, H, 32])
        patt = [sb(f"patt{i}", [P, 4, P]) for i in range(4)]
        z_t = sb("z_t", [P, 4, T])
        p_turn = [ps(f"p_turn{i}") for i in range(2)]
        p_patt = [ps(f"p_patt{i}") for i in range(2)]
        p_misc = ps("p_misc")
        p_kv = ps("p_kv")
        p_z = ps("p_z")
        p_y = ps("p_y")

        weights = sem("aa_weights_loaded")
        cleared = sem("aa_cleared")
        xn_done = sem("aa_xn_done")
        xt_done = sem("aa_xt_done")
        xt_copied = sem("aa_xt_copied")
        v_done = sem("aa_v_done")
        v_copied = sem("aa_v_copied")
        proj_done = sem("aa_projections_done")
        terms_done = sem("aa_rotation_terms_done")
        roped_done = sem("aa_roped_done")
        feat_q_done = sem("aa_query_features_done")
        feat_k_done = sem("aa_key_features_done")
        feat_turned = sem("aa_features_turned")
        feat_copied = sem("aa_features_copied")
        kv_done = sem("aa_kv_done")
        kv_copied = sem("aa_kv_copied")
        p_done = sem("aa_pattern_done")
        masked = sem("aa_masked")
        z_done = sem("aa_z_done")
        z_copied = sem("aa_z_copied")
        y_done = sem("aa_y_done")
        x_added = sem("aa_x_added")
        measured = sem("aa_x_measured")

        TURNS = [("k", 0, 0), ("k", 0, 1), ("q", 0, 0), ("q", 0, 1), ("k", 1, 0), ("k", 1, 1), ("q", 1, 0), ("q", 1, 1)]
        NT = len(TURNS)
        U = QUADS * PER

        def plan(eng, turn):
            with eng.Fori(0, (B - 2) // 2) as i:
                for par in range(2):
                    turn(2 * i + par, par, True, True)
            turn(B - 2, 0, True, False)
            turn(B - 1, 1, False, False)

        def at(n, count=1):
            return slice(n, n + count) if isinstance(n, int) else bass.ds(n, count)

        with nc.Block() as block:
            @block.sync
            def _(sp):
                for counter in (xt_done, xt_copied, kv_done, y_done, z_copied, feat_copied, v_done):
                    sp.sem_inc(counter, ROOM)
                sp.sem_inc(z_done, 4)
                sp.sem_inc(masked, 2)
                sp.dma_start(w_qk[:], d["w_qk"]).then_inc(weights, 16)
                sp.dma_start(w_v[:], d["w_v_t"]).then_inc(weights, 16)
                sp.dma_start(w_proj[:], d["w_proj_pad"]).then_inc(weights, 16)
                sp.dma_start(rope[:], d["c_rope"]).then_inc(weights, 16)
                sp.dma_start(causal[:], d["c_causal"]).then_inc(weights, 16)

            @block.gpsimd
            def _(pool):
                for t in (q_t[0], q_t[1], v[0], v[1]):
                    pool.memset(t[:], 0.0).then_inc(cleared, 1)

                def prepare(g):
                    for t in range(PER):
                        pool.wait_ge(terms_done, 2 * PER * g + 2 * t + 2)
                        if not isinstance(g, int) or g > 0:
                            pool.wait_ge(feat_q_done, PER * g)
                            pool.wait_ge(feat_k_done, PER * g)
                        r = roped[:, t, :, :, :].rearrange("p s h (a e) -> p (s h) a e", a=2)
                        for half in range(2):
                            pool.tensor_tensor(r[:, :, half, :], straight[:, t, :, half, :], crossed[:, t, :, 1 - half, :],
                                               ALU.add).then_inc(roped_done, 1)
                        pool.wait_ge(roped_done, 2 * PER * g + 2 * t + 2)
                        if not isinstance(g, int) or g > 0:
                            pool.wait_ge(feat_turned, NT * g)
                            pool.wait_ge(kv_done, ROOM + g)
                        pool.tensor_tensor(feat_k[:, t, :, :, :], roped[:, t, 2, :, :, None].broadcast_to([P, H, DH, DH]),
                                           roped[:, t, 3, :, None, :].broadcast_to([P, H, DH, DH]), ALU.mult).then_inc(feat_k_done, 1)

                prepare(0)

                def turn(g, par, more, more2):
                    if more:
                        prepare(g + 1)

                plan(pool, turn)

            @block.scalar
            def _(act):
                act.wait_ge(cleared, 4)

                def normalise(g):
                    act.wait_ge(xt_done, ROOM + g)
                    for t in range(PER):
                        n = PER * g + t
                        act.activation(xn[:, t, :], k["x"][:, at(n), :].rearrange("p a e -> p (a e)"), ACT.Identity,
                                       bias=k["shift"][:, at(n)], scale=k["rstd"][:, at(n)]).then_inc(xn_done, 1)

                def copy_xt(g):
                    act.wait_ge(xt_done, ROOM + g + 1)
                    act.wait_ge(v_done, ROOM + g)
                    act.activation(xn_t[:], p_misc[:, 0:T], ACT.Identity).then_inc(xt_copied, 1)

                def copy_v(g, par):
                    act.wait_ge(v_done, ROOM + g + 1)
                    act.activation(v[par][:, :, :, 0:DH], p_misc[:, T:2 * T].rearrange("p (t h e) -> p t h e", t=PER, e=DH),
                                   ACT.Identity).then_inc(v_copied, 1)

                def copy_feat(g, par, n):
                    side, t, half = TURNS[n]
                    act.wait_ge(feat_turned, NT * g + n + 1)
                    cols = slice(t * P, (t + 1) * P)
                    src = p_turn[n % 2][:, :].rearrange("p (m q) -> p m q", m=PAIRS // 2)
                    if side == "k":
                        act.activation(k_t[par][:, half * PAIRS // 2:(half + 1) * PAIRS // 2, cols], src, ACT.Identity).then_inc(feat_copied, 1)
                    else:
                        for odd in range(2):
                            rows = slice(odd * FH, (odd + 1) * FH)
                            heads = slice(half * H // 2 + odd, (half + 1) * H // 2, 2)
                            ins = act.activation(q_t[par][rows, heads, cols], src[rows], ACT.Identity)
                        ins.then_inc(feat_copied, 1)

                def copy_z(g, half):
                    act.wait_ge(z_done, 4 + U * g + (half + 1) * U // 2)
                    act.wait_ge(y_done, ROOM + g)
                    act.activation(z_t[:, 2 * half:2 * half + 2, :], p_z[:, :].rearrange("p (c q) -> p c q", c=2),
                                   ACT.Identity).then_inc(z_copied, 1)

                normalise(0)
                copy_xt(0)
                copy_v(0, 0)
                for n in range(NT):
                    copy_feat(0, 0, n)
                normalise(1)

                def turn(g, par, more, more2):
                    act.wait_ge(kv_done, ROOM + g + 1)
                    act.wait_ge(z_done, 4 + U * g)
                    act.activation(kv[:], p_kv[:, :].rearrange("p (h e) -> p h e", e=32), ACT.Identity).then_inc(kv_copied, 1)
                    if more:
                        copy_xt(g + 1)
                        copy_v(g + 1, 1 - par)
                        copy_feat(g + 1, 1 - par, 0)
                    copy_z(g, 0)
                    if more:
                        for n in range(1, 5):
                            copy_feat(g + 1, 1 - par, n)
                    copy_z(g, 1)
                    if more:
                        for n in range(5, NT):
                            copy_feat(g + 1, 1 - par, n)
                    if more2:
                        normalise(g + 2)

                plan(act, turn)

            @block.vector
            def _(dve):
                dve.wait_ge(weights, 80)

                def rotate(g, t):
                    dve.wait_ge(proj_done, PER * g + t + 1)
                    if not isinstance(g, int) or g > 0:
                        dve.wait_ge(roped_done, 2 * PER * g)
                    src = p_turn[t][:, :].rearrange("p (s e) -> p s e", e=DH)
                    for n, dst in enumerate((straight, crossed)):
                        dve.tensor_tensor(dst[:, t, :, :, :].rearrange("p s a e -> p s (a e)"), src,
                                          rope[:, t, n, None, :].broadcast_to([P, 4 * H, DH]), ALU.mult).then_inc(terms_done, 1)

                def features(g, t):
                    dve.wait_ge(roped_done, 2 * PER * g + 2 * t + 2)
                    if not isinstance(g, int) or g > 0:
                        dve.wait_ge(feat_turned, NT * g)
                    dve.tensor_tensor(feat_q[:, t, :, :, :], roped[:, t, 0, :, :, None].broadcast_to([P, H, DH, DH]),
                                      roped[:, t, 1, :, None, :].broadcast_to([P, H, DH, DH]), ALU.mult).then_inc(feat_q_done, 1)

                def mask(g, u):
                    dve.wait_ge(p_done, U * g + u + 1)
                    dve.wait_ge(z_done, U * g + u + 1)
                    dve.tensor_tensor(patt[u % 4][:], p_patt[u % 2][:, :].rearrange("p (h q) -> p h q", q=P),
                                      causal[:, None, :].broadcast_to([P, 4, P]), ALU.mult).then_inc(masked, 1)

                rotate(0, 0)
                rotate(0, 1)
                features(0, 0)
                features(0, 1)

                def turn(g, par, more, more2):
                    mask(g, 0)
                    mask(g, 1)
                    if more:
                        rotate(g + 1, 0)
                        rotate(g + 1, 1)
                    mask(g, 2)
                    mask(g, 3)
                    if more:
                        features(g + 1, 0)
                    mask(g, 4)
                    mask(g, 5)
                    if more:
                        features(g + 1, 1)
                    mask(g, 6)
                    mask(g, 7)
                    dve.wait_ge(y_done, ROOM + g + 1)
                    xs = k["x"][:, at(PER * g, PER), :]
                    dve.scalar_tensor_tensor(xs, p_y[:, 0:T].rearrange("p (t e) -> p t e", t=PER), 1.0 / (DH * DH),
                                             xs, ALU.mult, ALU.add).then_inc(x_added, 1)
                    dve.wait_ge(x_added, g + 1)
                    for t in range(PER):
                        dve.bn_stats(k["halves"][:, at(PER * g + t), :].rearrange("p a s -> p (a s)"),
                                     k["x"][:, at(PER * g + t), :].rearrange("p a e -> p (a e)")).then_inc(measured, 1)

                plan(dve, turn)

            @block.tensor
            def _(pe):
                pe.wait_ge(weights, 80)

                def transposes(g):
                    pe.wait_ge(xn_done, PER * g + PER)
                    if not isinstance(g, int) or g > 0:
                        pe.wait_ge(v_copied, g)
                    for t in range(PER):
                        mm = pe.transpose(p_misc[:, t * P:(t + 1) * P], xn[:, t, :], k["ident"][:])
                    mm.then_inc(xt_done, 1)

                def projections(g):
                    pe.wait_ge(xt_copied, ROOM + g + 1)
                    for t in range(PER):
                        if not isinstance(g, int) or g > 0:
                            pe.wait_ge(feat_copied, ROOM + NT * g - PER + t + 1)
                        pe.matmul(p_turn[t][:], xn_t[:, t * P:(t + 1) * P], w_qk[:].rearrange("p s e -> p (s e)"),
                                  start=True, stop=True).then_inc(proj_done, 1)

                def values(g):
                    pe.wait_ge(xt_copied, ROOM + g + 1)
                    for t in range(PER):
                        mm = pe.matmul(p_misc[:, T + t * P:T + (t + 1) * P], xn_t[:, t * P:(t + 1) * P], w_v[:],
                                       start=True, stop=True)
                    mm.then_inc(v_done, 1)

                def turn_features(g, n):
                    side, t, half = TURNS[n]
                    if side == "k":
                        pe.wait_ge(feat_k_done, PER * g + t + 1)
                        src = feat_k
                    else:
                        pe.wait_ge(feat_q_done, PER * g + t + 1)
                        src = feat_q
                    if n < PER:
                        pe.wait_ge(terms_done, 2 * PER * g + 2 * n + 2)
                    else:
                        pe.wait_ge(feat_copied, ROOM + NT * g + n - 1)
                    flat = src[:, t, :, :, :].rearrange("p h i j -> p (h i j)")
                    for m in range(PAIRS // 2):
                        pair = half * PAIRS // 2 + m
                        mm = pe.transpose(p_turn[n % 2][:, m * P:(m + 1) * P], flat[:, pair * P:(pair + 1) * P], k["ident"][:])
                    mm.then_inc(feat_turned, 1)

                def keys_and_values(g, par):
                    pe.wait_ge(v_copied, g + 1)
                    pe.wait_ge(feat_k_done, PER * g + PER)
                    flat = feat_k[:, 0, :, :, :].rearrange("p h i j -> p (h i j)")
                    if not isinstance(g, int) or g > 0:
                        pe.wait_ge(kv_copied, g)
                    for m in range(PAIRS):
                        mm = pe.matmul(p_kv[:, m * 64:(m + 1) * 64], flat[:, m * P:(m + 1) * P],
                                       v[par][:, 0, 2 * m:2 * m + 2, :].rearrange("p h e -> p (h e)"), start=True, stop=True)
                    mm.then_inc(kv_done, 1)

                def pattern(g, par, u):
                    quad, t = u // PER, u % PER
                    pe.wait_ge(masked, U * g + u + 1)
                    cols = slice(t * P, (t + 1) * P)
                    for m in range(2):
                        pair = 2 * quad + m
                        mm = pe.matmul(p_patt[u % 2][:, m * 2 * P:(m + 1) * 2 * P], k_t[par][:, pair, cols],
                                       q_t[par][:, 2 * pair:2 * pair + 2, cols], start=True, stop=True)
                    mm.then_inc(p_done, 1)

                def z(g, par, u):
                    quad, t = u // PER, u % PER
                    pe.wait_ge(masked, 2 + U * g + u + 1)
                    if u == 0:
                        pe.wait_ge(z_copied, ROOM + 2 * g)
                    if u == U // 2:
                        pe.wait_ge(z_copied, ROOM + 2 * g + 1)
                    if u == 1:
                        pe.wait_ge(kv_copied, g + 1)
                    for c in range(4):
                        h = 4 * quad + c
                        out = p_z[32 * c:32 * c + 32, (quad % 2) * T + t * P:(quad % 2) * T + (t + 1) * P]
                        mm = pe.matmul(out, v[par][:, t, h, :], patt[u % 4][:, c, :], start=True, stop=(t == 0))
                        if t:
                            mm = pe.matmul(out, kv[:, h, :], q_t[par][:, h, P:T], start=False, stop=True)
                    mm.then_inc(z_done, 1)

                def output(g):
                    pe.wait_ge(z_copied, ROOM + 2 * g + 2)
                    if not isinstance(g, int) or g > 0:
                        pe.wait_ge(x_added, g)
                    for t in range(PER):
                        for j in range(4):
                            mm = pe.matmul(p_y[:, t * P:(t + 1) * P], z_t[:, j, t * P:(t + 1) * P], w_proj[:, j, :],
                                           start=(j == 0), stop=(j == 3))
                    mm.then_inc(y_done, 1)

                transposes(0)
                projections(0)
                values(0)
                for n in range(NT):
                    turn_features(0, n)

                def turn(g, par, more, more2):
                    keys_and_values(g, par)
                    if more:
                        transposes(g + 1)
                    pe.wait_ge(feat_copied, ROOM + NT * g + NT)
                    pattern(g, par, 0)
                    pattern(g, par, 1)
                    if more:
                        projections(g + 1)
                    z(g, par, 0)
                    pattern(g, par, 2)
                    if more:
                        values(g + 1)
                    z(g, par, 1)
                    pattern(g, par, 3)
                    z(g, par, 2)
                    for u in range(4, U):
                        pattern(g, par, u)
                        if more:
                            turn_features(g + 1, u - 4)
                        z(g, par, u - 1)
                    if more:
                        turn_features(g + 1, 4)
                    z(g, par, U - 1)
                    if more:
                        for n in range(5, NT):
                            turn_features(g + 1, n)
                    output(g)

                plan(pe, turn)


def normalise_for_experts(nc, sem, d, k, norm_rows, layer):
    tag = f"n{layer}"
    steps = TILES // GROUP
    NB = 4
    with ExitStack() as ctx:
        def sb(name, shape, dt=F32):
            return ctx.enter_context(nc.sbuf_tensor(f"{name}_{tag}", shape, dt))

        def ps(name):
            return ctx.enter_context(nc.psum_tensor(f"{name}_{tag}", [P, 512], F32))

        k = {**k, "rstd_1": sb("rstd_1", [P, TILES]), "rstd_2": sb("rstd_2", [P, TILES]), "shift_2": sb("shift_2", [P, TILES])}
        statistics(nc, sem, k, tag, twice=True)
        gain = sb("gain", [P, D])
        bias = sb("bias", [P, D])
        cent = sb("cent", [P, E])
        raw = [sb(f"raw{i}", [P, GROUP, D]) for i in range(2)]
        gained = [sb(f"gained{i}", [P, GROUP, D]) for i in range(2)]
        norm = [sb(f"norm{i}", [P, GROUP, D]) for i in range(NB)]
        norm_t = [sb(f"norm_t{i}", [P, GROUP, P]) for i in range(2)]
        p_t = [ps(f"p_t{i}") for i in range(2)]
        p_sc = ps("p_sc")
        loaded = sem(f"gb_loaded_{tag}")
        raw_done = sem(f"raw_done_{tag}")
        gained_done = sem(f"gained_done_{tag}")
        norm_done = sem(f"norm_done_{tag}")
        stored = [sem(f"norm_stored{i}_{tag}") for i in range(NB)]
        turned = sem(f"turned_{tag}")
        copied = sem(f"turned_copied_{tag}")
        scored = sem(f"scored_{tag}")
        kept = sem(f"scores_kept_{tag}")
        x_done = sem(f"x_done_{tag}")
        rows = norm_rows.rearrange("(n p) d -> p n d", p=P)

        def plan(eng, turn):
            with eng.Fori(0, steps // NB) as i:
                for b in range(NB):
                    turn(NB * i + b, b, i)

        with nc.Block() as block:
            @block.sync
            def _(sp):
                for counter in (gained_done, norm_done, copied, scored):
                    sp.sem_inc(counter, 2)
                for counter in stored:
                    sp.sem_inc(counter, ROOM)
                sp.sem_inc(turned, NB)
                sp.dma_start(gain[:], d["L0_ffn_ln_g"].rearrange("(a d) -> a d", a=1).broadcast_to([P, D])).then_inc(loaded, 16)
                sp.dma_start(bias[:], d["L0_ffn_ln_b"].rearrange("(a d) -> a d", a=1).broadcast_to([P, D])).then_inc(loaded, 16)
                sp.dma_start(cent[:], d["centroids_t"]).then_inc(loaded, 16)

                def turn(g, b, i):
                    sp.wait_ge(norm_done, g + 3)
                    sp.dma_start(rows[:, bass.ds(GROUP * g, GROUP), :], norm[b][:]).then_inc(stored[b], 16)

                plan(sp, turn)
                for counter in stored:
                    sp.wait_ge(counter, ROOM + 16 * (steps // NB))

            @block.vector
            def _(dve):
                dve.wait_ge(loaded, 48)

                def turn(g, b, i):
                    dve.wait_ge(gained_done, g + 1)
                    for j in range(GROUP):
                        n = GROUP * g + j
                        dve.tensor_scalar(raw[b % 2][:, j, :], k["x"][:, n, :], k["rstd_2"][:, bass.ds(n, 1)],
                                          k["shift_2"][:, bass.ds(n, 1)], ALU.mult, ALU.add).then_inc(raw_done, 1)
                    dve.wait_ge(raw_done, GROUP * g + GROUP)
                    dve.wait_ge(norm_done, g + 1)
                    dve.tensor_tensor(gained[b % 2][:], raw[b % 2][:], gain[:, None, :].broadcast_to([P, GROUP, D]),
                                      ALU.mult).then_inc(gained_done, 1)

                plan(dve, turn)
                dve.wait_ge(scored, steps + 2)
                dve.tensor_copy(k["scores"][:, :, :], p_sc[:, :].rearrange("p (n e) -> p e n", e=E)).then_inc(kept, 1)

            @block.gpsimd
            def _(pool):
                pool.wait_ge(loaded, 48)

                def turn(g, b, i):
                    pool.wait_ge(gained_done, g + 3)
                    pool.wait_ge(stored[b], ROOM + 16 * i)
                    pool.wait_ge(turned, g + 1)
                    pool.tensor_tensor(norm[b][:], gained[b % 2][:], bias[:, None, :].broadcast_to([P, GROUP, D]),
                                       ALU.add).then_inc(norm_done, 1)

                plan(pool, turn)

            @block.tensor
            def _(pe):
                pe.wait_ge(loaded, 48)

                def turn(g, b, i):
                    pe.wait_ge(norm_done, g + 3)
                    pe.wait_ge(copied, g + 1)
                    for j in range(GROUP):
                        mm = pe.transpose(p_t[b % 2][:, j * P:(j + 1) * P], norm[b][:, j, :], k["ident"][:])
                    mm.then_inc(turned, 1)
                    pe.wait_ge(copied, g + 3)
                    for j in range(GROUP):
                        mm = pe.matmul(p_sc[:, bass.ds((GROUP * g + j) * E, E)], norm_t[b % 2][:, j, :], cent[:],
                                       start=True, stop=True)
                    mm.then_inc(scored, 1)

                plan(pe, turn)

            @block.scalar
            def _(act):
                def turn(g, b, i):
                    act.wait_ge(raw_done, GROUP * g + GROUP)
                    for j in range(GROUP):
                        n = GROUP * g + j
                        act.activation(k["x"][:, n, :], k["x"][:, n, :], ACT.Identity, bias=k["shift"][:, bass.ds(n, 1)],
                                       scale=k["rstd_1"][:, bass.ds(n, 1)]).then_inc(x_done, 1)
                    act.wait_ge(turned, g + NB + 1)
                    act.wait_ge(scored, g + 1)
                    act.activation(norm_t[b % 2][:], p_t[b % 2][:, :].rearrange("p (j q) -> p j q", j=GROUP),
                                   ACT.Identity).then_inc(copied, 1)

                plan(act, turn)


def experts(nc, sem, d, k, norm_rows, ffn_rows, layer):
    tag = f"e{layer}"
    CHUNKS = 8
    per = TILES // CHUNKS
    with ExitStack() as ctx:
        def sb(name, shape, dt=F32):
            return ctx.enter_context(nc.sbuf_tensor(f"{name}_{tag}", shape, dt))

        def ps(name):
            return ctx.enter_context(nc.psum_tensor(f"{name}_{tag}", [P, 512], F32))

        first_cand = sb("first_cand", [P, CANDS])
        digits = sb("digits", [P, PASSES, CANDS], U32)
        weight = sb("weight", [P, PASSES])
        before = sb("before", [P, P], BF16)
        ones = sb("ones", [P, P], BF16)
        lanes = sb("lanes", [P, P], BF16)
        place = sb("place", [P, TILES, 2, SLOTS], BF16)
        eighth = sb("eighth", [P, 2, SLOTS], BF16)
        ones_f = sb("ones_f", [P, TILES])
        avail = sb("avail", [P, TILES])
        s = sb("s", [P, TILES])
        cand = sb("cand", [P, CANDS], U32)
        reach = sb("reach", [P, TILES, CANDS], BF16)
        count = sb("count", [P, CANDS])
        passed = sb("passed", [P, CANDS])
        found = sb("found", [P, 1], U32)
        prefix = sb("prefix", [P, 1], U32)
        flip = sb("flip", [P, 1], U32)
        above = sb("above", [P, TILES], BF16)
        equal = sb("equal", [P, TILES], BF16)
        total = sb("total", [P, TILES])
        sure = sb("sure", [P, 1])
        need = sb("need", [P, 1])
        rank = sb("rank", [P, TILES])
        within = sb("within", [P, TILES])
        chosen = [sb(f"chosen{i}", [P, TILES], BF16) for i in range(2)]
        upto = sb("upto", [P, TILES])
        order = sb("order", [P, TILES])
        slot = sb("slot", [P, TILES])
        slot_i = sb("slot_i", [P, TILES], I32)
        low = sb("low", [P, TILES], I32)
        high = sb("high", [P, TILES], I32)
        low_b = sb("low_b", [P, TILES], BF16)
        high_b = sb("high_b", [P, TILES], BF16)
        lane_of = sb("lane_of", [P, TILES, P], BF16)
        tile_is = sb("tile_is", [P, TILES, 2 * SLOTS], BF16)
        tile_of = sb("tile_of", [P, TILES, 2, SLOTS], BF16)
        tok_hi = sb("tok_hi", [P, SLOTS])
        index = [sb(f"index{i}", [P, SLOTS], U32) for i in range(2)]
        w1 = [sb(f"w1_{i}", [P, F]) for i in range(2)]
        w2 = [sb(f"w2_{i}", [P, FC, D]) for i in range(2)]
        b1 = [sb(f"b1_{i}", [P, FC]) for i in range(2)]
        b2 = [sb(f"b2_{i}", [P, D]) for i in range(2)]
        rows = [sb(f"rows{i}", [P, SLOTS, D]) for i in range(2)]
        rows_t = sb("rows_t", [P, CAP])
        hid = sb("hid", [P, FC, CAP])
        y = sb("y", [P, SLOTS, D])
        yb = [sb(f"yb{i}", [P, SLOTS, D]) for i in range(2)]
        p_cnt = ps("p_cnt")
        p_rank = ps("p_rank")
        p_list = ps("p_list")
        p_t = ps("p_t")
        p_h = [ps(f"p_h{i}") for i in range(2)]
        p_y = [ps(f"p_y{i}") for i in range(2)]
        p_idx = p_list[:, 2 * TILES:2 * TILES + 2 * SLOTS]

        consts = sem(f"consts_{tag}")
        wl = [sem(f"expert_loaded{i}_{tag}") for i in range(2)]
        reached = sem(f"reached_{tag}")
        counted = sem(f"counted_{tag}")
        sv = sem(f"search_step_{tag}")
        lv = sem(f"list_step_{tag}")
        prefixed = sem(f"prefixed_{tag}")
        marked = sem(f"marked_{tag}")
        ranked = sem(f"ranked_{tag}")
        chosen_done = sem(f"chosen_{tag}")
        chosen_ranked = sem(f"chosen_ranked_{tag}")
        slots_done = sem(f"slots_done_{tag}")
        lanes_done = sem(f"lanes_done_{tag}")
        tiles_done = sem(f"tiles_done_{tag}")
        listed = sem(f"listed_{tag}")
        index_done = sem(f"index_done_{tag}")
        gathered = [sem(f"gathered{i}_{tag}") for i in range(2)]
        rt_done = sem(f"rows_turned_{tag}")
        rt_copied = sem(f"rows_t_copied_{tag}")
        up_done = sem(f"up_done_{tag}")
        gelu_done = sem(f"gelu_done_{tag}")
        down_done = sem(f"down_done_{tag}")
        y_copied = sem(f"y_copied_{tag}")
        y_ready = sem(f"y_ready_{tag}")
        scattered = [sem(f"scattered{i}_{tag}") for i in range(2)]
        scatters_seen = sem(f"scatters_seen_{tag}")
        wait_passed = sem(f"passed_{tag}")

        def plan(eng, turn):
            for e in range(3):
                turn(e, e % 2, e // 2)
            with eng.Fori(0, (E - 4) // 2) as i:
                turn(2 * i + 3, 1, i + 1)
                turn(2 * i + 4, 0, i + 2)
            for e in range(E - 1, E + 2):
                turn(e, e % 2, e // 2)

        def does(e):
            if not isinstance(e, int):
                return True, (e - 1,), True
            lists = () if e == 0 or e > E - 1 else (e - 1,) if e < E - 1 else (e - 1, e)
            return e < E - 1, lists, e >= 2

        MARK_LINKS = 1 + 4 * PASSES + 3 + 1
        SEARCH_LINKS = MARK_LINKS + 6
        PREFIXES = PASSES - 2
        LIST_LINKS = 8

        with nc.Block() as block:
            @block.sync
            def _(sp):
                for dst, src in ((first_cand, "c_first_cand"), (digits, "c_digits"), (weight, "c_weight"),
                                 (before, "c_before"), (lanes, "c_lanes"), (place, "c_place"), (eighth, "c_eighth")):
                    sp.dma_start(dst[:], d[src]).then_inc(consts, 16)

                def turn(e, par, half):
                    if isinstance(e, int) and e >= E:
                        return
                    at = bass.ds(e, 1) if not isinstance(e, int) else slice(e, e + 1)
                    w1_src = d["L0_ffn_w1"][at, :, :].rearrange("a p f -> (a p) f")
                    w2_src = d["L0_ffn_w2"][at, :, :].rearrange("a (p c) n -> (a p) c n", c=FC)
                    b1_src = d["L0_ffn_b1"][at, :].rearrange("a (p c) -> (a p) c", c=FC)
                    b2_src = d["L0_ffn_b2"][at, :].broadcast_to([P, D])
                    if not isinstance(e, int) or e > 1:
                        sp.wait_ge(y_ready, e - 1)
                    sp.dma_start(w1[par][:], w1_src).then_inc(wl[par], 16)
                    sp.dma_start(w2[par][:], w2_src).then_inc(wl[par], 16)
                    sp.dma_start(b1[par][:], b1_src).then_inc(wl[par], 16)
                    sp.dma_start(b2[par][:], b2_src).then_inc(wl[par], 16)

                plan(sp, turn)

            @block.vector
            def _(dve):
                dve.wait_ge(consts, 16 * 7)
                dve.memset(ones[:], 1.0).then_inc(sv, 1)
                dve.memset(ones_f[:], 1.0).then_inc(sv, 1)
                dve.memset(avail[:], -TAKEN).then_inc(sv, 1)
                dve.wait_ge(sv, 3)

                def listing(l, par):
                    done = [0]

                    def link(ins):
                        done[0] += 1
                        ins.then_inc(lv, 1)
                        dve.wait_ge(lv, LIST_LINKS * l + done[0])

                    def slots():
                        dve.wait_ge(chosen_ranked, l + 1)
                        link(dve.tensor_tensor_scan(upto[:], ones_f[:], p_list[:, TILES:2 * TILES], 0.0, ALU.mult, ALU.add))
                        link(dve.tensor_tensor(order[:], upto[:], p_list[:, 0:TILES], ALU.add))
                        link(dve.scalar_tensor_tensor(slot[:], order[:], 1.0, chosen[par][:], ALU.add, ALU.mult))

                    def parts():
                        link(dve.tensor_scalar(slot_i[:], slot[:], -1.0, None, ALU.add))
                        dve.tensor_scalar(low[:], slot_i[:], P - 1, None, ALU.bitwise_and).then_inc(lv, 1)
                        done[0] += 1
                        link(dve.tensor_scalar(high[:], slot_i[:], 7, None, ALU.arith_shift_right))

                    def narrow():
                        dve.tensor_copy(low_b[:], low[:]).then_inc(lv, 1)
                        done[0] += 1
                        link(dve.tensor_copy(high_b[:], high[:]))
                        if not isinstance(l, int) or l > 0:
                            dve.wait_ge(tiles_done, l)
                        dve.tensor_tensor(tile_is[:], high_b[:, :, None].broadcast_to([P, TILES, 2 * SLOTS]),
                                          eighth[:].rearrange("p a b -> p (a b)")[:, None, :].broadcast_to([P, TILES, 2 * SLOTS]),
                                          ALU.is_equal).then_inc(slots_done, 1)

                    def lane_chunk(c):
                        if c == 0 and (not isinstance(l, int) or l > 0):
                            dve.wait_ge(listed, l)
                        part = slice(c * per, (c + 1) * per)
                        dve.tensor_tensor(lane_of[:, part, :], low_b[:, part, None].broadcast_to([P, per, P]),
                                          lanes[:, None, :].broadcast_to([P, per, P]), ALU.is_equal).then_inc(lanes_done, 1)

                    def result():
                        dve.wait_ge(listed, l + 1)
                        if not isinstance(l, int) or l > 1:
                            dve.wait_ge(scatters_seen, l - 1)
                        dve.tensor_scalar(tok_hi[:], p_idx[:, 0:SLOTS], float(P), None, ALU.mult).then_inc(index_done, 1)
                        dve.wait_ge(index_done, 2 * l + 1)
                        dve.tensor_tensor(index[par][:], tok_hi[:], p_idx[:, SLOTS:2 * SLOTS], ALU.add).then_inc(index_done, 1)
                        assert done[0] == LIST_LINKS, done

                    return slots, parts, narrow, lane_chunk, result

                def turn(e, par, half):
                    seek, lists, _ = does(e)
                    done = [0]

                    def link(ins):
                        done[0] += 1
                        ins.then_inc(sv, 1)
                        dve.wait_ge(sv, 3 + SEARCH_LINKS * e + done[0])

                    if isinstance(e, int) and e >= E:
                        return
                    at = bass.ds(e, 1) if not isinstance(e, int) else slice(e, e + 1)
                    if not seek:
                        dve.tensor_scalar(chosen[par][:], avail[:], 0.0, None, ALU.is_gt).then_inc(chosen_done, 1)
                        for l in lists:
                            slots, parts, narrow, lane_chunk, result = listing(l, l % 2)
                            slots(), parts(), narrow()
                            for c in range(CHUNKS):
                                lane_chunk(c)
                            result()
                        return
                    windows = [[] for _ in range(PASSES)]
                    if lists:
                        slots, parts, narrow, lane_chunk, result = listing(lists[0], 1 - par)
                        chunks = [lambda c=c: lane_chunk(c) for c in range(CHUNKS)]
                        windows = [[slots], [parts, narrow], chunks[0:2], chunks[2:4], chunks[4:6], chunks[6:8], [], [result]]
                    link(dve.tensor_tensor(s[:], k["scores"][:, at, :].rearrange("p a n -> p (a n)"), avail[:], ALU.min))
                    for n in range(PASSES):
                        c = (first_cand[:] if n == 0 else cand[:].bitcast(F32))[:, None, :].broadcast_to([P, TILES, CANDS])
                        dve.tensor_tensor(reach[:], s[:, :, None].broadcast_to([P, TILES, CANDS]), c,
                                          ALU.is_ge).then_inc(reached, 1)
                        for piece in windows[n]:
                            piece()
                        dve.wait_ge(counted, PASSES * e + n + 1)
                        link(dve.tensor_reduce(count[:], p_cnt[:, 0:8 * CANDS].rearrange("p (n c) -> p c n", c=CANDS), AX.X, ALU.add))
                        link(dve.tensor_scalar(passed[:], count[:], float(CAP), weight[:, n:n + 1], ALU.is_ge, ALU.mult))
                        with nc.allow_low_precision(reason="a digit times its weight is exact in both"):
                            link(dve.tensor_reduce(found[:], passed[:], AX.X, ALU.add))
                        if n == 0:
                            link(dve.tensor_scalar(flip[:].bitcast(I32), found[:].bitcast(I32), -1, 31, ALU.bitwise_xor, ALU.arith_shift_right))
                            link(dve.tensor_scalar(flip[:].bitcast(I32), flip[:].bitcast(I32), -2**31, None, ALU.bitwise_or))
                            link(dve.tensor_tensor(prefix[:], found[:], flip[:], ALU.bitwise_xor))
                            link(dve.tensor_scalar(cand[:], digits[:, 1, :], prefix[:, 0:1], None, ALU.bitwise_xor))
                        elif n + 1 < PASSES:
                            link(dve.tensor_scalar(cand[:], digits[:, n + 1, :], prefix[:, 0:1], found[:, 0:1],
                                                   ALU.bitwise_xor, ALU.bitwise_xor))
                            dve.tensor_tensor(prefix[:], prefix[:], found[:], ALU.bitwise_xor).then_inc(prefixed, 1)
                            dve.wait_ge(prefixed, PREFIXES * e + n)
                        else:
                            link(dve.tensor_tensor(prefix[:], prefix[:], found[:], ALU.bitwise_xor))
                    limit = prefix[:].bitcast(F32)
                    dve.tensor_scalar(equal[:], s[:], limit, None, ALU.is_equal).then_inc(marked, 1)
                    link(dve.tensor_scalar(above[:], s[:], limit, None, ALU.is_gt))
                    dve.wait_ge(ranked, e + 1)
                    link(dve.tensor_reduce(sure[:], p_rank[:, 2 * TILES:3 * TILES], AX.X, ALU.add))
                    link(dve.tensor_scalar(need[:], sure[:], -1.0, float(CAP), ALU.mult, ALU.add))
                    link(dve.tensor_tensor_scan(total[:], ones_f[:], p_rank[:, TILES:2 * TILES], 0.0, ALU.mult, ALU.add))
                    link(dve.tensor_tensor(rank[:], total[:], p_rank[:, 0:TILES], ALU.add))
                    link(dve.scalar_tensor_tensor(within[:], rank[:], need[:, 0:1], equal[:], ALU.is_lt, ALU.mult))
                    dve.tensor_tensor(chosen[par][:], within[:], above[:], ALU.add).then_inc(chosen_done, 1)
                    dve.wait_ge(chosen_done, e + 1)
                    link(dve.scalar_tensor_tensor(avail[:], chosen[par][:], 2 * TAKEN, avail[:], ALU.mult, ALU.add))
                    assert done[0] == SEARCH_LINKS, done

                plan(dve, turn)

            @block.tensor
            def _(pe):
                pe.wait_ge(consts, 16 * 7)
                pe.wait_ge(sv, 3)

                def turn(e, par, half):
                    seek, lists, compute = does(e)
                    c = e - 2

                    def turn_rows(h):
                        if h == 0:
                            pe.wait_ge(gathered[par], 16 * SLOTS * half)
                            pe.wait_ge(wl[par], 64 * half)
                        if not isinstance(e, int) or c > 0 or h > 0:
                            pe.wait_ge(rt_copied, 2 * c + h)
                        for j in range(4):
                            mm = pe.transpose(p_t[:, j * P:(j + 1) * P], rows[par][:, 4 * h + j, :], k["ident"][:])
                        mm.then_inc(rt_done, 1)

                    def up(m):
                        f, h = m % FC, m // FC
                        pe.wait_ge(rt_copied, 2 * c + h + 1)
                        if m >= 2:
                            pe.wait_ge(gelu_done, 8 * c + m - 1)
                        pe.matmul(p_h[m % 2][:], w1[par][:, f:F:FC], rows_t[:, h * 512:(h + 1) * 512],
                                  start=True, stop=True).then_inc(up_done, 1)

                    def down(t):
                        pe.wait_ge(gelu_done, 8 * c + (4 if t < 4 else 8))
                        if t % 4 == 0 and (not isinstance(e, int) or c > 0):
                            pe.wait_ge(y_copied, 2 * c - 1 + t // 4)
                        for f in range(FC):
                            mm = pe.matmul(p_y[t // 4][:, (t % 4) * D:(t % 4 + 1) * D], hid[:, f, t * P:(t + 1) * P], w2[par][:, f, :],
                                           start=(f == 0), stop=(f == FC - 1))
                        if t % 4 == 3:
                            mm.then_inc(down_done, 1)

                    def list_chunk(l, n):
                        pe.wait_ge(lanes_done, CHUNKS * l + n + 1)
                        if n == 0:
                            pe.wait_ge(tiles_done, l + 1)
                        for t in range(n * per, (n + 1) * per):
                            mm = pe.matmul(p_idx, lane_of[:, t, :], tile_of[:, t, :, :].rearrange("p a b -> p (a b)"),
                                           start=(t == 0), stop=(t == TILES - 1))
                        if n == CHUNKS - 1:
                            mm.then_inc(listed, 1)

                    def rank_chosen(l, lpar):
                        pe.wait_ge(chosen_done, l + 1)
                        if not isinstance(l, int) or l > 0:
                            pe.wait_ge(index_done, 2 * l)
                        pe.matmul(p_list[:, 0:TILES], before[:], chosen[lpar][:], start=True, stop=True)
                        pe.matmul(p_list[:, TILES:2 * TILES], ones[:], chosen[lpar][:], start=True, stop=True).then_inc(chosen_ranked, 1)

                    pieces = [[] for _ in range(PASSES + 2)]
                    if compute:
                        pieces = [[lambda: turn_rows(0)], [lambda: turn_rows(1), lambda: up(0)],
                                  [lambda: up(1), lambda: up(2)], [lambda: up(3), lambda: up(4)],
                                  [lambda: up(5), lambda: up(6)], [lambda: up(7), lambda: down(0)],
                                  [lambda: down(1), lambda: down(2)], [lambda: down(3), lambda: down(4)],
                                  [lambda: down(5)], [lambda: down(6), lambda: down(7)]]
                    if not seek:
                        for l in lists:
                            if l == E - 1:
                                rank_chosen(l, l % 2)
                            for n in range(CHUNKS):
                                list_chunk(l, n)
                        for piece in sum(pieces, []):
                            piece()
                        return
                    if lists:
                        l = lists[0]
                        for n in range(2, 6):
                            pieces[n + 1] = [lambda n=n: list_chunk(l, 2 * n - 4), lambda n=n: list_chunk(l, 2 * n - 3)] + pieces[n + 1]
                    for n in range(PASSES):
                        pe.wait_ge(reached, PASSES * e + n + 1)
                        for q in range(8):
                            mm = pe.matmul(p_cnt[:, 0:8 * CANDS], ones[:],
                                           reach[:, q * 8:(q + 1) * 8, :].rearrange("p n c -> p (n c)"),
                                           start=(q == 0), stop=(q == 7))
                        mm.then_inc(counted, 1)
                        for piece in pieces[n]:
                            piece()
                    pe.wait_ge(marked, e + 1)
                    pe.matmul(p_rank[:, 0:TILES], before[:], equal[:], start=True, stop=True)
                    pe.matmul(p_rank[:, TILES:2 * TILES], ones[:], equal[:], start=True, stop=True)
                    pe.wait_ge(sv, 3 + SEARCH_LINKS * e + MARK_LINKS)
                    pe.matmul(p_rank[:, 2 * TILES:3 * TILES], ones[:], above[:], start=True, stop=True).then_inc(ranked, 1)
                    for piece in pieces[PASSES]:
                        piece()
                    rank_chosen(e, par)
                    for piece in pieces[PASSES + 1]:
                        piece()

                plan(pe, turn)

            @block.scalar
            def _(act):
                def turn(e, par, half):
                    _, _, compute = does(e)
                    if not compute:
                        return
                    c = e - 2
                    later = not isinstance(e, int) or c > 0

                    def copy_rows(h):
                        act.wait_ge(rt_done, 2 * c + h + 1)
                        if later:
                            act.wait_ge(up_done, 8 * c)
                        act.activation(rows_t[:, h * 512:(h + 1) * 512], p_t[:], ACT.Identity).then_inc(rt_copied, 1)

                    def gelu(m):
                        f, h = m % FC, m // FC
                        act.wait_ge(up_done, 8 * c + m + 1)
                        if later:
                            act.wait_ge(down_done, 2 * c)
                        act.wait_ge(wl[par], 64 * half)
                        act.activation(hid[:, f, h * 512:(h + 1) * 512], p_h[m % 2][:], ACT.Gelu_apprx_tanh,
                                       bias=b1[par][:, f:f + 1]).then_inc(gelu_done, 1)

                    def copy_y(h):
                        act.wait_ge(down_done, 2 * c + h + 1)
                        if later:
                            act.wait_ge(y_ready, c)
                        act.activation(y[:, 4 * h:4 * h + 4, :], p_y[h][:, :].rearrange("p (t n) -> p t n", n=D),
                                       ACT.Identity).then_inc(y_copied, 1)

                    copy_rows(0)
                    copy_rows(1)
                    for m in range(8):
                        gelu(m)
                    copy_y(0)
                    copy_y(1)

                plan(act, turn)

            @block.gpsimd
            def _(pool):
                pool.wait_ge(consts, 16 * 7)

                def tiles(l):
                    pool.wait_ge(slots_done, l + 1)
                    if not isinstance(l, int) or l > 0:
                        pool.wait_ge(listed, l)
                    pool.tensor_tensor(tile_of[:].rearrange("p n a b -> p n (a b)"), tile_is[:],
                                       place[:].rearrange("p n a b -> p n (a b)"), ALU.mult).then_inc(tiles_done, 1)

                def gather(l, lpar, seen):
                    if not isinstance(l, int) or l > 1:
                        pool.wait_ge(scattered[lpar], 16 * SLOTS * seen)
                        pool.sem_inc(scatters_seen, 1)
                        pool.wait_ge(rt_done, 2 * l - 2)
                    wait_apart(pool, index_done, 2 * l + 2, wait_passed)
                    for j in range(SLOTS):
                        pool.indirect_dma_start(rows[lpar][:, j, :], None, norm_rows,
                                                bass.IndirectOffsetOnAxis(ap=index[lpar][:, j:j + 1], axis=0)).then_inc(gathered[lpar], 16)

                def scatter(c, par, half):
                    pool.wait_ge(y_copied, 2 * c + 2)
                    pool.wait_ge(wl[par], 64 * half)
                    pool.tensor_tensor(yb[par][:], y[:], b2[par][:, None, :].broadcast_to([P, SLOTS, D]), ALU.add).then_inc(y_ready, 1)
                    wait_apart(pool, y_ready, c + 1, wait_passed)
                    for j in range(SLOTS):
                        pool.indirect_dma_start(ffn_rows, bass.IndirectOffsetOnAxis(ap=index[par][:, j:j + 1], axis=0),
                                                yb[par][:, j, :], None).then_inc(scattered[par], 16)

                def turn(e, par, half):
                    _, lists, compute = does(e)
                    if lists:
                        tiles(lists[0])
                        gather(lists[0], 1 - par, half - 1 + par)
                    for l in lists[1:]:
                        tiles(l)
                    if compute:
                        scatter(e - 2, par, half)
                    for l in lists[1:]:
                        gather(l, par, half)

                plan(pool, turn)
                for par in range(2):
                    pool.wait_ge(scattered[par], 16 * SLOTS * (E // 2))


def add_rows(nc, sem, k, rows_dram, out, layer):
    tag = f"r{layer}"
    steps = 8
    per = TILES // steps
    with ExitStack() as ctx:
        buf = [ctx.enter_context(nc.sbuf_tensor(f"buf{i}_{tag}", [P, per, D], F32)) for i in range(4)]
        loaded = [sem(f"rows_loaded{i}_{tag}") for i in range(4)]
        added = sem(f"rows_added_{tag}")
        measured = sem(f"rows_measured_{tag}")
        stored = sem(f"out_stored_{tag}")
        rows = rows_dram.rearrange("(n p) d -> p n d", p=P)
        out_v = out.rearrange("b (t p) d -> p (b t) d", p=P) if out is not None else None
        with nc.Block() as block:
            @block.sync
            def _(sp):
                for g in range(steps):
                    if g >= 4:
                        sp.wait_ge(added, g - 3)
                    sp.dma_start(buf[g % 4][:], rows[:, g * per:(g + 1) * per, :]).then_inc(loaded[g % 4], 16)
            if out is not None:
                @block.scalar
                def _(act):
                    for g in range(steps):
                        act.wait_ge(added, g + 1)
                        act.dma_start(out_v[:, g * per:(g + 1) * per, :], k["x"][:, g * per:(g + 1) * per, :]).then_inc(stored, 16)
                    act.wait_ge(stored, 16 * steps)

            @block.vector
            def _(dve):
                for g in range(steps):
                    dve.wait_ge(loaded[g % 4], 16 * (g // 4) + 16)
                    part = k["x"][:, g * per:(g + 1) * per, :]
                    dve.tensor_tensor(part, part, buf[g % 4][:], ALU.add).then_inc(added, 1)
                    if out is None:
                        dve.wait_ge(added, g + 1)
                        for n in range(g * per, (g + 1) * per):
                            dve.bn_stats(k["halves"][:, n, :], k["x"][:, n, :]).then_inc(measured, 1)


def attention_b(nc, sem, d, k):
    with ExitStack() as outer:
        def keep(name, shape, dt=F32):
            return outer.enter_context(nc.sbuf_tensor(f"{name}_ab", shape, dt))

        values = keep("values", [P, TILES, D])
        phases = keep("phases", [P, TILES, 2, RFF])
        powers = keep("powers", [P, TILES, NM])
        decay = keep("decay", [P, T])
        features(nc, d, k, sem, values, phases, powers, decay)
        attend(nc, d, k, sem, values, phases, powers, decay)


def features(nc, d, k, sem, values, phases, powers, decay):
    W = FEAT + D
    steps = TILES // GROUP
    with ExitStack() as ctx:
        def sb(name, shape, dt=F32):
            return ctx.enter_context(nc.sbuf_tensor(f"{name}_fe", shape, dt))

        def ps(name):
            return ctx.enter_context(nc.psum_tensor(f"{name}_fe", [P, 512], F32))

        w_all = sb("w_all", [P, W])
        w_shell = sb("w_shell", [SHELL, D])
        omega_t = sb("omega_t", [SHELL, RFF])
        b_shell = sb("b_shell", [SHELL, P])
        b_all = sb("b_all", [P, W])
        b_rff = sb("b_rff", [P, RFF])
        temp = sb("temp", [P, 1])
        small = [sb(f"small{i}", [P, 1]) for i in range(6)]
        a = [sb(f"a{i}", [P, GROUP, D]) for i in range(2)]
        a_t = [sb(f"a_t{i}", [P, GROUP, P]) for i in range(2)]
        feat = sb("feat", [P, TILES, FEAT])
        sq = sb("sq", [P, TILES, SHELL])
        ss = sb("ss", [P, TILES])
        length = sb("length", [P, TILES])
        proj = sb("proj", [P, TILES, RFF])
        turns = sb("turns", [P, TILES, RFF])
        arg = sb("arg", [P, TILES, 2, RFF])
        charge = sb("charge", [P, TILES])
        c_mag = sb("c_mag", [P, NM])
        p_t = [ps(f"p_t{i}") for i in range(2)]
        p_f = [[ps(f"p_f{i}{j}") for j in range(2)] for i in range(2)]
        p_w = ps("p_w")

        loaded = sem("fe_loaded")
        product = sem("fe_weight_product")
        step = sem("fe_step")
        ast = sem("fe_act_step")
        a_done = sem("fe_a_done")
        turned = [sem(f"fe_turned{i}") for i in range(2)]
        copied = [sem(f"fe_copied{i}") for i in range(2)]
        made = [sem(f"fe_made{i}") for i in range(2)]
        kept = sem("fe_kept")
        ss_done = sem("fe_ss_done")
        arg_done = sem("fe_arg_done")
        with nc.Block() as block:
            @block.sync
            def _(sp):
                for counter in (*copied, kept, *turned, *made):
                    sp.sem_inc(counter, ROOM)
                for dst, src in ((w_all[:, 0:SHELL], d["w_shell_t"]), (w_all[:, SHELL:SHELL + 1], d["w_charge_t"]),
                                 (w_all[:, FEAT:W], d["w_vb_t"]), (w_shell[:], d["L0_attn_b_W_shell"]),
                                 (omega_t[:], d["omega_t"]),
                                 (b_shell[:], d["b_shell_wide"]),
                                 (b_all[:, 0:SHELL], d["L0_attn_b_b_shell"].rearrange("(a b) -> a b", a=1).broadcast_to([P, SHELL])),
                                 (b_all[:, SHELL:SHELL + 1], d["L0_attn_b_b_charge"].rearrange("(a b) -> a b", a=1).broadcast_to([P, 1])),
                                 (b_all[:, FEAT:W], d["L0_attn_b_b_v"].rearrange("(a b) -> a b", a=1).broadcast_to([P, D])),
                                 (b_rff[:], d["L0_attn_b_rff_bias"].rearrange("(a b) -> a b", a=1).broadcast_to([P, RFF])),
                                 (temp[:], d["L0_attn_b_log_temp"].broadcast_to([P, 1])),
                                 (decay[:], d["c_decay"]), (c_mag[:], d["c_mag"])):
                    sp.dma_start(dst, src).then_inc(loaded, 16)

            @block.tensor
            def _(pe):
                pe.wait_ge(loaded, 16 * 13)
                pe.matmul(p_w[:, 0:RFF], w_shell[:], omega_t[:], start=True, stop=True).then_inc(product, 1)
                pe.matmul(p_w[:, RFF:2 * RFF], b_shell[:], omega_t[:], start=True, stop=True).then_inc(product, 1)
                pe.wait_ge(step, 2)
                with pe.Fori(0, steps // 2) as i:
                    for par in range(2):
                        g = 2 * i + par
                        pe.wait_ge(a_done, GROUP * g + GROUP)
                        pe.wait_ge(copied[par], ROOM + i)
                        for j in range(GROUP):
                            mm = pe.transpose(p_t[par][:, j * P:(j + 1) * P], a[par][:, j, :], k["ident"][:])
                        mm.then_inc(turned[par], 1)
                        pe.wait_ge(copied[par], ROOM + i + 1)
                        pe.wait_ge(kept, ROOM + 8 * i)
                        for j in range(GROUP):
                            mm = pe.matmul(p_f[par][j // 2][:, (j % 2) * 256:(j % 2) * 256 + W], a_t[par][:, j, :], w_all[:],
                                           start=True, stop=True)
                        mm.then_inc(made[par], 1)

            @block.scalar
            def _(act):
                link = Chain(act, ast)
                act.wait_ge(loaded, 16 * 13)
                link(act.activation(small[0][:], temp[:], ACT.Abs))
                link(act.activation(small[1][:], small[0][:], ACT.Exp, scale=-1.0))
                link(act.activation(small[2][:], small[1][:], ACT.Ln, bias=1.0))
                link(act.activation(small[3][:], temp[:], ACT.Relu))
                with act.Fori(0, steps // 2) as i:
                    for par in range(2):
                        g = 2 * i + par
                        act.wait_ge(turned[par], ROOM + i)
                        for j in range(GROUP):
                            n = GROUP * g + j
                            act.activation(a[par][:, j, :], k["x"][:, n, :], ACT.Identity, bias=k["shift"][:, bass.ds(n, 1)],
                                           scale=k["rstd"][:, bass.ds(n, 1)]).then_inc(a_done, 1)
                        act.wait_ge(turned[par], ROOM + i + 1)
                        act.wait_ge(made[par], ROOM + i)
                        act.activation(a_t[par][:], p_t[par][:, :].rearrange("p (j q) -> p j q", j=GROUP),
                                       ACT.Identity).then_inc(copied[par], 1)
                act.wait_ge(ss_done, 1)
                link(act.activation(length[:], ss[:], ACT.Sqrt))
                act.wait_ge(kept, ROOM + 4 * steps)
                link(act.activation(charge[:], feat[:, :, SHELL], ACT.Tanh))
                act.wait_ge(arg_done, 1)
                link(act.activation(phases[:], arg[:], ACT.Sin))

            @block.vector
            def _(dve):
                link = Chain(dve, step)
                dve.wait_ge(product, 2)
                link(dve.tensor_copy(w_all[:, SHELL + 1:FEAT], p_w[:, 0:RFF]))
                link(dve.tensor_copy(b_all[:, SHELL + 1:FEAT], p_w[:, RFF:2 * RFF]))
                dve.wait_ge(ast, 4)
                link(dve.tensor_tensor(small[4][:], small[2][:], small[3][:], ALU.add))
                link(dve.tensor_scalar(small[4][:], small[4][:], 0.1, None, ALU.add))
                link(dve.reciprocal(small[5][:], small[4][:]))
                link(dve.tensor_scalar(decay[:], decay[:], small[5][:, 0:1], None, ALU.mult))
                with dve.Fori(0, steps // 2) as i:
                    for par in range(2):
                        g = 2 * i + par
                        dve.wait_ge(made[par], ROOM + i + 1)
                        for half in range(2):
                            part = bass.ds(GROUP * g + 2 * half, 2)
                            src = p_f[par][half][:, :].rearrange("p (t w) -> p t w", t=2)
                            dve.tensor_tensor(feat[:, part, :], src[:, :, 0:FEAT],
                                              b_all[:, None, 0:FEAT].broadcast_to([P, 2, FEAT]), ALU.add).then_inc(kept, 1)
                            dve.tensor_tensor(values[:, part, :], src[:, :, FEAT:W],
                                              b_all[:, None, FEAT:W].broadcast_to([P, 2, D]), ALU.add).then_inc(kept, 1)
                dve.wait_ge(kept, ROOM + 4 * steps)
                shell = feat[:, :, 0:SHELL]
                link(dve.tensor_tensor(sq[:], shell, shell, ALU.mult))
                dve.tensor_reduce(ss[:], sq[:], AX.X, ALU.add).then_inc(ss_done, 1)
                dve.wait_ge(ast, 5)
                link(dve.tensor_scalar(length[:], length[:], 1e-12, None, ALU.max))
                link(dve.reciprocal(ss[:], length[:]))
                link(dve.tensor_tensor(proj[:], feat[:, :, SHELL + 1:FEAT], ss[:, :, None].broadcast_to([P, TILES, RFF]), ALU.mult))
                link(dve.tensor_tensor(proj[:], proj[:], b_rff[:, None, :].broadcast_to([P, TILES, RFF]), ALU.add))
                for half, quarter in ((0, 0.25), (1, 0.0)):
                    to = arg[:, :, half, :]
                    link(dve.tensor_scalar(turns[:], proj[:], 1.0 / (2 * math.pi), quarter, ALU.mult, ALU.add))
                    link(dve.tensor_scalar(turns[:], turns[:], ROUND, ROUND, ALU.add, ALU.subtract))
                    link(dve.scalar_tensor_tensor(to, turns[:], -TWO_PI[0], proj[:], ALU.mult, ALU.add))
                    link(dve.scalar_tensor_tensor(to, turns[:], -TWO_PI[1], to, ALU.mult, ALU.add))
                    link(dve.scalar_tensor_tensor(to, turns[:], -TWO_PI[2], to, ALU.mult, ALU.add))
                    if half == 0:
                        link(dve.tensor_scalar(to, to, math.pi / 2, None, ALU.add))
                    ins = dve.tensor_scalar(to, to, -PI, PI, ALU.max, ALU.min)
                    if half == 0:
                        link(ins)
                    else:
                        ins.then_inc(arg_done, 1)
                dve.wait_ge(ast, 6)
                link(dve.memset(powers[:, :, 0], 1.0))
                for m in range(1, NM):
                    link(dve.tensor_tensor(powers[:, :, m], powers[:, :, m - 1], charge[:], ALU.mult))
                link(dve.tensor_tensor(powers[:], powers[:], c_mag[:, None, :].broadcast_to([P, TILES, NM]), ALU.mult))


def attend(nc, d, k, sem, values, phases, powers, decay):
    KC = 3
    with ExitStack() as ctx:
        def sb(name, shape, dt=F32):
            return ctx.enter_context(nc.sbuf_tensor(f"{name}_at", shape, dt))

        def ps(name):
            return ctx.enter_context(nc.psum_tensor(f"{name}_at", [P, 512], F32))

        w_comb = sb("w_comb", [P, KC, P])
        w_out = sb("w_out", [P, D])
        b_out = sb("b_out", [P, D])
        bar = sb("bar", [P, P], BF16)
        ident_b = sb("ident_b", [P, P], BF16)
        tp = [sb(f"tp{i}", [P, PER, KC * P]) for i in range(2)]
        tp_t = [sb(f"tp_t{i}", [P, KC, T]) for i in range(2)]
        phi_t = [sb(f"phi_t{i}", [P, T]) for i in range(2)]
        v = [sb(f"v{i}", [P, PER, D]) for i in range(2)]
        logit = [sb(f"logit{i}", [P, 384]) for i in range(2)]
        prob = [sb(f"prob{i}", [P, 384]) for i in range(2)]
        prob_t = [sb(f"prob_t{i}", [P, 384]) for i in range(2)]
        o_t = [sb(f"o_t{i}", [P, T]) for i in range(2)]
        top = [sb(f"top{i}", [P, PER]) for i in range(2)]
        ntop = [sb(f"ntop{i}", [P, PER]) for i in range(2)]
        mass = [sb(f"mass{i}", [P, PER]) for i in range(2)]
        rmass = [sb(f"rmass{i}", [P, PER]) for i in range(2)]
        p_tp = [ps(f"p_tp{i}") for i in range(2)]
        p_phi = ps("p_phi")
        p_s = [ps(f"p_s{i}") for i in range(2)]
        p_pt = ps("p_pt")
        p_o = ps("p_o")
        p_y = ps("p_y")

        loaded = sem("at_loaded")
        padded = sem("at_padded")
        tp_done = sem("at_tp_done")
        v_done = sem("at_v_done")
        tpt_done = sem("at_tp_turned")
        tpt_copied = sem("at_tp_copied")
        phi_done = sem("at_phi_done")
        phi_copied = sem("at_phi_copied")
        s_done = sem("at_scores_done")
        l_done = sem("at_logits_done")
        n_done = sem("at_ntop_done")
        e_done = sem("at_exp_done")
        pt_done = sem("at_prob_turned")
        pt_copied = sem("at_prob_copied")
        o_done = sem("at_o_done")
        o_copied = sem("at_o_copied")
        y_done = sem("at_y_done")
        r_done = sem("at_mass_inverted")
        xb_done = sem("at_bias_added")
        x_done = sem("at_x_added")
        passed = sem("at_passed")
        measured = sem("at_x_measured")

        def plan(eng, turn):
            with eng.Fori(0, (B - 2) // 2) as i:
                for par in range(2):
                    turn(2 * i + par, par, True)
            turn(B - 2, 0, True)
            turn(B - 1, 1, False)

        def at(n, count=1):
            return slice(n, n + count) if isinstance(n, int) else bass.ds(n, count)

        with nc.Block() as block:
            @block.sync
            def _(sp):
                for counter in (tpt_copied, phi_copied, pt_copied, o_copied):
                    sp.sem_inc(counter, ROOM)
                for counter in (tpt_done, l_done, x_done, pt_done, y_done, s_done):
                    sp.sem_inc(counter, 2 * PER)
                sp.sem_inc(o_done, 2)
                for dst, src in ((w_comb[:], d["w_comb_pad"]), (w_out[:], d["w_out_t"]),
                                 (b_out[:], d["L0_attn_b_b_out"].rearrange("(a b) -> a b", a=1).broadcast_to([P, D])),
                                 (bar[:], d["c_bar"]), (ident_b[:], d["c_ident_b"])):
                    sp.dma_start(dst, src).then_inc(loaded, 16)

            @block.gpsimd
            def _(pool):
                pool.wait_ge(loaded, 80)
                for par in range(2):
                    pool.memset(tp[par][:, :, NM * 2 * RFF:KC * P], 0.0).then_inc(padded, 1)
                pool.wait_ge(padded, 2)

                def turn(g, par, more):
                    pool.wait_ge(tpt_done, PER * (g + 1))
                    for t in range(PER):
                        tile = at(PER * g + t)
                        pool.tensor_tensor(tp[par][:, t, 0:NM * 2 * RFF].rearrange("p (m f) -> p m f", m=NM),
                                           phases[:, tile, :, :].rearrange("p a b c -> p a (b c)").broadcast_to([P, NM, 2 * RFF]),
                                           powers[:, tile, :].rearrange("p a m -> p m a").broadcast_to([P, NM, 2 * RFF]),
                                           ALU.mult).then_inc(tp_done, 1)
                    pool.wait_ge(o_done, g + 1)
                    pool.tensor_copy(v[par][:], values[:, at(PER * g, PER), :]).then_inc(v_done, 1)
                    pool.tensor_tensor(k["x"][:, at(PER * g, PER), :], k["x"][:, at(PER * g, PER), :],
                                       b_out[:, None, :].broadcast_to([P, PER, D]), ALU.add).then_inc(xb_done, 1)

                plan(pool, turn)

            @block.tensor
            def _(pe):
                pe.wait_ge(loaded, 80)

                def turn_products(g, par):
                    for t in range(PER):
                        pe.wait_ge(tp_done, PER * g + t + 1)
                        pe.wait_ge(tpt_copied, ROOM + PER * g)
                        for c in range(KC):
                            mm = pe.transpose(p_tp[t][:, c * P:(c + 1) * P], tp[par][:, t, c * P:(c + 1) * P], k["ident"][:])
                        mm.then_inc(tpt_done, 1)

                def combine(g, par):
                    pe.wait_ge(tpt_copied, ROOM + PER * g + PER)
                    pe.wait_ge(phi_copied, ROOM + g)
                    for c in range(KC):
                        mm = pe.matmul(p_phi[:, 0:T], w_comb[:, c, :], tp_t[par][:, c, :], start=(c == 0), stop=(c == KC - 1))
                    mm.then_inc(phi_done, 1)

                def scores(g, par):
                    pe.wait_ge(phi_copied, ROOM + g + 1)
                    pe.wait_ge(l_done, 2 * g + 2)
                    pe.matmul(p_s[par][:, 0:P], phi_t[par][:, 0:P], phi_t[par][:, 0:P], start=True, stop=False)
                    pe.matmul(p_s[par][:, 0:P], ident_b[:], bar[:], start=False, stop=True)
                    pe.matmul(p_s[par][:, P:2 * P], phi_t[par][:, P:T], phi_t[par][:, 0:P], start=True, stop=True)
                    pe.matmul(p_s[par][:, 2 * P:3 * P], phi_t[par][:, P:T], phi_t[par][:, P:T], start=True, stop=False)
                    pe.matmul(p_s[par][:, 2 * P:3 * P], ident_b[:], bar[:], start=False, stop=True).then_inc(s_done, 1)

                def turn_probs(g, par):
                    pe.wait_ge(e_done, 2 * g + 2)
                    pe.wait_ge(pt_copied, ROOM + g)
                    for c in range(3):
                        mm = pe.transpose(p_pt[:, c * P:(c + 1) * P], prob[par][:, c * P:(c + 1) * P], k["ident"][:])
                    mm.then_inc(pt_done, 1)

                def mix(g, par):
                    pe.wait_ge(pt_copied, ROOM + g + 1)
                    pe.wait_ge(v_done, g + 1)
                    pe.wait_ge(o_copied, ROOM + g)
                    pe.matmul(p_o[:, 0:T], v[par][:, 0, :], prob_t[par][:, 0:T], start=True, stop=False)
                    pe.matmul(p_o[:, P:T], v[par][:, 1, :], prob_t[par][:, T:384], start=False, stop=True).then_inc(o_done, 1)

                def output(g, par):
                    pe.wait_ge(o_copied, ROOM + g + 1)
                    pe.wait_ge(x_done, 2 * PER + 2 * g)
                    for t in range(PER):
                        mm = pe.matmul(p_y[:, t * D:(t + 1) * D], o_t[par][:, t * P:(t + 1) * P], w_out[:], start=True, stop=True)
                    mm.then_inc(y_done, 1)

                turn_products(0, 0)
                combine(0, 0)
                scores(0, 0)

                def turn(g, par, more):
                    if more:
                        turn_products(g + 1, 1 - par)
                    turn_probs(g, par)
                    if more:
                        combine(g + 1, 1 - par)
                    mix(g, par)
                    if more:
                        scores(g + 1, 1 - par)
                    output(g, par)

                plan(pe, turn)

            @block.scalar
            def _(act):
                def copy_products(g, par):
                    for t in range(PER):
                        act.wait_ge(tpt_done, PER * (g + 2) + t + 1)
                        act.activation(tp_t[par][:, :, t * P:(t + 1) * P], p_tp[t][:, 0:KC * P].rearrange("p (c q) -> p c q", c=KC),
                                       ACT.Identity).then_inc(tpt_copied, 1)

                def copy_phi(g, par):
                    act.wait_ge(phi_done, g + 1)
                    act.wait_ge(s_done, 2 * PER - 2 + g + 1)
                    act.activation(phi_t[par][:], p_phi[:, 0:T], ACT.Identity).then_inc(phi_copied, 1)

                def exponentials(g, par):
                    act.wait_ge(n_done, g + 1)
                    act.wait_ge(pt_done, 2 * PER - 2 + g + 1)
                    for t in range(PER):
                        cols = slice(0, P) if t == 0 else slice(P, 384)
                        act.activation(prob[par][:, cols], logit[par][:, cols], ACT.Exp, bias=ntop[par][:, t:t + 1],
                                       accum_out=mass[par][:, t:t + 1]).then_inc(e_done, 1)

                def copy_o(g, par):
                    act.wait_ge(o_done, g + 3)
                    act.wait_ge(y_done, 2 * PER - 2 + g + 1)
                    act.activation(o_t[par][:], p_o[:, 0:T], ACT.Identity).then_inc(o_copied, 1)

                copy_products(0, 0)
                copy_phi(0, 0)
                exponentials(0, 0)

                def turn(g, par, more):
                    if more:
                        copy_products(g + 1, 1 - par)
                        copy_phi(g + 1, 1 - par)
                    copy_o(g, par)
                    if more:
                        exponentials(g + 1, 1 - par)

                plan(act, turn)

            @block.vector
            def _(dve):
                def logits(g, par):
                    wait_apart(dve, s_done, 2 * PER + g + 1, passed)
                    dve.tensor_tensor_reduce(logit[par][:, 0:P], p_s[par][:, 0:P], decay[:, P:T], 1.0, -3.0e38,
                                             ALU.mult, ALU.max, top[par][:, 0:1]).then_inc(l_done, 1)
                    dve.tensor_tensor_reduce(logit[par][:, P:384], p_s[par][:, P:384], decay[:], 1.0, -3.0e38,
                                             ALU.mult, ALU.max, top[par][:, 1:2]).then_inc(l_done, 1)
                    dve.wait_ge(l_done, 2 * PER + 2 * g + 2)
                    dve.tensor_scalar(ntop[par][:], top[par][:], -1.0, None, ALU.mult).then_inc(n_done, 1)

                def copy_probs(g, par):
                    dve.wait_ge(pt_done, 2 * PER + g + 1)
                    dve.tensor_copy(prob_t[par][:], p_pt[:, 0:384]).then_inc(pt_copied, 1)

                def add(g, par):
                    dve.wait_ge(e_done, 2 * g + 2)
                    dve.reciprocal(rmass[par][:], mass[par][:]).then_inc(r_done, 1)
                    dve.wait_ge(y_done, 2 * PER + g + 1)
                    dve.wait_ge(r_done, g + 1)
                    dve.wait_ge(xb_done, g + 1)
                    for t in range(PER):
                        xs = k["x"][:, at(PER * g + t), :].rearrange("p a e -> p (a e)")
                        dve.scalar_tensor_tensor(xs, p_y[:, t * D:(t + 1) * D], rmass[par][:, t:t + 1], xs,
                                                 ALU.mult, ALU.add).then_inc(x_done, 1)
                    for t in range(PER):
                        dve.wait_ge(x_done, 2 * PER + 2 * g + t + 1)
                        dve.bn_stats(k["halves"][:, at(PER * g + t), :].rearrange("p a s -> p (a s)"),
                                     k["x"][:, at(PER * g + t), :].rearrange("p a e -> p (a e)")).then_inc(measured, 1)

                logits(0, 0)

                def turn(g, par, more):
                    copy_probs(g, par)
                    if more:
                        logits(g + 1, 1 - par)
                    add(g, par)

                plan(dve, turn)


def _layouts(i):
    import numpy as np

    out = {}
    ws = [np.asarray(i[n]).T for n in ("L0_attn_a_Wq", "L0_attn_a_Wq2", "L0_attn_a_Wk", "L0_attn_a_Wk2")]
    out["w_qk"] = np.stack(ws, 1)
    out["w_v_t"] = np.asarray(i["L0_attn_a_Wv"]).T
    proj_t = np.asarray(i["L0_attn_a_Wproj"]).T.reshape(4, 4, DH, D)
    pad = np.zeros((4, 32, 4, D), np.float32)
    pad[:, :DH] = proj_t.transpose(1, 2, 0, 3)
    out["w_proj_pad"] = pad.reshape(P, 4, D)
    out["centroids_t"] = np.asarray(i["L0_ffn_centroids"]).T
    out["w_shell_t"] = np.asarray(i["L0_attn_b_W_shell"]).T
    out["w_charge_t"] = np.asarray(i["L0_attn_b_W_charge"]).T
    out["w_vb_t"] = np.asarray(i["L0_attn_b_W_v"]).T
    out["w_out_t"] = np.asarray(i["L0_attn_b_W_out"]).T
    out["omega_t"] = np.asarray(i["L0_attn_b_omega"]).T
    out["b_shell_wide"] = np.repeat(np.asarray(i["L0_attn_b_b_shell"])[:, None], P, 1)
    comb = np.zeros((3 * P, P), np.float32)
    comb[:NM * 2 * RFF, :64] = np.asarray(i["L0_attn_b_W_combine"]).T
    out["w_comb_pad"] = comb.reshape(3, P, P).transpose(1, 0, 2)
    return {n: np.ascontiguousarray(a) for n, a in out.items()}


def _constants():
    import numpy as np
    bfloat16 = mybir.dt.np(BF16)
    c = {"c_ident": np.eye(P, dtype=np.float32)}
    inv = 1.0 / 10000.0 ** (np.arange(0, DH, 2, dtype=np.float32) / np.float32(DH))
    freqs = np.outer(np.arange(T, dtype=np.float32), inv.astype(np.float32)).astype(np.float32)
    cos, sin = (f(freqs).astype(np.float32).reshape(PER, P, DH // 2).transpose(1, 0, 2) for f in (np.cos, np.sin))
    c["c_rope"] = np.stack([np.concatenate([cos, cos], -1), np.concatenate([-sin, sin], -1)], 2)
    c["c_causal"] = (np.arange(P)[:, None] <= np.arange(P)[None, :]).astype(np.float32)
    keys = (np.arange(1, CANDS + 1, dtype=np.uint64) << 28).astype(np.uint32)
    bits = np.where(keys >> 31, keys ^ np.uint32(1 << 31), ~keys)
    c["c_first_cand"] = np.tile(bits.view(np.float32), (P, 1))
    shifts = 28 - 4 * np.arange(PASSES)
    dig = np.stack([(np.arange(1, CANDS + 1, dtype=np.uint64) << int(s)).astype(np.uint32) for s in shifts])
    c["c_digits"] = np.tile(dig, (P, 1, 1))
    c["c_weight"] = np.tile((2.0 ** shifts).astype(np.float32), (P, 1))
    p = np.arange(P)
    c["c_before"] = ((p[:, None] < p[None, :]) - 1.0).astype(bfloat16)
    c["c_lanes"] = np.tile(p.astype(bfloat16), (P, 1))
    place = np.zeros((P, TILES, 2, SLOTS), np.float32)
    place[:, :, 0, :] = np.arange(TILES)[None, :, None]
    place[:, :, 1, :] = p[:, None, None]
    c["c_place"] = place.astype(bfloat16)
    c["c_eighth"] = np.tile(np.arange(SLOTS).astype(bfloat16), (P, 2, 1))
    q, m = np.arange(P)[:, None], np.arange(T)[None, :]
    c["c_decay"] = np.exp(np.float32(-0.3) * np.abs(q + P - m).astype(np.float32) / np.float32(10.0)).astype(np.float32)
    c["c_bar"] = np.where(p[:, None] < p[None, :], -1e30, 0.0).astype(bfloat16)
    c["c_ident_b"] = np.eye(P).astype(bfloat16)
    scale = math.sqrt(2.0 / (2 * RFF)) * math.sqrt(math.exp(-0.5))
    mags = [math.sqrt(1.0 / math.factorial(m) + 1e-10) * scale for m in range(NM)]
    c["c_mag"] = np.tile(np.array(mags, np.float32), (P, 1))
    return c


_DIRECT = ["L0_attn_a_x", "L0_attn_b_b_charge", "L0_attn_b_W_shell", "L0_attn_b_b_shell", "L0_attn_b_rff_bias",
           "L0_attn_b_b_v", "L0_attn_b_b_out", "L0_ffn_ln_g", "L0_ffn_ln_b", "L0_ffn_w1", "L0_ffn_b1", "L0_ffn_w2",
           "L0_ffn_b2"]


def kernel(**inputs):
    import numpy as _np
    import concourse.bacc as _bacc
    from concourse import mybir as _mybir
    from concourse.bass_utils import run_bass_kernel_spmd as _run

    nc = _bacc.Bacc("TRN2", target_bir_lowering=False, num_devices=1)
    arrays = {n: _np.ascontiguousarray(inputs[n]) for n in _DIRECT}
    arrays["L0_attn_b_log_temp"] = _np.asarray(inputs["L0_attn_b_log_temp"]).reshape(1, 1)
    arrays.update(_layouts(inputs))
    arrays.update({n: _np.ascontiguousarray(a) for n, a in _constants().items()})
    handles = {n: nc.dram_tensor(n, a.shape, _mybir.dt.from_np(a.dtype), kind="ExternalInput").ap() for n, a in arrays.items()}
    handles["out"] = nc.dram_tensor("out", (B, T, D), F32, kind="ExternalOutput").ap()
    build(nc, handles)
    r = _run(nc, [arrays], core_ids=[0])
    return r.results[0]["out"]
```

```python
import math
from contextlib import ExitStack

import concourse.bass as bass
from concourse import mybir

F32 = mybir.dt.float32
BF16 = mybir.dt.bfloat16
I32 = mybir.dt.int32
U32 = mybir.dt.uint32
ALU = mybir.AluOpType
ACT = mybir.ActivationFunctionType
AX = mybir.AxisListType

P = 128
D = 128
B, T = 32, 256
TOKENS = B * T
TILES = TOKENS // P
PER = T // P
H = 16
DH = D // H
E = 8
CAP = TOKENS // E
F = 512
FC = F // P
SLOTS = CAP // P
SHELL, RFF, ORDER = 64, 32, 4
NM = ORDER + 1
FEAT = SHELL + 1 + RFF
EPS = 1e-5
GROUP = 4
PASSES = 8
CANDS = 15
TAKEN = -1.5e38
ROUND = 1.5 * 2.0**23
TWO_PI = (6.28125, 0.0019350051879882812, 3.0199159819567e-07)
PI = 3.1415925
ROOM = 1


def wait_apart(eng, semaphore, value, passed):
    eng.wait_ge(semaphore, value)
    eng.sem_inc(passed, 1)


class Chain:

    def __init__(self, eng, sem):
        self.eng, self.sem, self.n = eng, sem, 0

    def __call__(self, ins):
        self.n += 1
        ins.then_inc(self.sem, 1)
        self.eng.wait_ge(self.sem, self.n)


def phase(nc, body, *args):
    used = []

    def sem(name):
        used.append(nc.alloc_semaphore(name))
        return used[-1]

    body(nc, sem, *args)
    nc.clear_and_free_semaphores(used)
    nc.all_engine_barrier()


def build(nc, d):
    with ExitStack() as whole:
        def keep(name, shape, dt=F32):
            return whole.enter_context(nc.sbuf_tensor(name, shape, dt))

        k = {
            "x": keep("x", [P, TILES, D]),
            "ident": keep("ident", [P, P]),
            "rstd": keep("rstd", [P, TILES]),
            "shift": keep("shift", [P, TILES]),
            "halves": keep("halves", [P, TILES, 6]),
            "scores": keep("scores", [P, E, TILES]),
        }
        norm_rows = nc.dram_tensor("norm_rows", (TOKENS, D), F32, kind="Internal").ap()
        ffn_rows = nc.dram_tensor("ffn_rows", (TOKENS, D), F32, kind="Internal").ap()
        phase(nc, load_x, d, k)
        phase(nc, statistics, k, "a")
        phase(nc, attention_a, d, k)
        phase(nc, normalise_for_experts, d, k, norm_rows, 0)
        phase(nc, experts, d, k, norm_rows, ffn_rows, 0)
        phase(nc, add_rows, k, ffn_rows, None, 0)
        phase(nc, statistics, k, "b")
        phase(nc, attention_b, d, k)
        phase(nc, normalise_for_experts, d, k, norm_rows, 1)
        phase(nc, experts, d, k, norm_rows, ffn_rows, 1)
        phase(nc, add_rows, k, ffn_rows, d["out"], 1)


def load_x(nc, sem, d, k):
    loads = 4
    loaded = [sem(f"x_loaded{q}") for q in range(loads)]
    ident_loaded = sem("ident_loaded")
    measured = sem("x_measured")
    x_dram = d["L0_attn_a_x"].rearrange("b (t p) d -> p (b t) d", p=P)
    with nc.Block() as block:
        @block.sync
        def _(sp):
            for q in range(loads):
                part = slice(q * TILES // loads, (q + 1) * TILES // loads)
                sp.dma_start(k["x"][:, part, :], x_dram[:, part, :]).then_inc(loaded[q], 16)
            sp.dma_start(k["ident"][:], d["c_ident"]).then_inc(ident_loaded, 16)
            sp.wait_ge(ident_loaded, 16)

        @block.vector
        def _(dve):
            for q in range(loads):
                dve.wait_ge(loaded[q], 16)
                for n in range(q * TILES // loads, (q + 1) * TILES // loads):
                    dve.bn_stats(k["halves"][:, n, :], k["x"][:, n, :]).then_inc(measured, 1)


def statistics(nc, sem, k, tag, twice=False):
    with ExitStack() as ctx:
        def sb(name, shape, dt=F32):
            return ctx.enter_context(nc.sbuf_tensor(f"{name}_{tag}", shape, dt))

        halves = k["halves"]
        moment = sb("moment", [P, TILES])
        gap = sb("gap", [P, TILES])
        gap2 = sb("gap2", [P, TILES])
        var = sb("var", [P, TILES])
        std = sb("std", [P, TILES])
        msum = sb("msum", [P, TILES])
        eps = sb("eps", [P, 1])
        step = sem(f"stat_step_{tag}")
        var_done = sem(f"var_done_{tag}")
        std_done = sem(f"std_done_{tag}")
        with nc.Block() as block:
            @block.vector
            def _(dve):
                link = Chain(dve, step)
                link(dve.memset(eps[:], EPS))
                link(dve.tensor_tensor(moment[:], halves[:, :, 2], halves[:, :, 5], ALU.add))
                link(dve.tensor_tensor(gap[:], halves[:, :, 1], halves[:, :, 4], ALU.subtract))
                link(dve.tensor_tensor(msum[:], halves[:, :, 1], halves[:, :, 4], ALU.add))
                link(dve.tensor_tensor(gap2[:], gap[:], gap[:], ALU.mult))
                dve.scalar_tensor_tensor(var[:], gap2[:], D / 4.0, moment[:], ALU.mult, ALU.add).then_inc(var_done, 1)
                dve.wait_ge(std_done, 1)
                link(dve.reciprocal(k["rstd"][:], std[:]))
                link(dve.scalar_tensor_tensor(k["shift"][:], msum[:], -0.5, k["rstd"][:], ALU.mult, ALU.mult))
                if twice:
                    link(dve.tensor_tensor(gap[:], var[:], k["rstd"][:], ALU.mult))
                    link(dve.tensor_tensor(var[:], gap[:], k["rstd"][:], ALU.mult))
                    dve.tensor_scalar(k["rstd_1"][:], k["rstd"][:], 1.0, None, ALU.add).then_inc(var_done, 1)
                    dve.wait_ge(std_done, 2)
                    link(dve.reciprocal(gap2[:], std[:]))
                    link(dve.tensor_tensor(k["rstd_2"][:], k["rstd"][:], gap2[:], ALU.mult))
                    link(dve.tensor_tensor(k["shift_2"][:], k["shift"][:], gap2[:], ALU.mult))

            @block.scalar
            def _(act):
                act.wait_ge(step, 1)
                for n in range(2 if twice else 1):
                    act.wait_ge(var_done, n + 1)
                    if n:
                        act.wait_ge(step, 9)
                    act.activation(std[:], var[:], ACT.Sqrt, bias=eps[:], scale=1.0 / D).then_inc(std_done, 1)


def attention_a(nc, sem, d, k):
    QUADS = H // 4
    PAIRS = H // 2
    FH = DH * DH
    with ExitStack() as ctx:
        def sb(name, shape, dt=F32):
            return ctx.enter_context(nc.sbuf_tensor(f"{name}_aa", shape, dt))

        def ps(name):
            return ctx.enter_context(nc.psum_tensor(f"{name}_aa", [P, 512], F32))

        w_qk = sb("w_qk", [P, 4, D])
        w_v = sb("w_v", [P, D])
        w_proj = sb("w_proj", [P, D])
        rope = sb("rope", [P, PER, 2, DH])
        causal = sb("causal", [P, P])
        xn = sb("xn", [P, PER, D])
        xn_t = sb("xn_t", [P, T])
        straight = sb("straight", [P, PER, 4 * H, 2, DH // 2])
        crossed = sb("crossed", [P, PER, 4 * H, 2, DH // 2])
        roped = sb("roped", [P, PER, 4, H, DH])
        feat_q = sb("feat_q", [P, PER, H, DH, DH])
        feat_k = sb("feat_k", [P, PER, H, DH, DH])
        q_t = [sb(f"q_t{i}", [P, H, T]) for i in range(2)]
        k_t = [sb(f"k_t{i}", [P, PAIRS, T]) for i in range(2)]
        v = [sb(f"v{i}", [P, PER, QUADS * (4 * 32 + DH)]) for i in range(2)]
        kv = sb("kv", [P, H, 32])
        patt = [sb(f"patt{i}", [P, 4, P]) for i in range(4)]
        z_t = sb("z_t", [P, T])
        p_turn = [ps(f"p_turn{i}") for i in range(2)]
        p_patt = [ps(f"p_patt{i}") for i in range(2)]
        p_misc = ps("p_misc")
        p_kv = ps("p_kv")
        p_z = [ps(f"p_z{i}") for i in range(PER)]

        weights = sem("aa_weights_loaded")
        cleared = sem("aa_cleared")
        cleared_odd = sem("aa_cleared_odd")
        xn_done = sem("aa_xn_done")
        xt_done = sem("aa_xt_done")
        xt_copied = sem("aa_xt_copied")
        v_done = sem("aa_v_done")
        v_copied = sem("aa_v_copied")
        proj_done = sem("aa_projections_done")
        terms_done = sem("aa_rotation_terms_done")
        roped_done = sem("aa_roped_done")
        feat_q_done = sem("aa_query_features_done")
        feat_k_done = sem("aa_key_features_done")
        feat_turned = sem("aa_features_turned")
        feat_copied = sem("aa_features_copied")
        kv_done = sem("aa_kv_done")
        kv_copied = sem("aa_kv_copied")
        p_done = sem("aa_pattern_done")
        masked = sem("aa_masked")
        z_done = sem("aa_z_done")
        z_copied = sem("aa_z_copied")
        y_done = sem("aa_y_done")
        x_added = sem("aa_x_added")
        measured = sem("aa_x_measured")

        TURNS = [("k", 0, 0), ("k", 0, 1), ("q", 0, 0), ("q", 0, 1), ("k", 1, 0), ("k", 1, 1), ("q", 1, 0), ("q", 1, 1)]
        NT = len(TURNS)
        U = QUADS * PER

        def plan(eng, turn):
            with eng.Fori(0, (B - 2) // 2) as i:
                for par in range(2):
                    turn(2 * i + par, par, True, True)
            turn(B - 2, 0, True, False)
            turn(B - 1, 1, False, False)

        def at(n, count=1):
            return slice(n, n + count) if isinstance(n, int) else bass.ds(n, count)

        with nc.Block() as block:
            @block.sync
            def _(sp):
                for counter in (xt_done, xt_copied, kv_done, y_done, z_copied, feat_copied, v_done):
                    sp.sem_inc(counter, ROOM)
                sp.sem_inc(z_done, 4)
                sp.sem_inc(masked, 2)
                sp.sem_inc(x_added, 2)
                sp.dma_start(w_qk[:], d["w_qk"]).then_inc(weights, 16)
                sp.dma_start(w_v[:], d["w_v_t"]).then_inc(weights, 16)
                sp.dma_start(w_proj[:], d["w_proj_t"]).then_inc(weights, 16)
                sp.dma_start(rope[:], d["c_rope"]).then_inc(weights, 16)
                sp.dma_start(causal[:], d["c_causal"]).then_inc(weights, 16)

            @block.gpsimd
            def _(pool):
                for t in (v[0], v[1], q_t[0]):
                    pool.memset(t[:], 0.0).then_inc(cleared, 1)

                def prepare(g):
                    for t in range(PER):
                        pool.wait_ge(terms_done, 2 * PER * g + 2 * t + 2)
                        if not isinstance(g, int) or g > 0:
                            pool.wait_ge(feat_q_done, PER * g)
                            pool.wait_ge(feat_k_done, PER * g)
                        r = roped[:, t, :, :, :].rearrange("p s h (a e) -> p (s h) a e", a=2)
                        for half in range(2):
                            pool.tensor_tensor(r[:, :, half, :], straight[:, t, :, half, :], crossed[:, t, :, 1 - half, :],
                                               ALU.add).then_inc(roped_done, 1)
                        pool.wait_ge(roped_done, 2 * PER * g + 2 * t + 2)
                        if not isinstance(g, int) or g > 0:
                            pool.wait_ge(feat_turned, NT * g)
                            pool.wait_ge(kv_done, ROOM + g)
                        pool.tensor_tensor(feat_k[:, t, :, :, :], roped[:, t, 2, :, :, None].broadcast_to([P, H, DH, DH]),
                                           roped[:, t, 3, :, None, :].broadcast_to([P, H, DH, DH]), ALU.mult).then_inc(feat_k_done, 1)

                prepare(0)

                def turn(g, par, more, more2):
                    if more:
                        prepare(g + 1)

                plan(pool, turn)

            @block.scalar
            def _(act):
                def normalise(g):
                    act.wait_ge(xt_done, ROOM + g)
                    for t in range(PER):
                        n = PER * g + t
                        act.activation(xn[:, t, :], k["x"][:, at(n), :].rearrange("p a e -> p (a e)"), ACT.Identity,
                                       bias=k["shift"][:, at(n)], scale=k["rstd"][:, at(n)]).then_inc(xn_done, 1)

                def copy_xt(g):
                    act.wait_ge(xt_done, ROOM + g + 1)
                    act.wait_ge(v_done, ROOM + g)
                    act.activation(xn_t[:], p_misc[:, 0:T], ACT.Identity).then_inc(xt_copied, 1)

                def copy_v(g, par):
                    act.wait_ge(v_done, ROOM + g + 1)
                    for t in range(PER):
                        spread = v[par][:, t, :].rearrange("p (q r) -> p q r", q=QUADS)[:, :, 0:4 * 32]
                        act.activation(spread.rearrange("p q (c w) -> p q c w", c=4)[:, :, :, 0:DH],
                                       p_misc[:, T + t * P:T + (t + 1) * P].rearrange("p (q c e) -> p q c e", q=QUADS, e=DH),
                                       ACT.Identity).then_inc(v_copied, 1)

                def copy_feat(g, par, n):
                    side, t, half = TURNS[n]
                    act.wait_ge(feat_turned, NT * g + n + 1)
                    cols = slice(t * P, (t + 1) * P)
                    src = p_turn[n % 2][:, :].rearrange("p (m q) -> p m q", m=PAIRS // 2)
                    if side == "k":
                        act.activation(k_t[par][:, half * PAIRS // 2:(half + 1) * PAIRS // 2, cols], src, ACT.Identity).then_inc(feat_copied, 1)
                    else:
                        for odd in range(2):
                            rows = slice(odd * FH, (odd + 1) * FH)
                            heads = slice(half * H // 2 + odd, (half + 1) * H // 2, 2)
                            ins = act.activation(q_t[par][rows, heads, cols], src[rows], ACT.Identity)
                        ins.then_inc(feat_copied, 1)

                normalise(0)
                copy_xt(0)
                act.wait_ge(cleared, 2)
                copy_v(0, 0)
                act.wait_ge(cleared, 3)
                act.wait_ge(cleared_odd, 1)
                for n in range(NT):
                    copy_feat(0, 0, n)
                normalise(1)

                def turn(g, par, more, more2):
                    act.wait_ge(kv_done, ROOM + g + 1)
                    act.wait_ge(z_done, 4 + U * g)
                    act.activation(kv[:], p_kv[:, :].rearrange("p (h e) -> p h e", e=32), ACT.Identity).then_inc(kv_copied, 1)
                    if more:
                        copy_xt(g + 1)
                        copy_v(g + 1, 1 - par)
                        for n in range(NT):
                            copy_feat(g + 1, 1 - par, n)
                    if more2:
                        normalise(g + 2)

                plan(act, turn)

            @block.vector
            def _(dve):
                dve.memset(q_t[1][:], 0.0).then_inc(cleared_odd, 1)
                dve.wait_ge(weights, 80)

                def rotate(g, t):
                    dve.wait_ge(proj_done, PER * g + t + 1)
                    if not isinstance(g, int) or g > 0:
                        dve.wait_ge(roped_done, 2 * PER * g)
                    src = p_turn[t][:, :].rearrange("p (s e) -> p s e", e=DH)
                    for n, dst in enumerate((straight, crossed)):
                        dve.tensor_tensor(dst[:, t, :, :, :].rearrange("p s a e -> p s (a e)"), src,
                                          rope[:, t, n, None, :].broadcast_to([P, 4 * H, DH]), ALU.mult).then_inc(terms_done, 1)

                def features(g, t):
                    dve.wait_ge(roped_done, 2 * PER * g + 2 * t + 2)
                    if not isinstance(g, int) or g > 0:
                        dve.wait_ge(feat_turned, NT * g)
                    dve.tensor_tensor(feat_q[:, t, :, :, :], roped[:, t, 0, :, :, None].broadcast_to([P, H, DH, DH]),
                                      roped[:, t, 1, :, None, :].broadcast_to([P, H, DH, DH]), ALU.mult).then_inc(feat_q_done, 1)

                def mask(g, u):
                    dve.wait_ge(p_done, U * g + u + 1)
                    dve.wait_ge(z_done, U * g + u + 1)
                    dve.tensor_tensor(patt[u % 4][:], p_patt[u % 2][:, :].rearrange("p (h q) -> p h q", q=P),
                                      causal[:, None, :].broadcast_to([P, 4, P]), ALU.mult).then_inc(masked, 1)

                rotate(0, 0)
                rotate(0, 1)
                features(0, 0)
                features(0, 1)

                def turn(g, par, more, more2):
                    mask(g, 0)
                    mask(g, 1)
                    if more:
                        rotate(g + 1, 0)
                        rotate(g + 1, 1)
                    mask(g, 2)
                    mask(g, 3)
                    if more:
                        features(g + 1, 0)
                    mask(g, 4)
                    mask(g, 5)
                    if more:
                        features(g + 1, 1)
                    mask(g, 6)
                    mask(g, 7)
                    dve.wait_ge(z_done, 4 + U * g + U)
                    dve.wait_ge(y_done, ROOM + g)
                    for t in range(PER):
                        dve.tensor_copy(z_t[:, t * P:(t + 1) * P], p_z[t][:, 0:P]).then_inc(z_copied, 1)
                    dve.wait_ge(y_done, ROOM + g + 1)
                    xs = k["x"][:, at(PER * g, PER), :]
                    dve.scalar_tensor_tensor(xs, p_misc[:, 0:T].rearrange("p (t e) -> p t e", t=PER), 1.0 / (DH * DH),
                                             xs, ALU.mult, ALU.add).then_inc(x_added, 1)
                    dve.wait_ge(x_added, g + 3)
                    for t in range(PER):
                        dve.bn_stats(k["halves"][:, at(PER * g + t), :].rearrange("p a s -> p (a s)"),
                                     k["x"][:, at(PER * g + t), :].rearrange("p a e -> p (a e)")).then_inc(measured, 1)

                plan(dve, turn)

            @block.tensor
            def _(pe):
                pe.wait_ge(weights, 80)

                def transposes(g):
                    pe.wait_ge(xn_done, PER * g + PER)
                    pe.wait_ge(x_added, g + 1)
                    for t in range(PER):
                        mm = pe.transpose(p_misc[:, t * P:(t + 1) * P], xn[:, t, :], k["ident"][:])
                    mm.then_inc(xt_done, 1)

                def projections(g):
                    pe.wait_ge(xt_copied, ROOM + g + 1)
                    for t in range(PER):
                        if not isinstance(g, int) or g > 0:
                            pe.wait_ge(feat_copied, ROOM + NT * g - PER + t + 1)
                        pe.matmul(p_turn[t][:], xn_t[:, t * P:(t + 1) * P], w_qk[:].rearrange("p s e -> p (s e)"),
                                  start=True, stop=True).then_inc(proj_done, 1)

                def values(g):
                    pe.wait_ge(xt_copied, ROOM + g + 1)
                    for t in range(PER):
                        mm = pe.matmul(p_misc[:, T + t * P:T + (t + 1) * P], xn_t[:, t * P:(t + 1) * P], w_v[:],
                                       start=True, stop=True)
                    mm.then_inc(v_done, 1)

                def turn_features(g, n):
                    side, t, half = TURNS[n]
                    if side == "k":
                        pe.wait_ge(feat_k_done, PER * g + t + 1)
                        src = feat_k
                    else:
                        pe.wait_ge(feat_q_done, PER * g + t + 1)
                        src = feat_q
                    if n < PER:
                        pe.wait_ge(terms_done, 2 * PER * g + 2 * n + 2)
                    else:
                        pe.wait_ge(feat_copied, ROOM + NT * g + n - 1)
                    flat = src[:, t, :, :, :].rearrange("p h i j -> p (h i j)")
                    for m in range(PAIRS // 2):
                        pair = half * PAIRS // 2 + m
                        mm = pe.transpose(p_turn[n % 2][:, m * P:(m + 1) * P], flat[:, pair * P:(pair + 1) * P], k["ident"][:])
                    mm.then_inc(feat_turned, 1)

                def keys_and_values(g, par):
                    pe.wait_ge(v_copied, PER * g + PER)
                    pe.wait_ge(feat_k_done, PER * g + PER)
                    flat = feat_k[:, 0, :, :, :].rearrange("p h i j -> p (h i j)")
                    if not isinstance(g, int) or g > 0:
                        pe.wait_ge(kv_copied, g)
                    for m in range(PAIRS):
                        mm = pe.matmul(p_kv[:, m * 64:(m + 1) * 64], flat[:, m * P:(m + 1) * P],
                                       v[par][:, 0, m * 64:(m + 1) * 64], start=True, stop=True)
                    mm.then_inc(kv_done, 1)

                def pattern(g, par, u):
                    quad, t = u // PER, u % PER
                    pe.wait_ge(masked, U * g + u + 1)
                    cols = slice(t * P, (t + 1) * P)
                    for m in range(2):
                        pair = 2 * quad + m
                        mm = pe.matmul(p_patt[u % 2][:, m * 2 * P:(m + 1) * 2 * P], k_t[par][:, pair, cols],
                                       q_t[par][:, 2 * pair:2 * pair + 2, cols], start=True, stop=True)
                    mm.then_inc(p_done, 1)

                def z(g, par, u):
                    quad, t = u // PER, u % PER
                    pe.wait_ge(masked, 2 + U * g + u + 1)
                    if u == 0:
                        pe.wait_ge(z_copied, ROOM + PER * g)
                    if u == 1:
                        pe.wait_ge(kv_copied, g + 1)
                    for c in range(4):
                        h = 4 * quad + c
                        out = p_z[t][32 * c:32 * c + 32, 0:P]
                        first, final = quad == 0, quad == QUADS - 1
                        mm = pe.matmul(out, v[par][:, t, 32 * h:32 * h + 32], patt[u % 4][:, c, :], start=first,
                                       stop=final and t == 0)
                        if t:
                            mm = pe.matmul(out, kv[:, h, :], q_t[par][:, h, P:T], start=False, stop=final)
                    mm.then_inc(z_done, 1)

                def output(g):
                    pe.wait_ge(z_copied, ROOM + PER * g + PER)
                    pe.wait_ge(v_copied, PER * min(g + 2, B) if isinstance(g, int) else PER * g + 2 * PER)
                    for t in range(PER):
                        mm = pe.matmul(p_misc[:, t * P:(t + 1) * P], z_t[:, t * P:(t + 1) * P], w_proj[:], start=True, stop=True)
                    mm.then_inc(y_done, 1)

                transposes(0)
                projections(0)
                values(0)
                for n in range(NT):
                    turn_features(0, n)

                def turn(g, par, more, more2):
                    keys_and_values(g, par)
                    pe.wait_ge(feat_copied, ROOM + NT * g + NT)
                    pattern(g, par, 0)
                    if more:
                        transposes(g + 1)
                    pattern(g, par, 1)
                    if more:
                        projections(g + 1)
                    z(g, par, 0)
                    pattern(g, par, 2)
                    if more:
                        values(g + 1)
                    z(g, par, 1)
                    pattern(g, par, 3)
                    z(g, par, 2)
                    for u in range(4, U):
                        pattern(g, par, u)
                        if more:
                            turn_features(g + 1, u - 4)
                        z(g, par, u - 1)
                    if more:
                        turn_features(g + 1, 4)
                    z(g, par, U - 1)
                    if more:
                        for n in range(5, NT):
                            turn_features(g + 1, n)
                    output(g)

                plan(pe, turn)


def normalise_for_experts(nc, sem, d, k, norm_rows, layer):
    tag = f"n{layer}"
    steps = TILES // GROUP
    NB = 4
    with ExitStack() as ctx:
        def sb(name, shape, dt=F32):
            return ctx.enter_context(nc.sbuf_tensor(f"{name}_{tag}", shape, dt))

        def ps(name):
            return ctx.enter_context(nc.psum_tensor(f"{name}_{tag}", [P, 512], F32))

        k = {**k, "rstd_1": sb("rstd_1", [P, TILES]), "rstd_2": sb("rstd_2", [P, TILES]), "shift_2": sb("shift_2", [P, TILES])}
        statistics(nc, sem, k, tag, twice=True)
        gain = sb("gain", [P, D])
        bias = sb("bias", [P, D])
        cent = sb("cent", [P, E])
        raw = [sb(f"raw{i}", [P, GROUP, D]) for i in range(2)]
        gained = [sb(f"gained{i}", [P, GROUP, D]) for i in range(2)]
        norm = [sb(f"norm{i}", [P, GROUP, D]) for i in range(NB)]
        norm_t = [sb(f"norm_t{i}", [P, GROUP, P]) for i in range(2)]
        p_t = [ps(f"p_t{i}") for i in range(2)]
        p_sc = ps("p_sc")
        loaded = sem(f"gb_loaded_{tag}")
        raw_done = sem(f"raw_done_{tag}")
        gained_done = sem(f"gained_done_{tag}")
        norm_done = sem(f"norm_done_{tag}")
        stored = [sem(f"norm_stored{i}_{tag}") for i in range(NB)]
        turned = sem(f"turned_{tag}")
        copied = sem(f"turned_copied_{tag}")
        scored = sem(f"scored_{tag}")
        kept = sem(f"scores_kept_{tag}")
        x_done = sem(f"x_done_{tag}")
        rows = norm_rows.rearrange("(n p) d -> p n d", p=P)

        def plan(eng, turn):
            with eng.Fori(0, steps // NB - 1) as i:
                for b in range(NB):
                    turn(NB * i + b, b, i)
            for b in range(NB):
                turn(steps - NB + b, b, steps // NB - 1)

        def at(n, count=1):
            return slice(n, n + count) if isinstance(n, int) else bass.ds(n, count)

        with nc.Block() as block:
            @block.sync
            def _(sp):
                for counter in (gained_done, norm_done, copied, scored):
                    sp.sem_inc(counter, 2)
                for counter in stored:
                    sp.sem_inc(counter, ROOM)
                sp.sem_inc(turned, NB)
                sp.dma_start(gain[:], d["L0_ffn_ln_g"].rearrange("(a d) -> a d", a=1).broadcast_to([P, D])).then_inc(loaded, 16)
                sp.dma_start(bias[:], d["L0_ffn_ln_b"].rearrange("(a d) -> a d", a=1).broadcast_to([P, D])).then_inc(loaded, 16)
                sp.dma_start(cent[:], d["centroids_t"]).then_inc(loaded, 16)

                def turn(g, b, i):
                    sp.wait_ge(norm_done, g + 3)
                    sp.dma_start(rows[:, at(GROUP * g, GROUP), :], norm[b][:]).then_inc(stored[b], 16)

                plan(sp, turn)
                for counter in stored:
                    sp.wait_ge(counter, ROOM + 16 * (steps // NB))

            @block.vector
            def _(dve):
                dve.wait_ge(loaded, 48)

                def turn(g, b, i):
                    dve.wait_ge(gained_done, g + 1)
                    for j in range(GROUP):
                        n = GROUP * g + j
                        dve.tensor_scalar(raw[b % 2][:, j, :], k["x"][:, at(n), :].rearrange("p a e -> p (a e)"), k["rstd_2"][:, at(n)],
                                          k["shift_2"][:, at(n)], ALU.mult, ALU.add).then_inc(raw_done, 1)
                    dve.wait_ge(raw_done, GROUP * g + GROUP)
                    dve.wait_ge(norm_done, g + 1)
                    dve.tensor_tensor(gained[b % 2][:], raw[b % 2][:], gain[:, None, :].broadcast_to([P, GROUP, D]),
                                      ALU.mult).then_inc(gained_done, 1)

                plan(dve, turn)
                dve.wait_ge(scored, steps + 2)
                dve.tensor_copy(k["scores"][:, :, :], p_sc[:, :].rearrange("p (n e) -> p e n", e=E)).then_inc(kept, 1)

            @block.gpsimd
            def _(pool):
                pool.wait_ge(loaded, 48)

                def turn(g, b, i):
                    pool.wait_ge(gained_done, g + 3)
                    pool.wait_ge(stored[b], ROOM + 16 * i)
                    pool.wait_ge(turned, g + 1)
                    pool.tensor_tensor(norm[b][:], gained[b % 2][:], bias[:, None, :].broadcast_to([P, GROUP, D]),
                                       ALU.add).then_inc(norm_done, 1)

                plan(pool, turn)

            @block.tensor
            def _(pe):
                pe.wait_ge(loaded, 48)

                def turn_rows(g, b):
                    pe.wait_ge(norm_done, g + 3)
                    pe.wait_ge(copied, g + 1)
                    for j in range(GROUP):
                        mm = pe.transpose(p_t[b % 2][:, j * P:(j + 1) * P], norm[b % NB][:, j, :], k["ident"][:])
                    mm.then_inc(turned, 1)

                turn_rows(0, 0)

                def turn(g, b, i):
                    if not isinstance(g, int) or g < steps - 1:
                        turn_rows(g + 1, b + 1)
                    pe.wait_ge(copied, g + 3)
                    for j in range(GROUP):
                        mm = pe.matmul(p_sc[:, at((GROUP * g + j) * E, E)], norm_t[b % 2][:, j, :], cent[:],
                                       start=True, stop=True)
                    mm.then_inc(scored, 1)

                plan(pe, turn)

            @block.scalar
            def _(act):
                def turn(g, b, i):
                    act.wait_ge(turned, g + NB + 1)
                    act.wait_ge(scored, g + 1)
                    act.activation(norm_t[b % 2][:], p_t[b % 2][:, :].rearrange("p (j q) -> p j q", j=GROUP),
                                   ACT.Identity).then_inc(copied, 1)
                    act.wait_ge(raw_done, GROUP * g + GROUP)
                    for j in range(GROUP):
                        n = GROUP * g + j
                        xs = k["x"][:, at(n), :].rearrange("p a e -> p (a e)")
                        act.activation(xs, xs, ACT.Identity, bias=k["shift"][:, at(n)],
                                       scale=k["rstd_1"][:, at(n)]).then_inc(x_done, 1)

                plan(act, turn)


def experts(nc, sem, d, k, norm_rows, ffn_rows, layer):
    tag = f"e{layer}"
    CHUNKS = 8
    per = TILES // CHUNKS
    SPAN = TILES // 4
    with ExitStack() as ctx:
        def sb(name, shape, dt=F32):
            return ctx.enter_context(nc.sbuf_tensor(f"{name}_{tag}", shape, dt))

        def ps(name):
            return ctx.enter_context(nc.psum_tensor(f"{name}_{tag}", [P, 512], F32))

        first_cand = sb("first_cand", [P, CANDS])
        digits = sb("digits", [P, PASSES, CANDS], U32)
        weight = sb("weight", [P, PASSES])
        before = sb("before", [P, P], BF16)
        ones = sb("ones", [P, P], BF16)
        lanes = sb("lanes", [P, P, per], BF16)
        place = sb("place", [P, 2 * SLOTS, TILES], BF16)
        eighth = sb("eighth", [P, 2 * SLOTS, TILES], BF16)
        ones_f = sb("ones_f", [P, TILES])
        avail = sb("avail", [P, TILES])
        s = sb("s", [P, TILES])
        cand = sb("cand", [P, CANDS], U32)
        reach = sb("reach", [P, TILES, CANDS], BF16)
        count = sb("count", [P, CANDS])
        passed = sb("passed", [P, CANDS])
        found = sb("found", [P, 1], U32)
        prefix = sb("prefix", [P, 1], U32)
        flip = sb("flip", [P, 1], U32)
        above = sb("above", [P, TILES], BF16)
        equal = sb("equal", [P, TILES], BF16)
        total = sb("total", [P, TILES])
        sure = sb("sure", [P, 1])
        need = sb("need", [P, 1])
        rank = sb("rank", [P, TILES])
        within = sb("within", [P, TILES])
        chosen = [sb(f"chosen{i}", [P, TILES], BF16) for i in range(2)]
        upto = sb("upto", [P, TILES])
        order = sb("order", [P, TILES])
        slot = sb("slot", [P, TILES])
        slot_i = sb("slot_i", [P, TILES], I32)
        low = sb("low", [P, TILES], I32)
        high = sb("high", [P, TILES], I32)
        low_b = sb("low_b", [P, TILES], BF16)
        high_b = sb("high_b", [P, TILES], BF16)
        lane_of = sb("lane_of", [P, CHUNKS, P, per], BF16)
        tile_is = sb("tile_is", [P, 2 * SLOTS, TILES], BF16)
        tile_of = sb("tile_of", [P, 2 * SLOTS, TILES], BF16)
        tok_hi = sb("tok_hi", [P, SLOTS])
        index = [sb(f"index{i}", [P, SLOTS], U32) for i in range(3)]
        w1 = [sb(f"w1_{i}", [P, F]) for i in range(2)]
        w2 = [sb(f"w2_{i}", [P, FC, D]) for i in range(2)]
        b1 = [sb(f"b1_{i}", [P, FC]) for i in range(2)]
        b2 = [sb(f"b2_{i}", [P, D]) for i in range(2)]
        rows = [sb(f"rows{i}", [P, SLOTS, D]) for i in range(2)]
        rows_t = sb("rows_t", [P, CAP])
        hid = sb("hid", [P, FC, CAP])
        y = sb("y", [P, SLOTS, D])
        yb = [sb(f"yb{i}", [P, SLOTS, D]) for i in range(2)]
        p_cnt = ps("p_cnt")
        p_rank = ps("p_rank")
        p_list = ps("p_list")
        p_t = ps("p_t")
        p_h = [ps(f"p_h{i}") for i in range(2)]
        p_y = [ps(f"p_y{i}") for i in range(2)]
        p_idx = p_list[:, 2 * TILES:2 * TILES + 2 * SLOTS]

        consts = sem(f"consts_{tag}")
        wl = [sem(f"expert_loaded{i}_{tag}") for i in range(2)]
        reached = sem(f"reached_{tag}")
        counted = sem(f"counted_{tag}")
        sv = sem(f"search_step_{tag}")
        lv = sem(f"list_step_{tag}")
        prefixed = sem(f"prefixed_{tag}")
        marked = sem(f"marked_{tag}")
        ranked = sem(f"ranked_{tag}")
        chosen_done = sem(f"chosen_{tag}")
        chosen_ranked = sem(f"chosen_ranked_{tag}")
        lanes_done = sem(f"lanes_done_{tag}")
        tiles_done = sem(f"tiles_done_{tag}")
        listed = sem(f"listed_{tag}")
        index_done = sem(f"index_done_{tag}")
        gathered = [sem(f"gathered{i}_{tag}") for i in range(2)]
        rt_done = sem(f"rows_turned_{tag}")
        rt_copied = sem(f"rows_t_copied_{tag}")
        up_done = sem(f"up_done_{tag}")
        gelu_done = sem(f"gelu_done_{tag}")
        down_done = sem(f"down_done_{tag}")
        y_copied = sem(f"y_copied_{tag}")
        y_ready = sem(f"y_ready_{tag}")
        scattered = [sem(f"scattered{i}_{tag}") for i in range(2)]
        scatters_seen = sem(f"scatters_seen_{tag}")
        wait_passed = sem(f"passed_{tag}")

        def plan(eng, turn):
            for e in range(3):
                turn(e, e % 2, e // 2)
            with eng.Fori(0, (E - 4) // 2) as i:
                turn(2 * i + 3, 1, i + 1)
                turn(2 * i + 4, 0, i + 2)
            for e in range(E - 1, E + 2):
                turn(e, e % 2, e // 2)

        def does(e):
            if not isinstance(e, int):
                return True, (e - 1,), True
            lists = () if e == 0 or e > E - 1 else (e - 1,) if e < E - 1 else (e - 1, e)
            return e < E - 1, lists, e >= 2

        def list_of(l, par):
            return index[2] if isinstance(l, int) and l == E - 1 else index[par]

        MARK_LINKS = 1 + 4 * PASSES + 4 + 1
        SEARCH_LINKS = MARK_LINKS + 6
        PREFIXES = PASSES - 2
        LIST_LINKS = 9

        with nc.Block() as block:
            @block.sync
            def _(sp):
                for dst, src in ((first_cand, "c_first_cand"), (digits, "c_digits"), (weight, "c_weight"),
                                 (before, "c_before"), (lanes, "c_lanes"), (place, "c_place"), (eighth, "c_eighth")):
                    sp.dma_start(dst[:], d[src]).then_inc(consts, 16)

                def turn(e, par, half):
                    if isinstance(e, int) and e >= E:
                        return
                    at = bass.ds(e, 1) if not isinstance(e, int) else slice(e, e + 1)
                    w1_src = d["L0_ffn_w1"][at, :, :].rearrange("a p f -> (a p) f")
                    w2_src = d["L0_ffn_w2"][at, :, :].rearrange("a (p c) n -> (a p) c n", c=FC)
                    b1_src = d["L0_ffn_b1"][at, :].rearrange("a (p c) -> (a p) c", c=FC)
                    b2_src = d["L0_ffn_b2"][at, :].broadcast_to([P, D])
                    if not isinstance(e, int) or e > 1:
                        sp.wait_ge(y_ready, 2 * e - 2)
                    sp.dma_start(w1[par][:], w1_src).then_inc(wl[par], 16)
                    sp.dma_start(w2[par][:], w2_src).then_inc(wl[par], 16)
                    sp.dma_start(b1[par][:], b1_src).then_inc(wl[par], 16)
                    sp.dma_start(b2[par][:], b2_src).then_inc(wl[par], 16)

                plan(sp, turn)

            @block.vector
            def _(dve):
                dve.wait_ge(consts, 16 * 7)
                dve.memset(ones[:], 1.0).then_inc(sv, 1)
                dve.memset(ones_f[:], 1.0).then_inc(sv, 1)
                dve.memset(avail[:], -TAKEN).then_inc(sv, 1)
                dve.wait_ge(sv, 3)

                def listing(l, par):
                    done = [0]

                    def link(ins):
                        done[0] += 1
                        ins.then_inc(lv, 1)
                        dve.wait_ge(lv, LIST_LINKS * l + done[0])

                    def slots():
                        dve.wait_ge(chosen_ranked, l + 1)
                        link(dve.tensor_tensor_scan(upto[:], ones_f[:], p_list[:, TILES:2 * TILES], 0.0, ALU.mult, ALU.add))
                        link(dve.tensor_tensor(order[:], upto[:], p_list[:, 0:TILES], ALU.add))
                        link(dve.scalar_tensor_tensor(slot[:], order[:], 1.0, chosen[par][:], ALU.add, ALU.mult))

                    def parts():
                        link(dve.tensor_scalar(slot_i[:], slot[:], -1.0, None, ALU.add))
                        dve.tensor_scalar(low[:], slot_i[:], P - 1, None, ALU.bitwise_and).then_inc(lv, 1)
                        done[0] += 1
                        link(dve.tensor_scalar(high[:], slot_i[:], 7, None, ALU.arith_shift_right))

                    def narrow():
                        dve.tensor_copy(low_b[:], low[:]).then_inc(lv, 1)
                        done[0] += 1
                        link(dve.tensor_copy(high_b[:], high[:]))

                    def tiles():
                        link(dve.tensor_tensor(tile_is[:], high_b[:, None, :].broadcast_to([P, 2 * SLOTS, TILES]), eighth[:],
                                               ALU.is_equal))
                        if not isinstance(l, int) or l > 0:
                            dve.wait_ge(listed, l)
                        dve.tensor_tensor(tile_of[:], tile_is[:], place[:], ALU.mult).then_inc(tiles_done, 1)

                    def lane_chunk(c):
                        if c == 0 and (not isinstance(l, int) or l > 0):
                            dve.wait_ge(listed, l)
                        dve.tensor_tensor(lane_of[:, c, :, :], low_b[:, None, c * per:(c + 1) * per].broadcast_to([P, P, per]),
                                          lanes[:], ALU.is_equal).then_inc(lanes_done, 1)

                    def result():
                        dve.wait_ge(listed, l + 1)
                        if not isinstance(l, int) or 1 < l < E - 1:
                            dve.wait_ge(scatters_seen, l - 1)
                        dve.tensor_scalar(tok_hi[:], p_idx[:, 0:SLOTS], float(P), None, ALU.mult).then_inc(index_done, 1)
                        dve.wait_ge(index_done, 2 * l + 1)
                        dve.tensor_tensor(list_of(l, par)[:], tok_hi[:], p_idx[:, SLOTS:2 * SLOTS], ALU.add).then_inc(index_done, 1)
                        assert done[0] == LIST_LINKS, done

                    return slots, parts, narrow, tiles, lane_chunk, result

                def turn(e, par, half):
                    seek, lists, _ = does(e)
                    done = [0]

                    def link(ins):
                        done[0] += 1
                        ins.then_inc(sv, 1)
                        dve.wait_ge(sv, 3 + SEARCH_LINKS * e + done[0])

                    if isinstance(e, int) and e >= E:
                        return
                    at = bass.ds(e, 1) if not isinstance(e, int) else slice(e, e + 1)
                    if not seek:
                        dve.tensor_scalar(chosen[par][:], avail[:], 0.0, None, ALU.is_gt).then_inc(chosen_done, 1)
                        for l in lists:
                            slots, parts, narrow, tiles, lane_chunk, result = listing(l, l % 2)
                            slots(), parts(), narrow(), tiles()
                            for c in range(CHUNKS):
                                lane_chunk(c)
                            result()
                        return
                    windows = [[] for _ in range(PASSES)]
                    if lists:
                        slots, parts, narrow, tiles, lane_chunk, result = listing(lists[0], 1 - par)
                        chunks = [lambda c=c: lane_chunk(c) for c in range(CHUNKS)]
                        windows = [[slots], [parts, narrow], [tiles], chunks[0:2], chunks[2:4], chunks[4:6], chunks[6:8], [result]]
                    link(dve.tensor_tensor(s[:], k["scores"][:, at, :].rearrange("p a n -> p (a n)"), avail[:], ALU.min))
                    for n in range(PASSES):
                        c = (first_cand[:] if n == 0 else cand[:].bitcast(F32))[:, None, :].broadcast_to([P, TILES // 2, CANDS])
                        for part in (slice(0, TILES // 2), slice(TILES // 2, TILES)):
                            dve.tensor_tensor(reach[:, part, :], s[:, part, None].broadcast_to([P, TILES // 2, CANDS]), c,
                                              ALU.is_ge).then_inc(reached, 1)
                        if n > 1:
                            dve.tensor_tensor(prefix[:], prefix[:], found[:], ALU.bitwise_xor).then_inc(prefixed, 1)
                        for piece in windows[n]:
                            piece()
                        dve.wait_ge(counted, PASSES * e + n + 1)
                        link(dve.tensor_reduce(count[:], p_cnt[:, 0:SPAN * CANDS].rearrange("p (n c) -> p c n", c=CANDS), AX.X, ALU.add))
                        if n > 1:
                            dve.wait_ge(prefixed, PREFIXES * e + n - 1)
                        link(dve.tensor_scalar(passed[:], count[:], float(CAP), weight[:, n:n + 1], ALU.is_ge, ALU.mult))
                        with nc.allow_low_precision(reason="a digit times its weight is exact in both"):
                            link(dve.tensor_reduce(found[:], passed[:], AX.X, ALU.add))
                        if n == 0:
                            link(dve.tensor_scalar(found[:], found[:], 32 - 4, None, ALU.logical_shift_left))
                            link(dve.tensor_scalar(flip[:].bitcast(I32), found[:].bitcast(I32), -1, 31, ALU.bitwise_xor, ALU.arith_shift_right))
                            link(dve.tensor_scalar(flip[:].bitcast(I32), flip[:].bitcast(I32), -2**31, None, ALU.bitwise_or))
                            link(dve.tensor_tensor(prefix[:], found[:], flip[:], ALU.bitwise_xor))
                            link(dve.tensor_scalar(cand[:], digits[:, 1, :], prefix[:, 0:1], None, ALU.bitwise_xor))
                        elif n + 1 < PASSES:
                            link(dve.tensor_scalar(cand[:], digits[:, n + 1, :], prefix[:, 0:1], found[:, 0:1],
                                                   ALU.bitwise_xor, ALU.bitwise_xor))
                        else:
                            link(dve.tensor_tensor(prefix[:], prefix[:], found[:], ALU.bitwise_xor))
                    limit = prefix[:].bitcast(F32)
                    dve.tensor_scalar(equal[:], s[:], limit, None, ALU.is_equal).then_inc(marked, 1)
                    link(dve.tensor_scalar(above[:], s[:], limit, None, ALU.is_gt))
                    dve.wait_ge(ranked, e + 1)
                    link(dve.tensor_reduce(sure[:], p_rank[:, 2 * TILES:3 * TILES], AX.X, ALU.add))
                    link(dve.tensor_scalar(need[:], sure[:], -1.0, float(CAP), ALU.mult, ALU.add))
                    link(dve.tensor_tensor_scan(total[:], ones_f[:], p_rank[:, TILES:2 * TILES], 0.0, ALU.mult, ALU.add))
                    link(dve.tensor_tensor(rank[:], total[:], p_rank[:, 0:TILES], ALU.add))
                    link(dve.scalar_tensor_tensor(within[:], rank[:], need[:, 0:1], equal[:], ALU.is_lt, ALU.mult))
                    dve.tensor_tensor(chosen[par][:], within[:], above[:], ALU.add).then_inc(chosen_done, 1)
                    dve.wait_ge(chosen_done, e + 1)
                    link(dve.scalar_tensor_tensor(avail[:], chosen[par][:], 2 * TAKEN, avail[:], ALU.mult, ALU.add))
                    assert done[0] == SEARCH_LINKS, done

                plan(dve, turn)

            @block.tensor
            def _(pe):
                pe.wait_ge(consts, 16 * 7)
                pe.wait_ge(sv, 3)

                def turn(e, par, half):
                    seek, lists, compute = does(e)
                    c = e - 2

                    def turn_rows(h):
                        if h == 0:
                            pe.wait_ge(gathered[par], 16 * SLOTS * half)
                            pe.wait_ge(wl[par], 64 * half)
                        if not isinstance(e, int) or c > 0 or h > 0:
                            pe.wait_ge(rt_copied, 2 * c + h)
                        for j in range(4):
                            mm = pe.transpose(p_t[:, j * P:(j + 1) * P], rows[par][:, 4 * h + j, :], k["ident"][:])
                        mm.then_inc(rt_done, 1)

                    def up(m):
                        f, h = m % FC, m // FC
                        pe.wait_ge(rt_copied, 2 * c + h + 1)
                        if m >= 2:
                            pe.wait_ge(gelu_done, 8 * c + m - 1)
                        pe.matmul(p_h[m % 2][:], w1[par][:, f:F:FC], rows_t[:, h * 512:(h + 1) * 512],
                                  start=True, stop=True).then_inc(up_done, 1)

                    def down(t):
                        pe.wait_ge(gelu_done, 8 * c + (4 if t < 4 else 8))
                        if t % 4 == 0 and (not isinstance(e, int) or c > 0):
                            pe.wait_ge(y_copied, 2 * c - 1 + t // 4)
                        for f in range(FC):
                            mm = pe.matmul(p_y[t // 4][:, (t % 4) * D:(t % 4 + 1) * D], hid[:, f, t * P:(t + 1) * P], w2[par][:, f, :],
                                           start=(f == 0), stop=(f == FC - 1))
                        if t % 4 == 3:
                            mm.then_inc(down_done, 1)

                    def list_chunk(l, n):
                        pe.wait_ge(lanes_done, CHUNKS * l + n + 1)
                        if n == 0:
                            pe.wait_ge(tiles_done, l + 1)
                        for j in range(per):
                            t = n * per + j
                            mm = pe.matmul(p_idx, lane_of[:, n, :, j], tile_of[:, :, t], start=(t == 0), stop=(t == TILES - 1))
                        if n == CHUNKS - 1:
                            mm.then_inc(listed, 1)

                    def rank_chosen(l, lpar):
                        pe.wait_ge(chosen_done, l + 1)
                        if not isinstance(l, int) or l > 0:
                            pe.wait_ge(index_done, 2 * l)
                        pe.matmul(p_list[:, 0:TILES], before[:], chosen[lpar][:], start=True, stop=True)
                        pe.matmul(p_list[:, TILES:2 * TILES], ones[:], chosen[lpar][:], start=True, stop=True).then_inc(chosen_ranked, 1)

                    pieces = [[] for _ in range(PASSES + 2)]
                    if compute:
                        pieces = [[], [lambda: turn_rows(0)], [lambda: turn_rows(1), lambda: up(0), lambda: up(1)],
                                  [lambda: up(2), lambda: up(3)], [lambda: up(4), lambda: up(5)],
                                  [lambda: up(6), lambda: up(7)], [lambda: down(0), lambda: down(1)],
                                  [lambda: down(2), lambda: down(3)], [lambda: down(4), lambda: down(5)],
                                  [lambda: down(6), lambda: down(7)]]
                    if not seek:
                        for n, piece in enumerate(sum(pieces, [])):
                            if lists and n == 3:
                                for q in range(CHUNKS):
                                    list_chunk(E - 2, q)
                            if lists and n == 8:
                                rank_chosen(E - 1, (E - 1) % 2)
                            if lists and n == 14:
                                for q in range(CHUNKS):
                                    list_chunk(E - 1, q)
                            piece()
                        return
                    if lists:
                        l = lists[0]
                        for n in range(3, 7):
                            chunks = range(2 * n - 6, 2 * n - 4)
                            pieces[n] = pieces[n] + [lambda q=q: list_chunk(l, q) for q in chunks]
                    for n in range(PASSES):
                        for q in range(TILES // SPAN):
                            if q % 2 == 0:
                                pe.wait_ge(reached, 2 * PASSES * e + 2 * n + q // 2 + 1)
                            mm = pe.matmul(p_cnt[:, 0:SPAN * CANDS], ones[:],
                                           reach[:, q * SPAN:(q + 1) * SPAN, :].rearrange("p n c -> p (n c)"),
                                           start=(q == 0), stop=(q == TILES // SPAN - 1))
                        mm.then_inc(counted, 1)
                        for piece in pieces[n]:
                            piece()
                    pe.wait_ge(marked, e + 1)
                    pe.matmul(p_rank[:, 0:TILES], before[:], equal[:], start=True, stop=True)
                    pe.matmul(p_rank[:, TILES:2 * TILES], ones[:], equal[:], start=True, stop=True)
                    pe.wait_ge(sv, 3 + SEARCH_LINKS * e + MARK_LINKS)
                    pe.matmul(p_rank[:, 2 * TILES:3 * TILES], ones[:], above[:], start=True, stop=True).then_inc(ranked, 1)
                    for piece in pieces[PASSES]:
                        piece()
                    rank_chosen(e, par)
                    for piece in pieces[PASSES + 1]:
                        piece()

                plan(pe, turn)

            @block.scalar
            def _(act):
                def turn(e, par, half):
                    _, _, compute = does(e)
                    if not compute:
                        return
                    c = e - 2
                    later = not isinstance(e, int) or c > 0

                    def copy_rows(h):
                        act.wait_ge(rt_done, 2 * c + h + 1)
                        if later:
                            act.wait_ge(up_done, 8 * c)
                        act.activation(rows_t[:, h * 512:(h + 1) * 512], p_t[:], ACT.Identity).then_inc(rt_copied, 1)

                    def gelu(m):
                        f, h = m % FC, m // FC
                        act.wait_ge(up_done, 8 * c + m + 1)
                        if later:
                            act.wait_ge(down_done, 2 * c)
                        act.wait_ge(wl[par], 64 * half)
                        act.activation(hid[:, f, h * 512:(h + 1) * 512], p_h[m % 2][:], ACT.Gelu_apprx_tanh,
                                       bias=b1[par][:, f:f + 1]).then_inc(gelu_done, 1)

                    def copy_y(h):
                        act.wait_ge(down_done, 2 * c + h + 1)
                        if later:
                            act.wait_ge(y_ready, 2 * c + h - 1)
                        act.activation(y[:, 4 * h:4 * h + 4, :], p_y[h][:, :].rearrange("p (t n) -> p t n", n=D),
                                       ACT.Identity).then_inc(y_copied, 1)

                    copy_rows(0)
                    copy_rows(1)
                    for m in range(8):
                        gelu(m)
                    copy_y(0)
                    copy_y(1)

                plan(act, turn)

            @block.gpsimd
            def _(pool):
                pool.wait_ge(consts, 16 * 7)

                def gather(l, lpar, seen):
                    if not isinstance(l, int) or l > 1:
                        pool.wait_ge(rt_done, 2 * l - 2)
                    if not isinstance(l, int) or 1 < l < E - 1:
                        pool.wait_ge(scattered[lpar], 16 * SLOTS * seen)
                        pool.sem_inc(scatters_seen, 1)
                    wait_apart(pool, index_done, 2 * l + 2, wait_passed)
                    for j in range(SLOTS):
                        pool.indirect_dma_start(rows[lpar][:, j, :], None, norm_rows,
                                                bass.IndirectOffsetOnAxis(ap=list_of(l, lpar)[:, j:j + 1], axis=0)).then_inc(gathered[lpar], 16)

                def scatter(c, par, half):
                    pool.wait_ge(wl[par], 64 * half)
                    if isinstance(c, int) and c == E - 1:
                        pool.wait_ge(scattered[par], 16 * SLOTS * (half - 1))
                    for h in range(2):
                        part = slice(h * SLOTS // 2, (h + 1) * SLOTS // 2)
                        pool.wait_ge(y_copied, 2 * c + h + 1)
                        pool.tensor_tensor(yb[par][:, part, :], y[:, part, :], b2[par][:, None, :].broadcast_to([P, SLOTS // 2, D]),
                                           ALU.add).then_inc(y_ready, 1)
                        wait_apart(pool, y_ready, 2 * c + h + 1, wait_passed)
                        for j in range(part.start, part.stop):
                            pool.indirect_dma_start(ffn_rows, bass.IndirectOffsetOnAxis(ap=list_of(c, par)[:, j:j + 1], axis=0),
                                                    yb[par][:, j, :], None).then_inc(scattered[par], 16)

                def turn(e, par, half):
                    _, lists, compute = does(e)
                    if lists:
                        gather(lists[0], 1 - par, half - 1 + par)
                    for l in lists[1:]:
                        gather(l, par, half)
                    if compute:
                        scatter(e - 2, par, half)

                plan(pool, turn)
                for par in range(2):
                    pool.wait_ge(scattered[par], 16 * SLOTS * (E // 2))


def add_rows(nc, sem, k, rows_dram, out, layer):
    tag = f"r{layer}"
    steps = 8
    per = TILES // steps
    with ExitStack() as ctx:
        buf = [ctx.enter_context(nc.sbuf_tensor(f"buf{i}_{tag}", [P, per, D], F32)) for i in range(4)]
        loaded = [sem(f"rows_loaded{i}_{tag}") for i in range(4)]
        added = sem(f"rows_added_{tag}")
        measured = sem(f"rows_measured_{tag}")
        stored = sem(f"out_stored_{tag}")
        rows = rows_dram.rearrange("(n p) d -> p n d", p=P)
        out_v = out.rearrange("b (t p) d -> p (b t) d", p=P) if out is not None else None
        with nc.Block() as block:
            @block.sync
            def _(sp):
                for g in range(steps):
                    if g >= 4:
                        sp.wait_ge(added, g - 3)
                    sp.dma_start(buf[g % 4][:], rows[:, g * per:(g + 1) * per, :]).then_inc(loaded[g % 4], 16)
            if out is not None:
                @block.scalar
                def _(act):
                    for g in range(steps):
                        act.wait_ge(added, g + 1)
                        act.dma_start(out_v[:, g * per:(g + 1) * per, :], k["x"][:, g * per:(g + 1) * per, :]).then_inc(stored, 16)
                    act.wait_ge(stored, 16 * steps)

            @block.vector
            def _(dve):
                for g in range(steps):
                    dve.wait_ge(loaded[g % 4], 16 * (g // 4) + 16)
                    part = k["x"][:, g * per:(g + 1) * per, :]
                    dve.tensor_tensor(part, part, buf[g % 4][:], ALU.add).then_inc(added, 1)
                    if out is None:
                        dve.wait_ge(added, g + 1)
                        for n in range(g * per, (g + 1) * per):
                            dve.bn_stats(k["halves"][:, n, :], k["x"][:, n, :]).then_inc(measured, 1)


def attention_b(nc, sem, d, k):
    with ExitStack() as outer:
        def keep(name, shape, dt=F32):
            return outer.enter_context(nc.sbuf_tensor(f"{name}_ab", shape, dt))

        values = keep("values", [P, TILES, D])
        phases = keep("phases", [P, TILES, 2, RFF])
        powers = keep("powers", [P, TILES, NM])
        decay = keep("decay", [P, T])
        features(nc, d, k, sem, values, phases, powers, decay)
        attend(nc, d, k, sem, values, phases, powers, decay)


def features(nc, d, k, sem, values, phases, powers, decay):
    W = FEAT + D
    steps = TILES // GROUP
    with ExitStack() as ctx:
        def sb(name, shape, dt=F32):
            return ctx.enter_context(nc.sbuf_tensor(f"{name}_fe", shape, dt))

        def ps(name):
            return ctx.enter_context(nc.psum_tensor(f"{name}_fe", [P, 512], F32))

        w_all = sb("w_all", [P, W])
        w_shell = sb("w_shell", [SHELL, D])
        omega_t = sb("omega_t", [SHELL, RFF])
        b_shell = sb("b_shell", [SHELL, P])
        b_all = sb("b_all", [P, W])
        b_rff = sb("b_rff", [P, RFF])
        temp = sb("temp", [P, 1])
        small = [sb(f"small{i}", [P, 1]) for i in range(6)]
        a = [sb(f"a{i}", [P, GROUP, D]) for i in range(2)]
        a_t = [sb(f"a_t{i}", [P, GROUP, P]) for i in range(2)]
        feat = sb("feat", [P, TILES, FEAT])
        sq = sb("sq", [P, GROUP, SHELL])
        ss = sb("ss", [P, TILES])
        length = sb("length", [P, TILES])
        proj = sb("proj", [P, TILES, RFF])
        turns = sb("turns", [P, TILES, RFF])
        arg = sb("arg", [P, TILES, RFF])
        size = sb("size", [P, TILES, RFF])
        quarter = sb("quarter", [P, 1])
        charge = sb("charge", [P, TILES])
        c_mag = sb("c_mag", [P, NM])
        p_t = [ps(f"p_t{i}") for i in range(2)]
        p_f = [[ps(f"p_f{i}{j}") for j in range(2)] for i in range(2)]
        p_w = ps("p_w")

        loaded = sem("fe_loaded")
        product = sem("fe_weight_product")
        step = sem("fe_step")
        ast = sem("fe_act_step")
        a_done = sem("fe_a_done")
        turned = [sem(f"fe_turned{i}") for i in range(2)]
        copied = [sem(f"fe_copied{i}") for i in range(2)]
        made = [sem(f"fe_made{i}") for i in range(2)]
        kept = sem("fe_kept")
        ss_done = sem("fe_ss_done")
        squared = sem("fe_squared")
        arg_done = sem("fe_arg_done")

        def plan(eng, turn):
            with eng.Fori(0, steps // 2 - 1) as i:
                for par in range(2):
                    turn(2 * i + par, par, i, True)
            turn(steps - 2, 0, steps // 2 - 1, True)
            turn(steps - 1, 1, steps // 2 - 1, False)

        def at(n, count=1):
            return slice(n, n + count) if isinstance(n, int) else bass.ds(n, count)

        with nc.Block() as block:
            @block.sync
            def _(sp):
                for counter in (*copied, *turned, *made, ss_done):
                    sp.sem_inc(counter, ROOM)
                sp.sem_inc(kept, ROOM + 4)
                for dst, src in ((w_all[:, 0:SHELL], d["w_shell_t"]), (w_all[:, SHELL:SHELL + 1], d["w_charge_t"]),
                                 (w_all[:, FEAT:W], d["w_vb_t"]), (w_shell[:], d["L0_attn_b_W_shell"]),
                                 (omega_t[:], d["omega_t"]),
                                 (b_shell[:], d["b_shell_wide"]),
                                 (b_all[:, 0:SHELL], d["L0_attn_b_b_shell"].rearrange("(a b) -> a b", a=1).broadcast_to([P, SHELL])),
                                 (b_all[:, SHELL:SHELL + 1], d["L0_attn_b_b_charge"].rearrange("(a b) -> a b", a=1).broadcast_to([P, 1])),
                                 (b_all[:, FEAT:W], d["L0_attn_b_b_v"].rearrange("(a b) -> a b", a=1).broadcast_to([P, D])),
                                 (b_rff[:], d["L0_attn_b_rff_bias"].rearrange("(a b) -> a b", a=1).broadcast_to([P, RFF])),
                                 (temp[:], d["L0_attn_b_log_temp"].broadcast_to([P, 1])),
                                 (decay[:], d["c_decay"]), (c_mag[:], d["c_mag"])):
                    sp.dma_start(dst, src).then_inc(loaded, 16)

            @block.tensor
            def _(pe):
                pe.wait_ge(loaded, 16 * 13)
                pe.matmul(p_w[:, 0:RFF], w_shell[:], omega_t[:], start=True, stop=True).then_inc(product, 1)
                pe.matmul(p_w[:, RFF:2 * RFF], b_shell[:], omega_t[:], start=True, stop=True).then_inc(product, 1)
                pe.wait_ge(step, 2)
                def turn_rows(g, par, i):
                    pe.wait_ge(a_done, GROUP * g + GROUP)
                    pe.wait_ge(copied[par], ROOM + i)
                    for j in range(GROUP):
                        mm = pe.transpose(p_t[par][:, j * P:(j + 1) * P], a[par][:, j, :], k["ident"][:])
                    mm.then_inc(turned[par], 1)

                turn_rows(0, 0, 0)

                def turn(g, par, i, more):
                    if more:
                        turn_rows(g + 1, 1 - par, i + par)
                    pe.wait_ge(copied[par], ROOM + i + 1)
                    pe.wait_ge(kept, ROOM + 4 * g)
                    for j in range(GROUP):
                        mm = pe.matmul(p_f[par][j // 2][:, (j % 2) * 256:(j % 2) * 256 + W], a_t[par][:, j, :], w_all[:],
                                       start=True, stop=True)
                    mm.then_inc(made[par], 1)

                plan(pe, turn)

            @block.scalar
            def _(act):
                link = Chain(act, ast)
                act.wait_ge(loaded, 16 * 13)
                link(act.activation(small[0][:], temp[:], ACT.Abs))
                link(act.activation(small[1][:], small[0][:], ACT.Exp, scale=-1.0))
                link(act.activation(small[2][:], small[1][:], ACT.Ln, bias=1.0))
                link(act.activation(small[3][:], temp[:], ACT.Relu))

                def normalise(g, par, i):
                    act.wait_ge(turned[par], ROOM + i)
                    for j in range(GROUP):
                        n = GROUP * g + j
                        act.activation(a[par][:, j, :], k["x"][:, at(n), :].rearrange("p a e -> p (a e)"), ACT.Identity,
                                       bias=k["shift"][:, at(n)], scale=k["rstd"][:, at(n)]).then_inc(a_done, 1)

                normalise(0, 0, 0)

                def turn(g, par, i, more):
                    if more:
                        normalise(g + 1, 1 - par, i + par)
                    act.wait_ge(turned[par], ROOM + i + 1)
                    act.wait_ge(made[par], ROOM + i)
                    act.activation(a_t[par][:], p_t[par][:, :].rearrange("p (j q) -> p j q", j=GROUP),
                                   ACT.Identity).then_inc(copied[par], 1)

                plan(act, turn)
                act.wait_ge(ss_done, ROOM + steps)
                link(act.activation(length[:], ss[:], ACT.Sqrt))
                act.wait_ge(kept, ROOM + 4 + 4 * steps)
                link(act.activation(charge[:], feat[:, :, SHELL], ACT.Tanh))
                act.wait_ge(arg_done, 1)
                link(act.activation(size[:], arg[:], ACT.Abs))
                link(act.activation(phases[:, :, 0, :], size[:], ACT.Sin, bias=quarter[:], scale=-1.0))
                link(act.activation(phases[:, :, 1, :], arg[:], ACT.Sin))

            @block.vector
            def _(dve):
                link = Chain(dve, step)
                dve.wait_ge(product, 2)
                link(dve.tensor_copy(w_all[:, SHELL + 1:FEAT], p_w[:, 0:RFF]))
                link(dve.tensor_copy(b_all[:, SHELL + 1:FEAT], p_w[:, RFF:2 * RFF]))
                link(dve.memset(quarter[:], math.pi / 2))
                dve.wait_ge(ast, 4)
                link(dve.tensor_tensor(small[4][:], small[2][:], small[3][:], ALU.add))
                link(dve.tensor_scalar(small[4][:], small[4][:], 0.1, None, ALU.add))
                link(dve.reciprocal(small[5][:], small[4][:]))
                link(dve.tensor_scalar(decay[:], decay[:], small[5][:, 0:1], None, ALU.mult))

                def turn(g, par, i, more):
                    dve.wait_ge(made[par], ROOM + i + 1)
                    for half in range(2):
                        part = at(GROUP * g + 2 * half, 2)
                        src = p_f[par][half][:, :].rearrange("p (t w) -> p t w", t=2)
                        dve.tensor_tensor(feat[:, part, :], src[:, :, 0:FEAT],
                                          b_all[:, None, 0:FEAT].broadcast_to([P, 2, FEAT]), ALU.add).then_inc(kept, 1)
                        dve.tensor_tensor(values[:, part, :], src[:, :, FEAT:W],
                                          b_all[:, None, FEAT:W].broadcast_to([P, 2, D]), ALU.add).then_inc(kept, 1)
                    dve.wait_ge(kept, ROOM + 4 + 4 * g + 4)
                    shell = feat[:, at(GROUP * g, GROUP), 0:SHELL]
                    dve.wait_ge(ss_done, ROOM + g)
                    dve.tensor_tensor(sq[:], shell, shell, ALU.mult).then_inc(squared, 1)
                    dve.wait_ge(squared, g + 1)
                    dve.tensor_reduce(ss[:, at(GROUP * g, GROUP)], sq[:], AX.X, ALU.add).then_inc(ss_done, 1)

                plan(dve, turn)
                dve.wait_ge(ast, 5)
                link(dve.tensor_scalar(length[:], length[:], 1e-12, None, ALU.max))
                link(dve.reciprocal(ss[:], length[:]))
                link(dve.tensor_tensor(proj[:], feat[:, :, SHELL + 1:FEAT], ss[:, :, None].broadcast_to([P, TILES, RFF]), ALU.mult))
                link(dve.tensor_tensor(proj[:], proj[:], b_rff[:, None, :].broadcast_to([P, TILES, RFF]), ALU.add))
                dve.wait_ge(ast, 6)
                link(dve.memset(powers[:, :, 0], 1.0))
                for m in range(1, NM):
                    link(dve.tensor_tensor(powers[:, :, m], powers[:, :, m - 1], charge[:], ALU.mult))
                link(dve.tensor_tensor(powers[:], powers[:], c_mag[:, None, :].broadcast_to([P, TILES, NM]), ALU.mult))
                link(dve.tensor_scalar(turns[:], proj[:], 1.0 / (2 * math.pi), ROUND, ALU.mult, ALU.add))
                link(dve.tensor_scalar(turns[:], turns[:], ROUND, None, ALU.subtract))
                for part in TWO_PI:
                    link(dve.scalar_tensor_tensor(proj[:], turns[:], -part, proj[:], ALU.mult, ALU.add))
                dve.tensor_scalar(arg[:], proj[:], -PI, PI, ALU.max, ALU.min).then_inc(arg_done, 1)


def attend(nc, d, k, sem, values, phases, powers, decay):
    KC = 3
    with ExitStack() as ctx:
        def sb(name, shape, dt=F32):
            return ctx.enter_context(nc.sbuf_tensor(f"{name}_at", shape, dt))

        def ps(name):
            return ctx.enter_context(nc.psum_tensor(f"{name}_at", [P, 512], F32))

        w_comb = sb("w_comb", [P, KC, P])
        w_out = sb("w_out", [P, D])
        b_out = sb("b_out", [P, D])
        bar = sb("bar", [P, P], BF16)
        ident_b = sb("ident_b", [P, P], BF16)
        tp = [sb(f"tp{i}", [P, PER, KC * P]) for i in range(2)]
        tp_t = [sb(f"tp_t{i}", [P, KC, T]) for i in range(2)]
        phi_t = [sb(f"phi_t{i}", [P, T]) for i in range(2)]
        v = [sb(f"v{i}", [P, PER, D]) for i in range(2)]
        logit = [sb(f"logit{i}", [P, 384]) for i in range(2)]
        prob = [sb(f"prob{i}", [P, 384]) for i in range(2)]
        prob_t = [sb(f"prob_t{i}", [P, 384]) for i in range(2)]
        o_t = [sb(f"o_t{i}", [P, T]) for i in range(2)]
        top = [sb(f"top{i}", [P, PER]) for i in range(2)]
        ntop = [sb(f"ntop{i}", [P, PER]) for i in range(2)]
        mass = [sb(f"mass{i}", [P, PER]) for i in range(2)]
        rmass = [sb(f"rmass{i}", [P, PER]) for i in range(2)]
        p_tp = [ps(f"p_tp{i}") for i in range(2)]
        p_phi = ps("p_phi")
        p_s = [ps(f"p_s{i}") for i in range(2)]
        p_pt = ps("p_pt")
        p_o = ps("p_o")
        p_y = ps("p_y")

        loaded = sem("at_loaded")
        padded = sem("at_padded")
        tp_done = sem("at_tp_done")
        v_done = sem("at_v_done")
        tpt_done = sem("at_tp_turned")
        tpt_copied = sem("at_tp_copied")
        phi_done = sem("at_phi_done")
        phi_copied = sem("at_phi_copied")
        s_done = sem("at_scores_done")
        l_done = sem("at_logits_done")
        n_done = sem("at_ntop_done")
        e_done = sem("at_exp_done")
        pt_done = sem("at_prob_turned")
        pt_copied = sem("at_prob_copied")
        o_done = sem("at_o_done")
        o_copied = sem("at_o_copied")
        y_done = sem("at_y_done")
        r_done = sem("at_mass_inverted")
        xb_done = sem("at_bias_added")
        x_done = sem("at_x_added")
        passed = sem("at_passed")
        measured = sem("at_x_measured")

        def plan(eng, turn):
            turn(0, 0)
            with eng.Fori(0, (B - 4) // 2) as i:
                turn(2 * i + 1, 1)
                turn(2 * i + 2, 0)
            for g in range(B - 3, B):
                turn(g, g % 2)

        def there(g):
            return not isinstance(g, int) or 0 <= g < B

        def at(n, count=1):
            return slice(n, n + count) if isinstance(n, int) else bass.ds(n, count)

        with nc.Block() as block:
            @block.sync
            def _(sp):
                for counter in (tpt_copied, phi_copied, pt_copied, o_copied):
                    sp.sem_inc(counter, ROOM)
                for counter in (tpt_done, l_done, x_done, pt_done, y_done, s_done):
                    sp.sem_inc(counter, 2 * PER)
                for counter in (o_done, r_done):
                    sp.sem_inc(counter, 2)
                for dst, src in ((w_comb[:], d["w_comb_pad"]), (w_out[:], d["w_out_t"]),
                                 (b_out[:], d["L0_attn_b_b_out"].rearrange("(a b) -> a b", a=1).broadcast_to([P, D])),
                                 (bar[:], d["c_bar"]), (ident_b[:], d["c_ident_b"])):
                    sp.dma_start(dst, src).then_inc(loaded, 16)

            @block.gpsimd
            def _(pool):
                pool.wait_ge(loaded, 80)
                for par in range(2):
                    pool.memset(tp[par][:, :, NM * 2 * RFF:KC * P], 0.0).then_inc(padded, 1)
                pool.wait_ge(padded, 2)

                def products(g, par):
                    pool.wait_ge(tpt_done, PER * (g + 1))
                    for t in range(PER):
                        tile = at(PER * g + t)
                        pool.tensor_tensor(tp[par][:, t, 0:NM * 2 * RFF].rearrange("p (m f) -> p m f", m=NM),
                                           phases[:, tile, :, :].rearrange("p a b c -> p a (b c)").broadcast_to([P, NM, 2 * RFF]),
                                           powers[:, tile, :].rearrange("p a m -> p m a").broadcast_to([P, NM, 2 * RFF]),
                                           ALU.mult).then_inc(tp_done, 1)

                def values_and_bias(g, par):
                    pool.wait_ge(o_done, g + 1)
                    pool.tensor_copy(v[par][:], values[:, at(PER * g, PER), :]).then_inc(v_done, 1)
                    pool.tensor_tensor(k["x"][:, at(PER * g, PER), :], k["x"][:, at(PER * g, PER), :],
                                       b_out[:, None, :].broadcast_to([P, PER, D]), ALU.add).then_inc(xb_done, 1)

                products(0, 0)
                products(1, 1)
                values_and_bias(0, 0)

                def turn(g, par):
                    if there(g + 2):
                        products(g + 2, par)
                    if there(g + 1):
                        values_and_bias(g + 1, 1 - par)

                plan(pool, turn)

            @block.tensor
            def _(pe):
                pe.wait_ge(loaded, 80)

                def turn_products(g, par):
                    for t in range(PER):
                        pe.wait_ge(tp_done, PER * g + t + 1)
                        pe.wait_ge(tpt_copied, ROOM + PER * g)
                        for c in range(KC):
                            mm = pe.transpose(p_tp[t][:, c * P:(c + 1) * P], tp[par][:, t, c * P:(c + 1) * P], k["ident"][:])
                        mm.then_inc(tpt_done, 1)

                def combine(g, par):
                    pe.wait_ge(tpt_copied, ROOM + PER * g + PER)
                    pe.wait_ge(phi_copied, ROOM + g)
                    for c in range(KC):
                        mm = pe.matmul(p_phi[:, 0:T], w_comb[:, c, :], tp_t[par][:, c, :], start=(c == 0), stop=(c == KC - 1))
                    mm.then_inc(phi_done, 1)

                def scores(g, par):
                    pe.wait_ge(phi_copied, ROOM + g + 1)
                    pe.wait_ge(l_done, 2 * g + 2)
                    pe.matmul(p_s[par][:, 0:P], phi_t[par][:, 0:P], phi_t[par][:, 0:P], start=True, stop=False)
                    pe.matmul(p_s[par][:, 0:P], ident_b[:], bar[:], start=False, stop=True)
                    pe.matmul(p_s[par][:, P:2 * P], phi_t[par][:, P:T], phi_t[par][:, 0:P], start=True, stop=True)
                    pe.matmul(p_s[par][:, 2 * P:3 * P], phi_t[par][:, P:T], phi_t[par][:, P:T], start=True, stop=False)
                    pe.matmul(p_s[par][:, 2 * P:3 * P], ident_b[:], bar[:], start=False, stop=True).then_inc(s_done, 1)

                def turn_probs(g, par):
                    pe.wait_ge(e_done, 2 * g + 2)
                    pe.wait_ge(pt_copied, ROOM + g)
                    for c in range(3):
                        mm = pe.transpose(p_pt[:, c * P:(c + 1) * P], prob[par][:, c * P:(c + 1) * P], k["ident"][:])
                    mm.then_inc(pt_done, 1)

                def mix(g, par):
                    pe.wait_ge(pt_copied, ROOM + g + 1)
                    pe.wait_ge(v_done, g + 1)
                    pe.wait_ge(o_copied, ROOM + g)
                    pe.matmul(p_o[:, 0:T], v[par][:, 0, :], prob_t[par][:, 0:T], start=True, stop=False)
                    pe.matmul(p_o[:, P:T], v[par][:, 1, :], prob_t[par][:, T:384], start=False, stop=True).then_inc(o_done, 1)

                def output(g, par):
                    pe.wait_ge(o_copied, ROOM + g + 1)
                    pe.wait_ge(x_done, 2 * PER + 2 * g)
                    for t in range(PER):
                        mm = pe.matmul(p_y[:, t * D:(t + 1) * D], o_t[par][:, t * P:(t + 1) * P], w_out[:], start=True, stop=True)
                    mm.then_inc(y_done, 1)

                turn_products(0, 0)
                combine(0, 0)
                turn_products(1, 1)
                scores(0, 0)

                def turn(g, par):
                    if there(g + 1):
                        combine(g + 1, 1 - par)
                    if there(g + 2):
                        turn_products(g + 2, par)
                    turn_probs(g, par)
                    if there(g + 1):
                        scores(g + 1, 1 - par)
                    if there(g - 1):
                        output(g - 1, 1 - par)
                    mix(g, par)

                plan(pe, turn)
                output(B - 1, 1)

            @block.scalar
            def _(act):
                def copy_products(g, par):
                    for t in range(PER):
                        act.wait_ge(tpt_done, PER * (g + 2) + t + 1)
                        act.activation(tp_t[par][:, :, t * P:(t + 1) * P], p_tp[t][:, 0:KC * P].rearrange("p (c q) -> p c q", c=KC),
                                       ACT.Identity).then_inc(tpt_copied, 1)

                def copy_phi(g, par):
                    act.wait_ge(phi_done, g + 1)
                    act.wait_ge(s_done, 2 * PER - 2 + g + 1)
                    act.activation(phi_t[par][:], p_phi[:, 0:T], ACT.Identity).then_inc(phi_copied, 1)

                def exponentials(g, par):
                    act.wait_ge(n_done, g + 1)
                    act.wait_ge(pt_done, 2 * PER - 2 + g + 1)
                    act.wait_ge(r_done, g + 1)
                    for t in range(PER):
                        cols = slice(0, P) if t == 0 else slice(P, 384)
                        act.activation(prob[par][:, cols], logit[par][:, cols], ACT.Exp, bias=ntop[par][:, t:t + 1],
                                       accum_out=mass[par][:, t:t + 1]).then_inc(e_done, 1)

                def copy_o(g, par):
                    act.wait_ge(o_done, g + 3)
                    act.wait_ge(y_done, 2 * PER - 2 + g + 1)
                    act.activation(o_t[par][:], p_o[:, 0:T], ACT.Identity).then_inc(o_copied, 1)

                copy_products(0, 0)
                copy_phi(0, 0)
                copy_products(1, 1)

                def turn(g, par):
                    exponentials(g, par)
                    if there(g + 1):
                        copy_phi(g + 1, 1 - par)
                    if there(g + 2):
                        copy_products(g + 2, par)
                    copy_o(g, par)

                plan(act, turn)

            @block.vector
            def _(dve):
                def logits(g, par):
                    wait_apart(dve, s_done, 2 * PER + g + 1, passed)
                    dve.tensor_tensor_reduce(logit[par][:, 0:P], p_s[par][:, 0:P], decay[:, P:T], 1.0, -3.0e38,
                                             ALU.mult, ALU.max, top[par][:, 0:1]).then_inc(l_done, 1)
                    dve.tensor_tensor_reduce(logit[par][:, P:384], p_s[par][:, P:384], decay[:], 1.0, -3.0e38,
                                             ALU.mult, ALU.max, top[par][:, 1:2]).then_inc(l_done, 1)
                    dve.wait_ge(l_done, 2 * PER + 2 * g + 2)
                    dve.tensor_scalar(ntop[par][:], top[par][:], -1.0, None, ALU.mult).then_inc(n_done, 1)

                def copy_probs(g, par):
                    dve.wait_ge(pt_done, 2 * PER + g + 1)
                    dve.tensor_copy(prob_t[par][:], p_pt[:, 0:384]).then_inc(pt_copied, 1)

                def add(g, par):
                    dve.wait_ge(e_done, 2 * g + 2)
                    dve.reciprocal(rmass[par][:], mass[par][:]).then_inc(r_done, 1)
                    dve.wait_ge(y_done, 2 * PER + g + 1)
                    dve.wait_ge(r_done, g + 3)
                    dve.wait_ge(xb_done, g + 1)
                    for t in range(PER):
                        xs = k["x"][:, at(PER * g + t), :].rearrange("p a e -> p (a e)")
                        dve.scalar_tensor_tensor(xs, p_y[:, t * D:(t + 1) * D], rmass[par][:, t:t + 1], xs,
                                                 ALU.mult, ALU.add).then_inc(x_done, 1)
                    for t in range(PER):
                        dve.wait_ge(x_done, 2 * PER + 2 * g + t + 1)
                        dve.bn_stats(k["halves"][:, at(PER * g + t), :].rearrange("p a s -> p (a s)"),
                                     k["x"][:, at(PER * g + t), :].rearrange("p a e -> p (a e)")).then_inc(measured, 1)

                logits(0, 0)

                def turn(g, par):
                    copy_probs(g, par)
                    if there(g + 1):
                        logits(g + 1, 1 - par)
                    if there(g - 1):
                        add(g - 1, 1 - par)

                plan(dve, turn)
                add(B - 1, 1)


def _layouts(i):
    import numpy as np

    out = {}
    ws = [np.asarray(i[n]).T for n in ("L0_attn_a_Wq", "L0_attn_a_Wq2", "L0_attn_a_Wk", "L0_attn_a_Wk2")]
    out["w_qk"] = np.stack(ws, 1)
    out["w_v_t"] = np.asarray(i["L0_attn_a_Wv"]).T
    proj_t = np.asarray(i["L0_attn_a_Wproj"]).T.reshape(H // 4, 4, DH, D)
    out["w_proj_t"] = proj_t.transpose(1, 0, 2, 3).reshape(P, D)
    out["centroids_t"] = np.asarray(i["L0_ffn_centroids"]).T
    out["w_shell_t"] = np.asarray(i["L0_attn_b_W_shell"]).T
    out["w_charge_t"] = np.asarray(i["L0_attn_b_W_charge"]).T
    out["w_vb_t"] = np.asarray(i["L0_attn_b_W_v"]).T
    out["w_out_t"] = np.asarray(i["L0_attn_b_W_out"]).T
    out["omega_t"] = np.asarray(i["L0_attn_b_omega"]).T
    out["b_shell_wide"] = np.repeat(np.asarray(i["L0_attn_b_b_shell"])[:, None], P, 1)
    comb = np.zeros((3 * P, P), np.float32)
    comb[:NM * 2 * RFF, :64] = np.asarray(i["L0_attn_b_W_combine"]).T
    out["w_comb_pad"] = comb.reshape(3, P, P).transpose(1, 0, 2)
    return {n: np.ascontiguousarray(a) for n, a in out.items()}


def _constants():
    import numpy as np
    bfloat16 = mybir.dt.np(BF16)
    c = {"c_ident": np.eye(P, dtype=np.float32)}
    inv = 1.0 / 10000.0 ** (np.arange(0, DH, 2, dtype=np.float32) / np.float32(DH))
    freqs = np.outer(np.arange(T, dtype=np.float32), inv.astype(np.float32)).astype(np.float32)
    cos, sin = (f(freqs).astype(np.float32).reshape(PER, P, DH // 2).transpose(1, 0, 2) for f in (np.cos, np.sin))
    c["c_rope"] = np.stack([np.concatenate([cos, cos], -1), np.concatenate([-sin, sin], -1)], 2)
    c["c_causal"] = (np.arange(P)[:, None] <= np.arange(P)[None, :]).astype(np.float32)
    keys = (np.arange(1, CANDS + 1, dtype=np.uint64) << 28).astype(np.uint32)
    bits = np.where(keys >> 31, keys ^ np.uint32(1 << 31), ~keys)
    c["c_first_cand"] = np.tile(bits.view(np.float32), (P, 1))
    shifts = 28 - 4 * np.arange(PASSES)
    dig = np.stack([(np.arange(1, CANDS + 1, dtype=np.uint64) << int(s)).astype(np.uint32) for s in shifts])
    c["c_digits"] = np.tile(dig, (P, 1, 1))
    c["c_weight"] = np.tile(np.where(shifts == shifts[0], 1.0, 2.0 ** shifts).astype(np.float32), (P, 1))
    p = np.arange(P)
    c["c_before"] = ((p[:, None] < p[None, :]) - 1.0).astype(bfloat16)
    c["c_lanes"] = np.broadcast_to(p[None, :, None], (P, P, 8)).astype(bfloat16)
    place = np.zeros((P, 2, SLOTS, TILES), np.float32)
    place[:, 0] = np.arange(TILES)
    place[:, 1] = p[:, None, None]
    c["c_place"] = place.reshape(P, 2 * SLOTS, TILES).astype(bfloat16)
    c["c_eighth"] = np.broadcast_to(np.tile(np.arange(SLOTS), 2)[None, :, None], (P, 2 * SLOTS, TILES)).astype(bfloat16)
    q, m = np.arange(P)[:, None], np.arange(T)[None, :]
    c["c_decay"] = np.exp(np.float32(-0.3) * np.abs(q + P - m).astype(np.float32) / np.float32(10.0)).astype(np.float32)
    c["c_bar"] = np.where(p[:, None] < p[None, :], -1e30, 0.0).astype(bfloat16)
    c["c_ident_b"] = np.eye(P).astype(bfloat16)
    scale = math.sqrt(2.0 / (2 * RFF)) * math.sqrt(math.exp(-0.5))
    mags = [math.sqrt(1.0 / math.factorial(m) + 1e-10) * scale for m in range(NM)]
    c["c_mag"] = np.tile(np.array(mags, np.float32), (P, 1))
    return c


_DIRECT = ["L0_attn_a_x", "L0_attn_b_b_charge", "L0_attn_b_W_shell", "L0_attn_b_b_shell", "L0_attn_b_rff_bias",
           "L0_attn_b_b_v", "L0_attn_b_b_out", "L0_ffn_ln_g", "L0_ffn_ln_b", "L0_ffn_w1", "L0_ffn_b1", "L0_ffn_w2",
           "L0_ffn_b2"]


def kernel(**inputs):
    import numpy as _np
    import concourse.bacc as _bacc
    from concourse import mybir as _mybir
    from concourse.bass_utils import run_bass_kernel_spmd as _run

    nc = _bacc.Bacc("TRN2", target_bir_lowering=False, num_devices=1)
    arrays = {n: _np.ascontiguousarray(inputs[n]) for n in _DIRECT}
    arrays["L0_attn_b_log_temp"] = _np.asarray(inputs["L0_attn_b_log_temp"]).reshape(1, 1)
    arrays.update(_layouts(inputs))
    arrays.update({n: _np.ascontiguousarray(a) for n, a in _constants().items()})
    handles = {n: nc.dram_tensor(n, a.shape, _mybir.dt.from_np(a.dtype), kind="ExternalInput").ap() for n, a in arrays.items()}
    handles["out"] = nc.dram_tensor("out", (B, T, D), F32, kind="ExternalOutput").ap()
    build(nc, handles)
    r = _run(nc, [arrays], core_ids=[0])
    return r.results[0]["out"]
```
